# Optimizing a Trainium2 kernel written in Bass

```python
import numpy as np
import jax
import jax.numpy as jnp

def _softmax(x, axis=-1):
    return jax.nn.softmax(x, axis=axis)

def _gelu(x):
    return jax.nn.gelu(x, approximate=True)

def _silu(x):
    return jax.nn.silu(x)

def _sigmoid(x):
    return jax.nn.sigmoid(x)

def _layernorm(x, axis=-1, eps=1e-05):
    m = jnp.mean(x, axis=axis, keepdims=True)
    v = jnp.var(x, axis=axis, keepdims=True)
    return (x - m) / jnp.sqrt(v + eps)

def _scatter_add(tgt, idx, src, axis=0):
    return tgt.at[idx].add(src)

def _segment_sum(src, seg, n):
    return jax.ops.segment_sum(src, seg, n)
kernel_name = 'mk_cond_resid_d2_seqx_r8_239618'

def setup_inputs(seed: int=0):
    np.random.seed(seed)
    _w = jnp.asarray

    def _rec_inputs():
        import jax
        import jax.numpy as jnp
        _rk = jax.random.key(seed)
        x = 7.22e-05 + 1 * jax.random.normal(jax.random.fold_in(_rk, 1), (16, 128, 128), jnp.float32)
        _lenS = 128 - jax.random.randint(jax.random.fold_in(_rk, 7), (16,), 0, max(1, 128 // 4) + 1, jnp.int32)
        _lenS2 = 128 - jax.random.randint(jax.random.fold_in(_rk, 8), (16,), 0, max(1, 128 // 4) + 1, jnp.int32)
        cond_64 = -0.104238 + 1.01173 * jax.random.normal(jax.random.fold_in(_rk, 11), (16, 64), jnp.float32)
        _validS = jnp.arange(128)[None, :] < _lenS[:, None]
        _validS2 = jnp.arange(128)[None, :] < _lenS2[:, None]
        _causal = jnp.tril(jnp.ones((128, 128), dtype=bool))
        mask_BxS_bf1 = jnp.ones((16, 128), dtype=bool)
        return (x, cond_64, mask_BxS_bf1)
    x, cond_64, mask_BxS_bf1 = _rec_inputs()

    def _L0_cond_setup():
        import jax, jax.numpy as jnp
        import numpy as np
        B, S, H = (4, 256, 128)
        E = 8
        M = 64
        K = 2
        N_SHARED = 2
        SM = M * N_SHARED
        G = 64
        GE_TEMP = 1.0
        ALPHA = 0.001
        SEQ_AUX = True
        NORM_TOPK = True
        COS_TEMP = 0.78
        CONS_ALPHA = 0.01
        LEAKY_SLOPE = 0.01
        EPS_COS = 1e-08

        def _leaky(x):
            return jnp.where(x >= 0, x, LEAKY_SLOPE * x)

        def _moe_forward(hidden_states, g, wt, wg, w_gate, w_up, w_down, sw_gate, sw_up, sw_down):
            b, s, h = hidden_states.shape
            x = hidden_states.reshape(-1, h)
            T = x.shape[0]
            logits_h = x @ wt.T
            logits_g = g @ wg.T
            logits_g = jnp.repeat(logits_g, s, axis=0)
            logits = (logits_h + logits_g / GE_TEMP) / (1.0 + 1.0 / GE_TEMP)
            scores = jax.nn.softmax(logits, axis=-1)
            topk_w, topk_idx = jax.lax.top_k(scores, K)
            if K > 1 and NORM_TOPK:
                topk_w = topk_w / (topk_w.sum(-1, keepdims=True) + 1e-20)
            onehot = jax.nn.one_hot(topk_idx.reshape(b, s * K), E, dtype=jnp.float32)
            ce = onehot.sum(1) / (s * K / E)
            aux_loss = (ce * scores.reshape(b, s, E).mean(1)).sum(1).mean() * ALPHA
            gp = _leaky(jnp.einsum('th,ehm->etm', x, w_gate))
            up = jnp.einsum('th,ehm->etm', x, w_up)
            y_all = jnp.einsum('etm,emh->eth', gp * up, w_down)
            y_sel = y_all[topk_idx, jnp.arange(T)[:, None], :]
            y = (y_sel * topk_w[..., None]).sum(1).reshape(b, s, h)
            p = _leaky(hidden_states @ sw_gate) * (hidden_states @ sw_up) @ sw_down
            y = y + p
            num = jnp.sum(y * p, -1)
            den = jnp.maximum(jnp.linalg.norm(y, axis=-1), EPS_COS) * jnp.maximum(jnp.linalg.norm(p, axis=-1), EPS_COS)
            closs = CONS_ALPHA * jnp.mean(num / den / (1.0 + COS_TEMP))
            return (y, aux_loss + closs)
        key = jax.random.key(seed)
        ks = jax.random.split(key, 12)
        sh = 1.0 / np.sqrt(H)
        sm = 1.0 / np.sqrt(M)
        ssm = 1.0 / np.sqrt(SM)
        sg = 1.0 / np.sqrt(G)
        return {'hidden_states': jax.random.normal(ks[0], (B, S, H), jnp.float32), 'g': jax.random.normal(ks[1], (B, G), jnp.float32), 'wt': jax.random.uniform(ks[2], (E, H), jnp.float32, -sh, sh), 'wg': jax.random.uniform(ks[3], (E, G), jnp.float32, -sg, sg), 'w_gate': jax.random.uniform(ks[4], (E, H, M), jnp.float32, -sh, sh), 'w_up': jax.random.uniform(ks[5], (E, H, M), jnp.float32, -sh, sh), 'w_down': jax.random.uniform(ks[6], (E, M, H), jnp.float32, -sm, sm), 'sw_gate': jax.random.uniform(ks[7], (H, SM), jnp.float32, -sh, sh), 'sw_up': jax.random.uniform(ks[8], (H, SM), jnp.float32, -sh, sh), 'sw_down': jax.random.uniform(ks[9], (SM, H), jnp.float32, -ssm, ssm)}
    _L0_cond_all = _L0_cond_setup()
    _L0_cond_in = {k: v for k, v in _L0_cond_all.items() if k in ('wt', 'wg', 'w_gate', 'w_up', 'w_down', 'sw_gate', 'sw_up', 'sw_down')}
    del _L0_cond_all

    def _L1_cond_setup():
        import jax, jax.numpy as jnp
        import numpy as np
        DIM = 128
        HEADS = 16
        DIM_HEAD = 64
        SCALE = 8.0

        def ln(x, g, eps=1e-05):
            mean = x.mean(axis=-1, keepdims=True)
            var = ((x - mean) ** 2).mean(axis=-1, keepdims=True)
            return (x - mean) * jax.lax.rsqrt(var + eps) * g

        def l2norm(t):
            n = jnp.maximum(jnp.linalg.norm(t, axis=-1, keepdims=True), 1e-12)
            return t / n

        def rel_pos_bias(n, w0, b0, g0, w1, b1, g1, w2, b2, dtype):
            pos = jnp.arange(-n + 1, n, dtype=dtype)[:, None]
            h = jax.nn.silu(ln(pos @ w0 + b0, g0))
            h = jax.nn.silu(ln(h @ w1 + b1, g1))
            h = h @ w2 + b2
            i = jnp.arange(n)
            idx = i[:, None] - i[None, :] + n - 1
            bias = h[idx]
            return jnp.transpose(bias, (2, 0, 1))
        key = jax.random.key(seed)
        ks = jax.random.split(key, 16)
        b, n = (2, 256)
        inner = HEADS * DIM_HEAD
        s = 0.02
        return {'x': jax.random.normal(ks[0], (b, n, DIM), jnp.float32), 'mask': jnp.ones((b, n), dtype=bool), 'g_norm': jnp.ones((DIM,), jnp.float32), 'Wq': jax.random.normal(ks[1], (DIM, inner), jnp.float32) * s, 'Wkv': jax.random.normal(ks[2], (DIM, 2 * DIM_HEAD), jnp.float32) * s, 'q_scale': jnp.ones((DIM_HEAD,), jnp.float32), 'k_scale': jnp.ones((DIM_HEAD,), jnp.float32), 'null_kv': jax.random.normal(ks[3], (2, DIM_HEAD), jnp.float32), 'null_attn_bias': jax.random.normal(ks[4], (HEADS,), jnp.float32), 'w0': jax.random.normal(ks[5], (1, DIM), jnp.float32) * s, 'b0': jnp.zeros((DIM,), jnp.float32), 'g0': jnp.ones((DIM,), jnp.float32), 'w1': jax.random.normal(ks[6], (DIM, DIM), jnp.float32) * s, 'b1': jnp.zeros((DIM,), jnp.float32), 'g1': jnp.ones((DIM,), jnp.float32), 'w2': jax.random.normal(ks[7], (DIM, HEADS), jnp.float32) * s, 'b2': jnp.zeros((HEADS,), jnp.float32), 'Wout': jax.random.normal(ks[8], (inner, DIM), jnp.float32) * s, 'g_out': jnp.ones((DIM,), jnp.float32)}
    _L1_cond_all = _L1_cond_setup()
    _L1_cond_in = {k: v for k, v in _L1_cond_all.items() if k in ('g_norm', 'Wq', 'Wkv', 'q_scale', 'k_scale', 'null_attn_bias', 'w0', 'b0', 'g0', 'w1', 'b1', 'g1', 'w2', 'b2', 'Wout', 'g_out')}
    del _L1_cond_all
    return {'x': x, 'cond_64': cond_64, 'mask_BxS_bf1': mask_BxS_bf1, 'L0_cond_wt': _L0_cond_in['wt'], 'L0_cond_wg': _L0_cond_in['wg'], 'L0_cond_w_gate': _L0_cond_in['w_gate'], 'L0_cond_w_up': _L0_cond_in['w_up'], 'L0_cond_w_down': _L0_cond_in['w_down'], 'L0_cond_sw_gate': _L0_cond_in['sw_gate'], 'L0_cond_sw_up': _L0_cond_in['sw_up'], 'L0_cond_sw_down': _L0_cond_in['sw_down'], 'L1_cond_g_norm': _L1_cond_in['g_norm'], 'L1_cond_Wq': _L1_cond_in['Wq'], 'L1_cond_Wkv': _L1_cond_in['Wkv'], 'L1_cond_q_scale': _L1_cond_in['q_scale'], 'L1_cond_k_scale': _L1_cond_in['k_scale'], 'L1_cond_null_attn_bias': _L1_cond_in['null_attn_bias'], 'L1_cond_w0': _L1_cond_in['w0'], 'L1_cond_b0': _L1_cond_in['b0'], 'L1_cond_g0': _L1_cond_in['g0'], 'L1_cond_w1': _L1_cond_in['w1'], 'L1_cond_b1': _L1_cond_in['b1'], 'L1_cond_g1': _L1_cond_in['g1'], 'L1_cond_w2': _L1_cond_in['w2'], 'L1_cond_b2': _L1_cond_in['b2'], 'L1_cond_Wout': _L1_cond_in['Wout'], 'L1_cond_g_out': _L1_cond_in['g_out']}

def reference(x, cond_64, mask_BxS_bf1, L0_cond_wt, L0_cond_wg, L0_cond_w_gate, L0_cond_w_up, L0_cond_w_down, L0_cond_sw_gate, L0_cond_sw_up, L0_cond_sw_down, L1_cond_g_norm, L1_cond_Wq, L1_cond_Wkv, L1_cond_q_scale, L1_cond_k_scale, L1_cond_null_attn_bias, L1_cond_w0, L1_cond_b0, L1_cond_g0, L1_cond_w1, L1_cond_b1, L1_cond_g1, L1_cond_w2, L1_cond_b2, L1_cond_Wout, L1_cond_g_out):
    import jax
    import jax.numpy as jnp

    def _L0_cond_ref(hidden_states, g, wt, wg, w_gate, w_up, w_down, sw_gate, sw_up, sw_down):
        import jax, jax.numpy as jnp
        import numpy as np
        B, S, H = (4, 256, 128)
        E = 8
        M = 64
        K = 2
        N_SHARED = 2
        SM = M * N_SHARED
        G = 64
        GE_TEMP = 1.0
        ALPHA = 0.001
        SEQ_AUX = True
        NORM_TOPK = True
        COS_TEMP = 0.78
        CONS_ALPHA = 0.01
        LEAKY_SLOPE = 0.01
        EPS_COS = 1e-08

        def _leaky(x):
            return jnp.where(x >= 0, x, LEAKY_SLOPE * x)

        def _moe_forward(hidden_states, g, wt, wg, w_gate, w_up, w_down, sw_gate, sw_up, sw_down):
            b, s, h = hidden_states.shape
            x = hidden_states.reshape(-1, h)
            T = x.shape[0]
            logits_h = x @ wt.T
            logits_g = g @ wg.T
            logits_g = jnp.repeat(logits_g, s, axis=0)
            logits = (logits_h + logits_g / GE_TEMP) / (1.0 + 1.0 / GE_TEMP)
            scores = jax.nn.softmax(logits, axis=-1)
            topk_w, topk_idx = jax.lax.top_k(scores, K)
            if K > 1 and NORM_TOPK:
                topk_w = topk_w / (topk_w.sum(-1, keepdims=True) + 1e-20)
            onehot = jax.nn.one_hot(topk_idx.reshape(b, s * K), E, dtype=jnp.float32)
            ce = onehot.sum(1) / (s * K / E)
            aux_loss = (ce * scores.reshape(b, s, E).mean(1)).sum(1).mean() * ALPHA
            gp = _leaky(jnp.einsum('th,ehm->etm', x, w_gate))
            up = jnp.einsum('th,ehm->etm', x, w_up)
            y_all = jnp.einsum('etm,emh->eth', gp * up, w_down)
            y_sel = y_all[topk_idx, jnp.arange(T)[:, None], :]
            y = (y_sel * topk_w[..., None]).sum(1).reshape(b, s, h)
            p = _leaky(hidden_states @ sw_gate) * (hidden_states @ sw_up) @ sw_down
            y = y + p
            num = jnp.sum(y * p, -1)
            den = jnp.maximum(jnp.linalg.norm(y, axis=-1), EPS_COS) * jnp.maximum(jnp.linalg.norm(p, axis=-1), EPS_COS)
            closs = CONS_ALPHA * jnp.mean(num / den / (1.0 + COS_TEMP))
            return (y, aux_loss + closs)
        y, _ = _moe_forward(hidden_states, g, wt, wg, w_gate, w_up, w_down, sw_gate, sw_up, sw_down)
        return y

    def _L1_cond_ref(x, mask, g_norm, Wq, Wkv, q_scale, k_scale, null_kv, null_attn_bias, w0, b0, g0, w1, b1, g1, w2, b2, Wout, g_out):
        import jax, jax.numpy as jnp
        import numpy as np
        DIM = 128
        HEADS = 16
        DIM_HEAD = 64
        SCALE = 8.0

        def ln(x, g, eps=1e-05):
            mean = x.mean(axis=-1, keepdims=True)
            var = ((x - mean) ** 2).mean(axis=-1, keepdims=True)
            return (x - mean) * jax.lax.rsqrt(var + eps) * g

        def l2norm(t):
            n = jnp.maximum(jnp.linalg.norm(t, axis=-1, keepdims=True), 1e-12)
            return t / n

        def rel_pos_bias(n, w0, b0, g0, w1, b1, g1, w2, b2, dtype):
            pos = jnp.arange(-n + 1, n, dtype=dtype)[:, None]
            h = jax.nn.silu(ln(pos @ w0 + b0, g0))
            h = jax.nn.silu(ln(h @ w1 + b1, g1))
            h = h @ w2 + b2
            i = jnp.arange(n)
            idx = i[:, None] - i[None, :] + n - 1
            bias = h[idx]
            return jnp.transpose(bias, (2, 0, 1))
        b, n, _ = x.shape
        xn = ln(x, g_norm)
        q = (xn @ Wq).reshape(b, n, HEADS, DIM_HEAD).transpose(0, 2, 1, 3)
        kv = xn @ Wkv
        k, v = (kv[..., :DIM_HEAD], kv[..., DIM_HEAD:])
        nk = jnp.broadcast_to(null_kv[0], (b, 1, DIM_HEAD))
        nv = jnp.broadcast_to(null_kv[1], (b, 1, DIM_HEAD))
        k = jnp.concatenate([nk, k], axis=1)
        v = jnp.concatenate([nv, v], axis=1)
        q = l2norm(q) * q_scale
        k = l2norm(k) * k_scale
        sim = jnp.einsum('bhid,bjd->bhij', q, k) * SCALE
        bias = rel_pos_bias(n, w0, b0, g0, w1, b1, g1, w2, b2, q.dtype)
        null_bias = jnp.broadcast_to(null_attn_bias[:, None, None], (HEADS, n, 1))
        attn_bias = jnp.concatenate([null_bias, bias], axis=-1)
        sim = sim + attn_bias
        neg = -jnp.finfo(sim.dtype).max
        causal = jnp.triu(jnp.ones((n, n + 1), dtype=bool), k=2)
        sim = jnp.where(causal, neg, sim)
        m = jnp.pad(mask, ((0, 0), (1, 0)), constant_values=True)[:, None, None, :]
        sim = jnp.where(m, sim, neg)
        attn = jax.nn.softmax(sim, axis=-1)
        out = jnp.einsum('bhij,bjd->bhid', attn, v)
        out = out.transpose(0, 2, 1, 3).reshape(b, n, HEADS * DIM_HEAD)
        return ln(out @ Wout, g_out)
    x = x + _L0_cond_ref(x, cond_64, L0_cond_wt, L0_cond_wg, L0_cond_w_gate, L0_cond_w_up, L0_cond_w_down, L0_cond_sw_gate, L0_cond_sw_up, L0_cond_sw_down)
    x = x + _L1_cond_ref(x, mask_BxS_bf1, L1_cond_g_norm, L1_cond_Wq, L1_cond_Wkv, L1_cond_q_scale, L1_cond_k_scale, cond_64, L1_cond_null_attn_bias, L1_cond_w0, L1_cond_b0, L1_cond_g0, L1_cond_w1, L1_cond_b1, L1_cond_g1, L1_cond_w2, L1_cond_b2, L1_cond_Wout, L1_cond_g_out)
    return x

_drawn_inputs = setup_inputs


def setup_inputs(seed=0):
    import zlib

    import numpy as np

    out = dict(_drawn_inputs(seed))
    spreads = {'L1_cond_g_norm': (1.0, 0.2),
     'L1_cond_q_scale': (1.0, 0.2),
     'L1_cond_k_scale': (1.0, 0.2),
     'L1_cond_b0': (0.0, 0.1),
     'L1_cond_g0': (1.0, 0.6),
     'L1_cond_b1': (0.0, 0.1),
     'L1_cond_g1': (1.0, 0.6),
     'L1_cond_b2': (0.0, 0.408),
     'L1_cond_g_out': (1.0, 0.2)}
    factors = {}
    for name, (base, spread) in spreads.items():
        noise = np.random.default_rng([zlib.crc32(name.encode()), seed]).standard_normal(out[name].shape)
        drawn = base * np.exp(spread * noise) if base else spread * noise
        out[name] = jnp.asarray(drawn.astype(out[name].dtype))
    for name, factor in factors.items():
        out[name] = (out[name] * factor).astype(out[name].dtype)
    return out
```

```python
from contextlib import ExitStack

import numpy as np

import concourse.bass as bass
from concourse import mybir

F32 = mybir.dt.float32
BF16 = mybir.dt.bfloat16
U8 = mybir.dt.uint8
ALU = mybir.AluOpType
ACT = mybir.ActivationFunctionType
AX = mybir.AxisListType

B, T, H = 16, 128, 128
E, M = 8, 64
NH, D = 16, 64
EC = E * M // 128
MC = EC + 1
GB = 4
NG = B // GB
GT = GB * T
HG = 4
HGS = NH // HG
PAIRS = NH // 2
LN_EPS = 1e-5
NEG = -1e30
NORM_MIN = 1e-12
NORM_SCALE = 256.0
SLOPE = 0.01
REL = 2 * T - 1


def head_view(ap, g):
    v = ap.rearrange("p (G i r) -> p G r i", G=NH // 8, r=2)
    return v[:, g // 2, g % 2, :]


def build(nc, a, out):
    ctx = ExitStack()
    with ctx:
        def sb(name, shape, dt=F32):
            return ctx.enter_context(nc.sbuf_tensor(name, shape, dt))

        def psum(name, shape, dt=F32):
            return ctx.enter_context(nc.psum_tensor(name, shape, dt))

        def sem(name):
            return ctx.enter_context(nc.semaphore(name))

        ident = sb("ident", [128, 128])
        identb = sb("identb", [128, 128], BF16)
        flip = sb("flip", [128, 128])
        esel = sb("esel", [3 * E, EC, 128], BF16)
        eself = sb("eself", [3 * E, EC, 128])
        nsel = sb("nsel", [128, PAIRS, NH])
        pos = sb("pos", [128, 1])
        rank = sb("rank", [128, B, E])
        ones = sb("ones", [128, 128])
        wg = sb("wg", [128, MC, 128])
        wu = sb("wu", [128, MC, 128])
        wd = sb("wd", [128, MC, 128])
        wq = sb("wq", [128, NH * D])
        wkvn = sb("wkvn", [128, NH + 2 * D])
        wo = sb("wo", [128, PAIRS, 128])
        wt8 = sb("wt8", [E, H])
        wg8 = sb("wg8", [E, D])
        cond = sb("cond", [B, D])
        wtT = sb("wtT", [128, E])
        wgT = sb("wgT", [D, E])
        condT = sb("condT", [D, B])
        gl = sb("gl", [B, B, E])
        gnorm = sb("gnorm", [128, 1])
        gout = sb("gout", [128, H])
        qsc = sb("qsc", [128, 1])
        ksc = sb("ksc", [128, 1])
        ksc8 = sb("ksc8", [128, 1])
        nvcol = sb("nvcol", [128, 1])
        nvblk = sb("nvblk", [128, PAIRS, NH])
        nvw = sb("nvw", [NH, H])
        nkrow = sb("nkrow", [128, D])
        qrow = sb("qrow", [128, D])
        krow = sb("krow", [128, D])
        nullb = sb("nullb", [128, NH])
        nulls = sb("nulls", [128, 8])
        w0 = sb("w0", [128, H])
        b0 = sb("b0", [128, H])
        g0 = sb("g0", [128, H])
        b1 = sb("b1", [128, H])
        g1 = sb("g1", [128, H])
        w1 = sb("w1", [128, H])
        w2 = sb("w2", [128, NH])
        b2 = sb("b2", [128, NH])
        ph = sb("ph", [128, 4, H])
        phT = sb("phT", [128, H])
        pstat = sb("pstat", [128, 16])
        rel = sb("rel", [128, NH])
        relT = sb("relT", [NH, REL])
        bias = sb("bias", [128, NH, T])
        biasr = sb("biasr", [128, NH, T])
        masku = sb("masku", [128, B, T], U8)
        maskb = sb("maskb", [128, B, T])
        biasm = sb("biasm", [128, NH, T])
        xa = sb("xa", [128, B, H])
        xT = sb("xT", [128, B * T])
        xc = sb("xc", [128, B, H])
        sq = sb("sq", [128, GB, H])
        msum = sb("msum", [128, GB])
        nmean = sb("nmean", [128, GB])
        var = sb("var", [128, B])
        rstd = sb("rstd", [128, 4, B])
        lg = sb("lg", [128, B, E])
        rt = sb("rt", [128, 8, B, E])
        rs = sb("rs", [128, 8, B])
        cp = sb("cp", [128, B, 3, E], BF16)
        cT = sb("cT", [3 * E, B * T], BF16)
        gs = sb("gs", [128, MC, GT])
        hub = sb("hub", [128, 2, GT])
        hh = sb("hh", [128, MC, GT])
        xnb = sb("xnb", [128, T])
        q2 = sb("q2", [128, NH, D])
        kvs = sb("kvs", [128, NH + 2 * D])
        vaug = sb("vaug", [128, D + 1])
        ss = sb("ss", [128, NH + 1])
        nw = sb("nw", [128, 4, NH + 1])
        lns = sb("lns", [128, NH + 1])
        qh = sb("qh", [128, NH, D])
        kk = sb("kk", [128, 2, D])
        k2 = sb("k2", [128, D])
        qT = sb("qT", [128, PAIRS, T])
        kT = sb("kT", [128, T])
        nnl = sb("nnl", [128, 2, NH])
        ssb = sb("ssb", [128, 2, HG, T])
        mx = sb("mx", [128, NH])
        nm = sb("nm", [128, NH])
        pnd = sb("pnd", [128, NH])
        pn = sb("pn", [128, NH])
        pr = sb("pr", [128, 2, HG, T])
        pT = sb("pT", [128, 2, HG, T])
        den = sb("den", [128, 2, HG])
        on = sb("on", [128, NH, D])
        an = sb("an", [128, NH])
        oT = sb("oT", [128, PAIRS, T])
        anT = sb("anT", [NH, T])
        ost = sb("ost", [128, 6])
        omv = sb("omv", [128, 2])
        onw = sb("onw", [128, 6])
        olin = sb("olin", [128, H])
        osc = sb("osc", [128, H])
        ores = sb("ores", [128, H])

        bk = [psum(f"bk{i}", [128, 512]) for i in range(6)]
        bq = psum("bq", [128, 2, 512])

        scratch = nc.dram_tensor("relbias_scratch", (NH, REL), F32, kind="Internal").ap()

        l_pos, l_x, l_route, l_moe, l_att, l_mask = (sem(n) for n in (
            "l_pos", "l_x", "l_route", "l_moe", "l_att", "l_mask"))
        d_rel, d_bias, d_out = sem("d_rel"), sem("d_bias"), sem("d_out")
        one = {n: sem(n) for n in (
            "p_wt", "p_gl", "p_xT", "p_lg", "p_cT", "p_h1T", "p_h1", "p_h2T", "p_rel", "p_relT", "p_nvw", "p_bias", "p_xnT",
            "a_e1", "a_e2", "a_r1", "a_exp", "a_ln", "a_var", "a_nk", "a_bias",
            "v_wt", "v_gl", "v_gld", "v_xT", "v_d", "v_cp", "v_cT", "v_hs", "v_hg", "v_hT", "v_relT", "v_var", "v_xn",
            "v_xnT", "v_nk", "v_nv", "v_nvw", "v_wkvn", "v_lnp", "v_ones", "g_sq", "g_mask")}
        v_set, a_set = sem("v_set"), sem("a_set")
        m_gate, m_up, m_cb, m_y, m_gs, m_lk, m_hu, m_h, m_x1, m_st, m_sq = (sem(n) for n in (
            "m_gate", "m_up", "m_cb", "m_y", "m_gs", "m_lk", "m_hu", "m_h", "m_x1", "m_st", "m_sq"))
        t_s, t_pT, t_av, t_q, t_kv, t_qT, t_kT, t_oT, t_anT, t_out = (sem(n) for n in (
            "t_s", "t_pT", "t_av", "t_q", "t_kv", "t_qT", "t_kT", "t_oT", "t_anT", "t_out"))
        c_exp, c_pT, c_q2, c_kv, c_qT, c_oT, c_anT, c_lnq, c_lno = (sem(n) for n in (
            "c_exp", "c_pT", "c_q2", "c_kv", "c_qT", "c_oT", "c_anT", "c_lnq", "c_lno"))
        e_s, e_mx, e_nm, e_dn, e_on, e_sq, e_ss, e_nq, e_qh, e_kk, e_nl, e_kT, e_st, e_var, e_no, e_out = (
            sem(n) for n in ("e_s", "e_mx", "e_nm", "e_dn", "e_on", "e_sq", "e_ss", "e_nq", "e_qh", "e_kk", "e_nl",
                             "e_kT", "e_st", "e_var", "e_no", "e_out"))
        settled = sem("settled")
        g_xn, g_bias, g_v, g_o = (sem(n) for n in ("g_xn", "g_bias", "g_v", "g_o"))

        block = ctx.enter_context(nc.Block())

        def settle(engine):
            engine.sem_inc(settled, 1)

        @block.sync
        def _(sp):
            def load(dst, src, s):
                sp.dma_start(dst, src).then_inc(s, 16)

            def row(v):
                return v.rearrange("(o n) -> o n", o=1).partition_broadcast(128) if len(v.shape) == 1 else v

            for g in range(NG):
                load(xa[:, g * GB:(g + 1) * GB, :], a["x"][g * GB:(g + 1) * GB].rearrange("b t h -> t b h"), l_x)
                if g == 0:
                    load(ident[:], a["c_ident"], l_route)
                    load(wt8[:], a["L0_cond_wt"], l_route)
                    load(wg8[:], a["L0_cond_wg"], l_route)
                    load(cond[:], a["cond_64"], l_route)
                    load(rank[:], a["c_rank"].rearrange("(o b) e -> o b e", o=1).to_broadcast([128, B, E]), l_route)
                    load(eself[:], a["c_esel"], l_route)
            load(pos[:], a["c_pos"], l_pos)
            for dst, name in ((w0, "w0"), (b0, "b0"), (g0, "g0"), (b1, "b1"), (g1, "g1")):
                v = a["L1_cond_" + name]
                v = v if len(v.shape) == 2 else v.rearrange("(o n) -> o n", o=1)
                load(dst[:], v.to_broadcast([128, H]), l_pos)
            load(b2[:], a["L1_cond_b2"].rearrange("(o n) -> o n", o=1).to_broadcast([128, NH]), l_pos)
            load(w1[:], a["L1_cond_w1"], l_pos)
            load(w2[:], a["L1_cond_w2"], l_pos)
            load(flip[:], a["c_flip"], l_pos)
            for dst, ex, sh in ((wg, "L0_cond_w_gate", "L0_cond_sw_gate"), (wu, "L0_cond_w_up", "L0_cond_sw_up")):
                load(dst[:, 0:EC, :].rearrange("p c (e m) -> p (c e) m", m=M), a[ex].rearrange("e h m -> h e m"), l_moe)
                load(dst[:, EC, :], a[sh], l_moe)
            load(wd[:, 0:EC, :], a["L0_cond_w_down"].rearrange("(c e) m h -> (e m) c h", e=2), l_moe)
            load(wd[:, EC, :], a["L0_cond_sw_down"], l_moe)
            load(masku[:], a["mask"].rearrange("(o b) t -> o b t", o=1).to_broadcast([128, B, T]), l_mask)
            load(wq[:], a["L1_cond_Wq"], l_att)
            load(wkvn[:, NH:], a["L1_cond_Wkv"], l_att)
            load(wo[:], a["L1_cond_Wout"].rearrange("(c p) n -> p c n", p=128), l_att)
            load(nsel[:], a["c_nsel"], l_att)
            load(gnorm[:], a["L1_cond_g_norm"].rearrange("(n o) -> n o", o=1), l_att)
            load(gout[:], a["L1_cond_g_out"].rearrange("(o n) -> o n", o=1).to_broadcast([128, H]), l_att)
            load(nullb[:], a["L1_cond_null_attn_bias"].rearrange("(o n) -> o n", o=1).to_broadcast([128, NH]), l_att)
            for half in range(2):
                hs = slice(half * D, (half + 1) * D)
                load(qsc[hs], a["L1_cond_q_scale"].rearrange("(n o) -> n o", o=1), l_att)
                load(ksc[hs], a["L1_cond_k_scale"].rearrange("(n o) -> n o", o=1), l_att)
                load(nvcol[hs], a["cond_64"][1:2, :].rearrange("o n -> n o"), l_att)
            load(nkrow[:], a["cond_64"][0:1, :].to_broadcast([128, D]), l_att)
            load(qrow[:], a["L1_cond_q_scale"].rearrange("(o n) -> o n", o=1).to_broadcast([128, D]), l_att)
            load(krow[:], a["L1_cond_k_scale"].rearrange("(o n) -> o n", o=1).to_broadcast([128, D]), l_att)
            sp.wait_ge(one["v_relT"], 2)
            sp.dma_start(scratch, relT[:]).then_inc(d_rel, 16)
            sp.wait_ge(d_rel, 16)
            for g in range(HGS):
                first = (8 * (g // 2) + g % 2) * REL
                src = bass.AP(tensor=scratch.tensor, offset=first, ap=[[1, 128], [2 * REL, HG], [1, T]])
                sp.dma_start(biasr[:, g * HG:(g + 1) * HG, :], src).then_inc(d_bias, 16)

            def store(m):
                sp.wait_ge(g_o, 2 * m + 2)
                sp.dma_start(out[bass.ds(m, 1)].rearrange("o t h -> (o t) h"), ores[:]).then_inc(d_out, 16)

            with sp.Fori(0, B) as m:
                store(m)
            sp.wait_ge(d_out, 16 * B)
        L_ROUTE, L_POS, L_MOE, L_ATT = 16 * 6, 16 * 10, 16 * 6, 16 * 16

        @block.tensor
        def _(pe):
            mm, tr = nc.tensor.matmul, nc.tensor.transpose

            pe.wait_ge(l_route, L_ROUTE)
            tr(bk[0][:, 0:E], wt8[:], ident[0:E, 0:E])
            tr(bk[0][0:D, E:2 * E], wg8[:], ident[0:E, 0:E])
            tr(bk[0][0:D, 2 * E:2 * E + B], cond[:], ident[0:B, 0:B]).then_inc(one["p_wt"], 1)
            pe.wait_ge(l_x, 16 * NG)
            for g in range(NG):
                for i in range(GB):
                    last = tr(bk[1 + g][:, i * T:(i + 1) * T], xa[:, g * GB + i, :], ident[:])
                last.then_inc(one["p_xT"], 1)
            pe.wait_ge(one["v_wt"], 3)
            mm(bk[0][0:B, 64:64 + E], condT[:], wgT[:], start=True, stop=True).then_inc(one["p_gl"], 1)
            pe.wait_ge(one["v_gld"], 1)
            pe.wait_ge(one["v_ones"], 1)
            mm(bk[5][:, 0:B * E], ones[0:B, :], gl[:].rearrange("p b e -> p (b e)"), start=True, stop=False,
               skip_group_check=True)
            for b in range(B):
                pe.wait_ge(one["v_xT"], b // GB + 1)
                last = mm(bk[5][:, b * E:(b + 1) * E], xT[:, b * T:(b + 1) * T], wtT[:], start=False,
                          stop=(b == B - 1), skip_group_check=True)
            last.then_inc(one["p_lg"], 1)

            pe.wait_ge(l_pos, L_POS)
            pe.wait_ge(one["v_hs"], 1)
            tr(bk[0][:, 0:H], ph[:, 0, :], ident[:]).then_inc(one["p_h1T"], 1)
            pe.wait_ge(one["v_hT"], 1)
            mm(bk[0][:, 0:H], phT[:], w1[:], start=True, stop=True).then_inc(one["p_h1"], 1)
            pe.wait_ge(one["v_cp"], 1)
            for b in range(B):
                dst = bk[1 + b // 8][:].bitcast(BF16)
                last = tr(dst[0:3 * E, (b % 8) * T:(b % 8 + 1) * T], cp[:, b].rearrange("p s e -> p (s e)"), identb[:])
            last.then_inc(one["p_cT"], 1)
            pe.wait_ge(one["v_hs"], 2)
            tr(bk[0][:, 0:H], ph[:, 0, :], ident[:]).then_inc(one["p_h2T"], 1)
            pe.wait_ge(one["v_hT"], 2)
            mm(bk[0][:, 0:NH], phT[:], w2[:], start=True, stop=True).then_inc(one["p_rel"], 1)
            pe.wait_ge(one["v_relT"], 1)
            mm(bk[0][0:NH, 0:T], rel[:], flip[:], start=True, stop=True).then_inc(one["p_relT"], 1)

            pe.wait_ge(l_moe, L_MOE)
            pe.wait_ge(one["v_cT"], 2)
            GATE, UP, CB, Y = (bk[1], bk[2]), (bk[3], bk[4]), bk[5], bq[:, 0, :]

            def down(q):
                pe.wait_ge(m_hu, MC * (q + 1))
                pe.wait_ge(m_h, EC * (q + 1))
                if not isinstance(q, int) or q > 0:
                    pe.wait_ge(m_x1, q)
                for i in range(GB):
                    for c in range(MC):
                        last = mm(Y[:, i * H:(i + 1) * H], hh[:, c, i * T:(i + 1) * T], wd[:, c, :],
                                  start=(c == 0), stop=(c == MC - 1))
                last.then_inc(m_y, 1)

            def hidden(q, first):
                x_q = xT[:, bass.ds(q * GT, GT)]
                c_q = cT[:, bass.ds(q * GT, GT)]
                for c in range(MC):
                    if c >= 2 or not first:
                        pe.wait_ge(m_lk, MC * q + (c - 1 if c >= 2 else -c))
                        pe.wait_ge(m_hu, MC * q + (c - 1 if c >= 2 else -c))
                    mm(GATE[c % 2][:], wg[:, c, :], x_q, start=True, stop=True).then_inc(m_gate, 1)
                    mm(UP[c % 2][:], wu[:, c, :], x_q, start=True, stop=True).then_inc(m_up, 1)
                    if c == 1 and not first:
                        down(q - 1)
                    if c < EC:
                        if c > 0 or not first:
                            pe.wait_ge(m_h, EC * q + c)
                        settle(pe)
                        mm(CB[:], esel[:, c, :], c_q, start=True, stop=True).then_inc(m_cb, 1)

            hidden(0, True)
            with pe.Fori(1, NG) as q:
                hidden(q, False)
            down(NG - 1)

            pe.wait_ge(l_att, L_ATT)
            pe.wait_ge(one["v_nv"], 1)
            for c in range(PAIRS):
                last = mm(bk[0][0:NH, 0:H], nvblk[:, c, :], wo[:, c, :], start=(c == 0), stop=(c == PAIRS - 1))
            last.then_inc(one["p_nvw"], 1)
            pe.wait_ge(d_bias, 16 * HGS)
            pe.wait_ge(m_x1, NG)
            for g in range(HGS):
                if g >= 2:
                    pe.wait_ge(one["a_bias"], g - 1)
                mm(bq[:, g % 2, :], flip[:], biasr[:, g * HG:(g + 1) * HG, :].rearrange("p i t -> p (i t)"),
                   start=True, stop=True).then_inc(one["p_bias"], 1)
            for g in range(NG):
                pe.wait_ge(one["v_xn"], g + 1)
                for i in range(GB):
                    last = tr(bk[1 + g][:, i * T:(i + 1) * T], xc[:, g * GB + i, :], ident[:])
                last.then_inc(one["p_xnT"], 1)

            SB, PTB, OB, MB, XB = (bk[0], bk[1]), bk[2], bk[3], bk[4], bk[5]

            def scores(m, g):
                pe.wait_ge(c_qT, 2 * m + 1 + g // 2)
                pe.wait_ge(e_kT, m + 1)
                if not isinstance(m, int) or 4 * m + g >= 2:
                    pe.wait_ge(e_s, 4 * m + g - 1)
                half = slice(D * (g % 2), D * (g % 2) + D)
                for i in range(HG):
                    last = mm(SB[g % 2][:, i * T:(i + 1) * T], qT[half, HG * (g // 2) + i, :], kT[half, :],
                              start=True, stop=True)
                last.then_inc(t_s, 1)

            def probs_T(m, g):
                pe.wait_ge(c_exp, 4 * m + g + 1)
                if not isinstance(m, int) or 4 * m + g >= 1:
                    pe.wait_ge(c_pT, 4 * m + g)
                for i in range(HG):
                    last = tr(PTB[:, i * T:(i + 1) * T], pr[:, g % 2, i, :], ident[:])
                last.then_inc(t_pT, 1)

            def values(m, g):
                pe.wait_ge(c_pT, 4 * m + g + 1)
                pe.wait_ge(g_v, m + 1)
                if not isinstance(m, int) or 4 * m + g >= 1:
                    pe.wait_ge(e_on, 4 * m + g)
                for i in range(HG):
                    last = mm(OB[:, i * (D + 1):(i + 1) * (D + 1)], pT[:, g % 2, i, :], vaug[:], start=True, stop=True)
                last.then_inc(t_av, 1)

            def step(n, prev, cur, nxt):
                p, x = n - 1, n + 1
                if prev:
                    probs_T(p, 3)
                    values(p, 2)
                if cur:
                    scores(n, 0)
                    scores(n, 1)
                if nxt:
                    pe.wait_ge(g_xn, x + 1)
                    if prev or cur:
                        pe.wait_ge(c_qT, 2 * x)
                    for c in range(2):
                        mm(bq[:, c, :], xnb[:], wq[:, c * 512:(c + 1) * 512], start=True, stop=True).then_inc(t_q, 1)
                    if cur:
                        pe.wait_ge(e_kT, x)
                    mm(MB[:, 0:NH + 2 * D], xnb[:], wkvn[:], start=True, stop=True).then_inc(t_kv, 1)
                if cur:
                    probs_T(n, 0)
                if prev:
                    values(p, 3)
                if cur:
                    scores(n, 2)
                if prev:
                    pe.wait_ge(e_on, 4 * p + 4)
                    if not isinstance(p, int) or p > 0:
                        pe.wait_ge(e_out, p)
                    for c in range(4):
                        last = tr(XB[:, c * T:(c + 1) * T], on[:, 2 * c:2 * c + 2, :].rearrange("p h d -> p (h d)"), ident[:])
                    last.then_inc(t_oT, 1)
                    if nxt:
                        pe.wait_ge(c_kv, x + 1)
                    else:
                        pe.wait_ge(e_kT, B)
                    tr(MB[0:NH, 256:256 + T], an[:], ident[:]).then_inc(t_anT, 1)
                if cur:
                    probs_T(n, 1)
                    values(n, 0)
                if prev:
                    pe.wait_ge(c_oT, 2 * p + 1)
                    for c in range(4, 8):
                        last = tr(XB[:, (c - 4) * T:(c - 3) * T], on[:, 2 * c:2 * c + 2, :].rearrange("p h d -> p (h d)"),
                                  ident[:])
                    last.then_inc(t_oT, 1)
                if cur:
                    scores(n, 3)
                    probs_T(n, 2)
                    values(n, 1)
                if prev:
                    pe.wait_ge(c_oT, 2 * p + 2)
                    pe.wait_ge(c_anT, p + 1)
                    for c in range(PAIRS):
                        mm(XB[:, 0:H], oT[:, c, :], wo[:, c, :], start=(c == 0), stop=False)
                    mm(XB[:, 0:H], anT[:], nvw[:], start=False, stop=True).then_inc(t_out, 1)
                if nxt:
                    pe.wait_ge(e_qh, x + 1)
                    for half in range(2):
                        for c in range(4):
                            cc = 4 * half + c
                            last = tr(bq[:, half, c * T:(c + 1) * T], qh[:, 2 * cc:2 * cc + 2, :].rearrange("p h d -> p (h d)"),
                                      ident[:])
                        last.then_inc(t_qT, 1)
                        if half == 0:
                            pe.wait_ge(e_kk, x + 1)
                            pe.wait_ge(c_kv, x + 1)
                            if prev:
                                pe.wait_ge(c_anT, p + 1)
                            tr(MB[:, 0:T], kk[:].rearrange("p r d -> p (r d)"), ident[:]).then_inc(t_kT, 1)

            pe.wait_ge(one["v_xnT"], NG)
            pe.wait_ge(one["a_bias"], HGS)
            pe.wait_ge(one["v_nvw"], 1)
            pe.wait_ge(one["v_wkvn"], 1)
            step(-1, False, False, True)
            step(0, False, True, True)
            with pe.Fori(1, B - 1) as n:
                step(n, True, True, True)
            step(B - 1, True, True, False)
            step(B, True, False, False)

        @block.scalar
        def _(act):
            fn = nc.scalar.activation
            nc.scalar.preload_act_table_set("natural_log_exp_and_others")

            def rsqrt_seed(dst, tmp, src, s, base):
                fn(tmp, src, ACT.Ln).then_inc(s, 1)
                act.wait_ge(s, base + 1)
                fn(dst, tmp, ACT.Exp, scale=-0.5).then_inc(s, 1)

            for k in range(2):
                act.wait_ge(one["v_lnp"], k + 1)
                rsqrt_seed(pstat[:, 11:12], pstat[:, 10:11], pstat[:, 8:9], one["a_r1"], 2 * k)
                act.wait_ge(one["v_hg"], k + 1)
                fn(ph[:, 2, :], ph[:, 1, :], ACT.Exp, scale=-1.0).then_inc(one["a_e1"], 1)
            act.wait_ge(one["v_d"], 1)
            fn(rt[:, 1], rt[:, 0], ACT.Exp).then_inc(one["a_exp"], 1)
            GATE = (bk[1], bk[2])

            def gates(q, first):
                for c in range(MC):
                    act.wait_ge(m_gate, MC * q + c + 1)
                    if not first:
                        act.wait_ge(m_hu, MC * (q - 1) + c + 1)
                    fn(gs[:, c, :], GATE[c % 2][:], ACT.Copy, scale=SLOPE).then_inc(m_gs, 1)

            gates(0, True)
            act.wait_ge(one["v_nk"], 1)
            rsqrt_seed(nulls[:, 2:3], nulls[:, 1:2], nulls[:, 0:1], one["a_nk"], 0)

            with act.Fori(1, NG) as q:
                gates(q, False)
            for g in range(HGS):
                act.wait_ge(one["p_bias"], g + 1)
                fn(bias[:, g * HG:(g + 1) * HG, :].rearrange("p i t -> p (i t)"), bq[:, g % 2, :],
                   ACT.Copy).then_inc(one["a_bias"], 1)
            act.wait_ge(one["v_var"], 1)
            rsqrt_seed(rstd[:, 2, :], rstd[:, 1, :], rstd[:, 0, :], one["a_var"], 0)

            PTB, OB, MB, XB = bk[2], bk[3], bk[4], bk[5]

            def exps(m, g):
                act.wait_ge(e_nm, 4 * m + g + 1)
                if not isinstance(m, int) or 4 * m + g >= 2:
                    act.wait_ge(t_pT, 4 * m + g - 1)
                hs = slice(HG * g, HG * g + HG)
                fn(pn[:, hs], pnd[:, hs], ACT.Exp)
                for i in range(HG):
                    last = fn(pr[:, g % 2, i, :], ssb[:, g % 2, i, :], ACT.Exp, bias=nm[:, HG * g + i:HG * g + i + 1])
                last.then_inc(c_exp, 1)

            def probs_T(m, g):
                act.wait_ge(t_pT, 4 * m + g + 1)
                if not isinstance(m, int) or 4 * m + g >= 2:
                    act.wait_ge(t_av, 4 * m + g - 1)
                fn(pT[:, g % 2].rearrange("p i t -> p (i t)"), PTB[:], ACT.Copy).then_inc(c_pT, 1)

            def step(n, prev, cur, nxt):
                p, x = n - 1, n + 1
                if prev:
                    probs_T(p, 3)
                if cur:
                    exps(n, 0)
                if nxt:
                    act.wait_ge(t_q, 2 * x + 2)
                    if cur:
                        act.wait_ge(e_ss, x)
                    fn(q2[:].rearrange("p h d -> p (h d)"), bq[:].rearrange("p c n -> p (c n)"), ACT.Square).then_inc(c_q2, 1)
                if cur:
                    probs_T(n, 0)
                    exps(n, 1)
                if nxt:
                    act.wait_ge(t_kv, x + 1)
                    if cur:
                        act.wait_ge(g_v, x)
                        act.wait_ge(e_nl, 2 * x)
                    fn(kvs[:], MB[:, 0:NH + 2 * D], ACT.Copy).then_inc(c_kv, 1)
                if prev:
                    act.wait_ge(t_oT, 2 * p + 1)
                    if not isinstance(p, int) or p > 0:
                        act.wait_ge(t_out, p)
                    fn(oT[:, 0:4, :].rearrange("p c t -> p (c t)"), XB[:], ACT.Copy).then_inc(c_oT, 1)
                    act.wait_ge(t_anT, p + 1)
                    fn(anT[:], MB[0:NH, 256:256 + T], ACT.Copy).then_inc(c_anT, 1)
                if cur:
                    probs_T(n, 1)
                    exps(n, 2)
                if nxt:
                    act.wait_ge(e_ss, x + 1)
                    if cur:
                        act.wait_ge(e_nq, 3 * x)
                    rsqrt_seed(nw[:, 0, :], lns[:], ss[:], c_lnq, 2 * x)
                if prev:
                    act.wait_ge(t_oT, 2 * p + 2)
                    fn(oT[:, 4:8, :].rearrange("p c t -> p (c t)"), XB[:], ACT.Copy).then_inc(c_oT, 1)
                if cur:
                    probs_T(n, 2)
                    exps(n, 3)
                if prev:
                    act.wait_ge(e_var, p + 1)
                    rsqrt_seed(onw[:, 2:3], onw[:, 1:2], onw[:, 0:1], c_lno, 2 * p)
                if nxt:
                    for half in range(2):
                        act.wait_ge(t_qT, 2 * x + half + 1)
                        if cur:
                            act.wait_ge(t_s, 4 * x - 2 + 2 * half)
                        fn(qT[:, 4 * half:4 * half + 4, :].rearrange("p c t -> p (c t)"), bq[:, half, :],
                           ACT.Copy).then_inc(c_qT, 1)

            step(-1, False, False, True)
            step(0, False, True, True)
            with act.Fori(1, B - 1) as n:
                step(n, True, True, True)
            step(B - 1, True, True, False)
            step(B, True, False, False)

        @block.vector
        def _(dve):
            v = nc.vector
            done = [0]

            def link(ins):
                done[0] += 1
                ins.then_inc(v_set, 1)
                dve.wait_ge(v_set, done[0])

            def newton(dst, y, x, t):
                link(v.tensor_tensor(t, y, y, ALU.mult))
                link(v.scalar_tensor_tensor(out=t, in0=t, scalar=-0.5, in1=x, op0=ALU.mult, op1=ALU.mult))
                link(v.scalar_tensor_tensor(out=dst, in0=t, scalar=1.5, in1=y, op0=ALU.add, op1=ALU.mult))

            v.memset(ones[:], 1.0).then_inc(one["v_ones"], 1)
            v.memset(vaug[:, D:D + 1], 1.0)
            v.memset(relT[:, T:], NEG).then_inc(v_set, 1)
            done[0] += 1
            dve.wait_ge(one["p_wt"], 1)
            v.tensor_copy(wtT[:], bk[0][:, 0:E]).then_inc(one["v_wt"], 1)
            v.tensor_copy(wgT[:], bk[0][0:D, E:2 * E]).then_inc(one["v_wt"], 1)
            v.tensor_copy(condT[:], bk[0][0:D, 2 * E:2 * E + B]).then_inc(one["v_wt"], 1)
            for g in range(NG):
                dve.wait_ge(one["p_xT"], g + 1)
                v.tensor_copy(xT[:, g * GT:(g + 1) * GT], bk[1 + g][:]).then_inc(one["v_xT"], 1)
                if g == 0:
                    dve.wait_ge(one["p_gl"], 1)
                    link(v.tensor_copy(rs[0:B, 0, 0:E], bk[0][0:B, 64:64 + E]))
                    v.tensor_tensor(gl[:], rs[0:B, 0:1, 0:E].to_broadcast([B, B, E]),
                                    ident[0:B, 0:B].rearrange("p (b o) -> p b o", o=1).to_broadcast([B, B, E]),
                                    ALU.mult).then_inc(one["v_gld"], 1)

            def layer(k):
                link(v.bn_stats(pstat[:, 0:6], ph[:, 0, :]))
                link(v.bn_aggr(pstat[:, 6:8], pstat[:, 0:6]))
                v.tensor_scalar(pstat[:, 8:9], pstat[:, 7:8], LN_EPS, None, ALU.add).then_inc(one["v_lnp"], 1)
                dve.wait_ge(one["a_r1"], 2 * k)
                newton(pstat[:, 12:13], pstat[:, 11:12], pstat[:, 8:9], pstat[:, 13:14])
                link(v.tensor_scalar(ph[:, 3, :], ph[:, 0, :], pstat[:, 6:7], pstat[:, 12:13], ALU.subtract, ALU.mult))
                return v.tensor_tensor(ph[:, 1, :], ph[:, 3, :], (g0, g1)[k - 1][:], ALU.mult)

            def silu(k):
                dve.wait_ge(one["a_e1"], k)
                link(v.tensor_scalar(ph[:, 3, :], ph[:, 2, :], 1.0, None, ALU.add))
                link(v.reciprocal(ph[:, 2, :], ph[:, 3, :]))
                return v.tensor_tensor(ph[:, 0, :], ph[:, 1, :], ph[:, 2, :], ALU.mult)

            dve.wait_ge(l_pos, L_POS)
            link(v.scalar_tensor_tensor(out=ph[:, 0, :], in0=w0[:], scalar=pos[:, 0:1], in1=b0[:],
                                        op0=ALU.mult, op1=ALU.add))
            layer(1).then_inc(one["v_hg"], 1)
            silu(1).then_inc(one["v_hs"], 1)
            dve.wait_ge(one["p_h1T"], 1)
            v.tensor_copy(phT[:], bk[0][:, 0:H]).then_inc(one["v_hT"], 1)
            dve.wait_ge(one["p_h1"], 1)
            link(v.tensor_tensor(ph[:, 0, :], bk[0][:, 0:H], b1[:], ALU.add))
            layer(2).then_inc(one["v_hg"], 1)

            def by_batch(ap):
                return ap.rearrange("p (b o) -> p b o", o=1).to_broadcast([128, B, E])

            dve.wait_ge(one["p_lg"], 1)
            link(v.tensor_scalar(lg[:].rearrange("p b e -> p (b e)"), bk[5][:, 0:B * E], 0.5, None, ALU.mult))
            link(v.tensor_reduce(rs[:, 1, :], lg[:], AX.X, ALU.max))
            v.tensor_tensor(rt[:, 0], lg[:], by_batch(rs[:, 1, :]), ALU.subtract).then_inc(one["v_d"], 1)

            def first_of(dst, src, largest, r):
                link(v.tensor_tensor(dst, src, by_batch(largest), ALU.is_equal))
                link(v.tensor_tensor(dst, dst, rank[:], ALU.mult))
                link(v.tensor_reduce(rs[:, r, :], dst, AX.X, ALU.max))
                link(v.tensor_tensor(dst, dst, by_batch(rs[:, r, :]), ALU.is_equal))

            first_of(rt[:, 2], lg[:], rs[:, 1, :], 2)
            link(v.scalar_tensor_tensor(out=rt[:, 4], in0=rt[:, 2], scalar=NEG, in1=lg[:], op0=ALU.mult, op1=ALU.add))
            link(v.tensor_reduce(rs[:, 3, :], rt[:, 4], AX.X, ALU.max))
            first_of(rt[:, 5], rt[:, 4], rs[:, 3, :], 4)
            link(v.tensor_tensor(rt[:, 2], rt[:, 2], rt[:, 5], ALU.add))
            dve.wait_ge(one["a_exp"], 1)
            link(v.tensor_tensor(rt[:, 6], rt[:, 2], rt[:, 1], ALU.mult))
            link(v.tensor_reduce(rs[:, 5, :], rt[:, 6], AX.X, ALU.add))
            link(v.tensor_reduce(rs[:, 6, :], rt[:, 1], AX.X, ALU.add))
            link(v.scalar_tensor_tensor(out=rs[:, 7, :], in0=rs[:, 6, :], scalar=1e-20, in1=rs[:, 5, :],
                                        op0=ALU.mult, op1=ALU.add))
            link(v.reciprocal(rs[:, 0, :], rs[:, 7, :]))
            link(v.tensor_tensor(rt[:, 7], rt[:, 6], by_batch(rs[:, 0, :]), ALU.mult))
            link(v.tensor_copy(identb[:], ident[:]))
            link(v.tensor_copy(esel[:], eself[:]))
            link(v.tensor_copy(cp[:, :, 0, :], rt[:, 7]))
            link(v.tensor_tensor(rt[:, 0], rt[:, 7], cp[:, :, 0, :], ALU.subtract))
            link(v.tensor_copy(cp[:, :, 1, :], rt[:, 0]))
            link(v.tensor_tensor(rt[:, 3], rt[:, 0], cp[:, :, 1, :], ALU.subtract))
            v.tensor_copy(cp[:, :, 2, :], rt[:, 3]).then_inc(one["v_cp"], 1)

            silu(2).then_inc(one["v_hs"], 1)
            for half in range(2):
                dve.wait_ge(one["p_cT"], 1)
                v.tensor_copy(cT[:, half * 1024:(half + 1) * 1024],
                              bk[1 + half][:].bitcast(BF16)[0:3 * E, :]).then_inc(one["v_cT"], 1)
            dve.wait_ge(one["p_h2T"], 1)
            v.tensor_copy(phT[:], bk[0][:, 0:H]).then_inc(one["v_hT"], 1)
            dve.wait_ge(one["p_rel"], 1)
            v.tensor_tensor(rel[:], bk[0][:, 0:NH], b2[:], ALU.add).then_inc(one["v_relT"], 1)
            dve.wait_ge(one["p_relT"], 1)
            v.tensor_copy(relT[:, 0:T], bk[0][0:NH, 0:T]).then_inc(one["v_relT"], 1)

            GATE, UP, CB, Y = (bk[1], bk[2]), (bk[3], bk[4]), bk[5], bq[:, 0, :]

            def chunk(q, c, first):
                dve.wait_ge(m_gs, MC * q + c + 1)
                v.tensor_tensor(gs[:, c, :], gs[:, c, :], GATE[c % 2][:], ALU.max).then_inc(m_lk, 1)
                dve.wait_ge(m_up, MC * q + c + 1)
                dve.wait_ge(m_lk, MC * q + c + 1)
                if c < EC:
                    v.tensor_tensor(hub[:, c % 2, :], gs[:, c, :], UP[c % 2][:], ALU.mult).then_inc(m_hu, 1)
                    dve.wait_ge(m_hu, MC * q + c + 1)
                    dve.wait_ge(m_cb, EC * q + c + 1)
                if not first:
                    dve.wait_ge(m_y, q)
                if c < EC:
                    v.tensor_tensor(hh[:, c, :], hub[:, c % 2, :], CB[:], ALU.mult).then_inc(m_h, 1)
                else:
                    v.tensor_tensor(hh[:, c, :], gs[:, c, :], UP[c % 2][:], ALU.mult).then_inc(m_hu, 1)

            def residual(q):
                x_q, xc_q = xa[:, bass.ds(q * GB, GB), :], xc[:, bass.ds(q * GB, GB), :]
                dve.wait_ge(m_y, q + 1)
                v.tensor_tensor(x_q, x_q, Y.rearrange("p (b h) -> p b h", b=GB), ALU.add).then_inc(m_x1, 1)
                dve.wait_ge(m_x1, q + 1)
                settle(dve)
                v.tensor_reduce(msum[:], x_q, AX.X, ALU.add).then_inc(m_st, 1)
                dve.wait_ge(m_st, 4 * q + 1)
                v.tensor_scalar(nmean[:], msum[:], 1.0 / H, None, ALU.mult).then_inc(m_st, 1)
                dve.wait_ge(m_st, 4 * q + 2)
                v.tensor_tensor(xc_q, x_q, nmean[:].rearrange("p (b o) -> p b o", o=1).to_broadcast([128, GB, H]),
                                ALU.subtract).then_inc(m_st, 1)

            def variance(q):
                dve.wait_ge(m_sq, q + 1)
                settle(dve)
                v.tensor_reduce(var[:, bass.ds(q * GB, GB)], sq[:], AX.X, ALU.add).then_inc(m_st, 1)

            def group(q, first):
                for c in range(MC):
                    chunk(q, c, first)
                    if c == 1 and not first:
                        residual(q - 1)
                    if c == 3 and not first:
                        variance(q - 1)

            group(0, True)

            dve.wait_ge(l_att, L_ATT)
            v.tensor_scalar(nvblk[:].rearrange("p c h -> p (c h)"), nsel[:].rearrange("p c h -> p (c h)"),
                            nvcol[:, 0:1], None, ALU.mult).then_inc(one["v_nv"], 1)
            SCALE = 8.0 * NORM_SCALE * NORM_SCALE
            link(v.tensor_scalar(ksc8[:], ksc[:], qsc[:, 0:1], SCALE, ALU.mult, ALU.mult))
            link(v.tensor_tensor_reduce(k2[:], nkrow[:], nkrow[:], 1.0, 0.0, ALU.mult, ALU.add, nulls[:, 3:4]))
            v.tensor_scalar(nulls[:, 0:1], nulls[:, 3:4], NORM_MIN ** 2, NORM_SCALE ** 2, ALU.max,
                            ALU.mult).then_inc(one["v_nk"], 1)
            link(v.tensor_tensor(qrow[:], qrow[:], krow[:], ALU.mult))
            dve.wait_ge(one["a_nk"], 2)
            newton(nulls[:, 4:5], nulls[:, 2:3], nulls[:, 0:1], nulls[:, 5:6])
            link(v.scalar_tensor_tensor(out=krow[:], in0=nkrow[:], scalar=nulls[:, 4:5], in1=qrow[:],
                                        op0=ALU.mult, op1=ALU.mult))
            link(v.tensor_scalar(nkrow[:], krow[:], SCALE, None, ALU.mult))
            link(v.tensor_tensor(q2[:], wq[:].rearrange("p (h d) -> p h d", d=D),
                                 nkrow[:].rearrange("p (o d) -> p o d", o=1).to_broadcast([128, NH, D]), ALU.mult))
            v.tensor_reduce(wkvn[:, 0:NH], q2[:], AX.X, ALU.add).then_inc(one["v_wkvn"], 1)

            with dve.Fori(1, NG) as q:
                group(q, False)
            residual(NG - 1)
            variance(NG - 1)
            dve.wait_ge(m_st, 4 * NG)
            v.tensor_scalar(rstd[:, 0, :], var[:], 1.0 / H, LN_EPS, ALU.mult, ALU.add).then_inc(one["v_var"], 1)
            dve.wait_ge(one["a_var"], 2)
            newton(rstd[:, 3, :], rstd[:, 2, :], rstd[:, 0, :], rstd[:, 1, :])
            for g in range(NG):
                gg = slice(g * GB, (g + 1) * GB)
                v.tensor_tensor(xc[:, gg, :], xc[:, gg, :],
                                rstd[:, 3, gg].rearrange("p (b o) -> p b o", o=1).to_broadcast([128, GB, H]),
                                ALU.mult).then_inc(one["v_xn"], 1)
            dve.wait_ge(one["p_nvw"], 1)
            v.tensor_copy(nvw[:], bk[0][0:NH, 0:H]).then_inc(one["v_nvw"], 1)
            for g in range(NG):
                dve.wait_ge(one["p_xnT"], g + 1)
                v.tensor_scalar(xT[:, g * GT:(g + 1) * GT], bk[1 + g][:], gnorm[:, 0:1], None,
                                ALU.mult).then_inc(one["v_xnT"], 1)

            SB, OB, MB, XB = (bk[0], bk[1]), bk[3], bk[4], bk[5]

            def scores(m, g):
                dve.wait_ge(t_s, 4 * m + g + 1)
                dve.wait_ge(g_bias, 4 * m + g + 1)
                if not isinstance(m, int) or 4 * m + g >= 2:
                    dve.wait_ge(c_exp, 4 * m + g - 1)
                settle(dve)
                for i in range(HG):
                    h = HG * g + i
                    last = v.tensor_tensor_reduce(ssb[:, g % 2, i, :], SB[g % 2][:, i * T:(i + 1) * T], biasm[:, h, :],
                                                  1.0, -3e38, ALU.add, ALU.max, mx[:, h:h + 1])
                last.then_inc(e_s, 1)
                hs = slice(HG * g, HG * g + HG)
                dve.wait_ge(e_s, 4 * m + g + 1)
                v.scalar_tensor_tensor(out=nm[:, hs], in0=mx[:, hs], scalar=-1.0, in1=nnl[:, 0, hs],
                                       op0=ALU.mult, op1=ALU.min).then_inc(e_mx, 1)
                dve.wait_ge(e_mx, 4 * m + g + 1)
                v.tensor_tensor(pnd[:, hs], nm[:, hs], nnl[:, 0, hs], ALU.subtract).then_inc(e_nm, 1)

            def normalise(m, g):
                o_g = OB[:, 0:HG * (D + 1)].rearrange("p (i d) -> p i d", d=D + 1)
                hs = slice(HG * g, HG * g + HG)
                dve.wait_ge(t_av, 4 * m + g + 1)
                v.tensor_tensor(den[:, 0, :], o_g[:, :, D], pn[:, hs], ALU.add).then_inc(e_dn, 1)
                dve.wait_ge(e_dn, 8 * m + 2 * g + 1)
                v.reciprocal(den[:, 1, :], den[:, 0, :]).then_inc(e_dn, 1)
                dve.wait_ge(e_dn, 8 * m + 2 * g + 2)
                if not isinstance(m, int) or m > 0:
                    dve.wait_ge(t_oT, 2 * m - 1 + g // 2)
                    dve.wait_ge(t_anT, m)
                v.tensor_tensor(head_view(an[:], g), pn[:, hs], den[:, 1, :], ALU.mult)
                on_g = on[:].rearrange("p (G i r) d -> p G r i d", G=2, r=2)[:, g // 2, g % 2]
                v.tensor_tensor(on_g, o_g[:, :, 0:D],
                                den[:, 1, :].rearrange("p (i o) -> p i o", o=1).to_broadcast([128, HG, D]),
                                ALU.mult).then_inc(e_on, 1)

            def norms(x, later):
                dve.wait_ge(c_kv, x + 1)
                if later:
                    dve.wait_ge(c_lnq, 2 * x)
                v.tensor_tensor_reduce(k2[:], kvs[:, NH:NH + D], kvs[:, NH:NH + D], 1.0, 0.0, ALU.mult, ALU.add,
                                       ss[:, NH:NH + 1]).then_inc(e_sq, 1)
                dve.wait_ge(c_q2, x + 1)
                v.tensor_reduce(ss[:, 0:NH], q2[:], AX.X, ALU.add).then_inc(e_sq, 1)
                dve.wait_ge(e_sq, 2 * x + 2)
                v.tensor_scalar(ss[:], ss[:], NORM_MIN ** 2, NORM_SCALE ** 2, ALU.max, ALU.mult).then_inc(e_ss, 1)

            def units(x, later):
                dve.wait_ge(c_lnq, 2 * x + 2)
                v.tensor_tensor(nw[:, 1, :], nw[:, 0, :], nw[:, 0, :], ALU.mult).then_inc(e_nq, 1)
                dve.wait_ge(e_nq, 3 * x + 1)
                v.scalar_tensor_tensor(out=nw[:, 1, :], in0=nw[:, 1, :], scalar=-0.5, in1=ss[:],
                                       op0=ALU.mult, op1=ALU.mult).then_inc(e_nq, 1)
                dve.wait_ge(e_nq, 3 * x + 2)
                v.scalar_tensor_tensor(out=nw[:, 2, :], in0=nw[:, 1, :], scalar=1.5, in1=nw[:, 0, :],
                                       op0=ALU.add, op1=ALU.mult).then_inc(e_nq, 1)
                dve.wait_ge(e_nq, 3 * x + 3)
                if later:
                    dve.wait_ge(t_qT, 2 * x)
                    dve.wait_ge(t_kT, x)
                v.tensor_scalar(kk[:], kvs[:, NH:NH + D].rearrange("p (o d) -> p o d", o=1).to_broadcast([128, 2, D]),
                                nw[:, 2, NH:NH + 1], None, ALU.mult).then_inc(e_kk, 1)
                v.tensor_tensor(qh[:], bq[:].rearrange("p c (h d) -> p (c h) d", d=D),
                                nw[:, 2, 0:NH].rearrange("p (h o) -> p h o", o=1).to_broadcast([128, NH, D]),
                                ALU.mult).then_inc(e_qh, 1)

            def null_logits(x):
                v.scalar_tensor_tensor(out=nnl[:, 1, :], in0=kvs[:, 0:NH], scalar=-1.0, in1=nw[:, 2, 0:NH],
                                       op0=ALU.mult, op1=ALU.mult).then_inc(e_nl, 1)
                dve.wait_ge(e_nl, 2 * x + 1)
                order = "p (G i r) -> p G r i"
                for G in range(2):
                    last = v.tensor_tensor(nnl[:, 0, :].rearrange("p (G r i) -> p G r i", G=2, r=2)[:, G],
                                           nnl[:, 1, :].rearrange(order, G=2, r=2)[:, G],
                                           nullb[:].rearrange(order, G=2, r=2)[:, G], ALU.subtract)
                last.then_inc(e_nl, 1)

            def output(p, later):
                dve.wait_ge(t_out, p + 1)
                v.bn_stats(ost[:], XB[:, 0:H]).then_inc(e_st, 1)
                dve.wait_ge(e_st, 2 * p + 1)
                settle(dve)
                v.bn_aggr(omv[:], ost[:]).then_inc(e_st, 1)
                dve.wait_ge(e_st, 2 * p + 2)
                if later:
                    dve.wait_ge(c_lno, 2 * p)
                v.tensor_scalar(onw[:, 0:1], omv[:, 1:2], LN_EPS, None, ALU.add).then_inc(e_var, 1)
                dve.wait_ge(c_lno, 2 * p + 2)
                v.tensor_tensor(onw[:, 3:4], onw[:, 2:3], onw[:, 2:3], ALU.mult).then_inc(e_no, 1)
                dve.wait_ge(e_no, 3 * p + 1)
                v.scalar_tensor_tensor(out=onw[:, 3:4], in0=onw[:, 3:4], scalar=-0.5, in1=onw[:, 0:1],
                                       op0=ALU.mult, op1=ALU.mult).then_inc(e_no, 1)
                dve.wait_ge(e_no, 3 * p + 2)
                v.scalar_tensor_tensor(out=onw[:, 4:5], in0=onw[:, 3:4], scalar=1.5, in1=onw[:, 2:3],
                                       op0=ALU.add, op1=ALU.mult).then_inc(e_no, 1)
                dve.wait_ge(e_no, 3 * p + 3)
                if later:
                    dve.wait_ge(g_o, 2 * p)
                v.tensor_scalar(olin[:], XB[:, 0:H], omv[:, 0:1], onw[:, 4:5], ALU.subtract,
                                ALU.mult).then_inc(e_out, 1)

            def step(n, prev, cur, nxt):
                p, x = n - 1, n + 1
                later = not isinstance(p, int) or p > 0
                if prev:
                    normalise(p, 2)
                if cur:
                    scores(n, 0)
                    scores(n, 1)
                if prev:
                    normalise(p, 3)
                if cur:
                    scores(n, 2)
                if nxt:
                    norms(x, cur)
                if cur:
                    normalise(n, 0)
                if nxt:
                    units(x, cur)
                if cur:
                    scores(n, 3)
                if nxt:
                    null_logits(x)
                if cur:
                    normalise(n, 1)
                if prev:
                    output(p, later)
                if nxt:
                    dve.wait_ge(t_kT, x + 1)
                    if cur:
                        dve.wait_ge(t_s, 4 * x)
                    v.tensor_scalar(kT[:], MB[:, 0:T], ksc8[:, 0:1], None, ALU.mult).then_inc(e_kT, 1)

            step(-1, False, False, True)
            step(0, False, True, True)
            with dve.Fori(1, B - 1) as n:
                step(n, True, True, True)
            step(B - 1, True, True, False)
            step(B, True, False, False)

        @block.gpsimd
        def _(pool):
            g_ = nc.gpsimd

            pool.wait_ge(l_mask, 16)
            g_.tensor_scalar(maskb[:], masku[:], -1.0, -NEG, ALU.add, ALU.mult).then_inc(one["g_mask"], 1)

            def squares(q):
                pool.wait_ge(m_st, 4 * q + 3)
                xc_q = xc[:, bass.ds(q * GB, GB), :]
                settle(pool)
                g_.tensor_tensor(sq[:], xc_q, xc_q, ALU.mult).then_inc(m_sq, 1)

            with pool.Fori(0, NG) as q:
                squares(q)

            def tokens(m):
                if not isinstance(m, int) or m > 0:
                    pool.wait_ge(t_kv, m)
                settle(pool)
                g_.tensor_copy(xnb[:], xT[:, bass.ds(m * T, T)]).then_inc(g_xn, 1)

            def masked_bias(m, g):
                if not isinstance(m, int) or m > 0:
                    pool.wait_ge(e_s, 4 * m - 4 + g + 1)
                hs = slice(HG * g, HG * g + HG)
                settle(pool)
                g_.tensor_tensor(biasm[:, hs, :], bias[:, hs, :], maskb[:, bass.ds(m, 1), :].to_broadcast([128, HG, T]),
                                 ALU.add).then_inc(g_bias, 1)

            def batch_values(m):
                pool.wait_ge(c_kv, m + 1)
                if not isinstance(m, int) or m > 0:
                    pool.wait_ge(t_av, 4 * m)
                settle(pool)
                g_.tensor_copy(vaug[:, 0:D], kvs[:, NH + D:NH + 2 * D]).then_inc(g_v, 1)

            def output(p):
                pool.wait_ge(e_out, p + 1)
                g_.tensor_tensor(osc[:], olin[:], gout[:], ALU.mult).then_inc(g_o, 1)
                pool.wait_ge(g_o, 2 * p + 1)
                if not isinstance(p, int) or p > 0:
                    pool.wait_ge(d_out, 16 * p)
                settle(pool)
                g_.tensor_tensor(ores[:], osc[:], xa[:, bass.ds(p, 1), :].rearrange("p o h -> p (o h)"),
                                 ALU.add).then_inc(g_o, 1)

            def step(n, prev, cur, nxt, more):
                p, x = n - 1, n + 1
                if cur:
                    batch_values(n)
                if nxt:
                    for g in range(HGS):
                        if g == 3 and more:
                            tokens(x + 1)
                        masked_bias(x, g)
                if prev:
                    output(p)

            pool.wait_ge(one["v_xnT"], NG)
            tokens(0)
            pool.wait_ge(one["a_bias"], HGS)
            pool.wait_ge(one["g_mask"], 1)
            step(-1, False, False, True, True)
            step(0, False, True, True, True)
            with pool.Fori(1, B - 2) as n:
                step(n, True, True, True, True)
            step(B - 2, True, True, True, False)
            step(B - 1, True, True, False, False)
            step(B, True, False, False, False)


_INS = ["x", "cond_64", "mask_BxS_bf1", "L0_cond_wt", "L0_cond_wg", "L0_cond_w_gate", "L0_cond_w_up",
        "L0_cond_w_down", "L0_cond_sw_gate", "L0_cond_sw_up", "L0_cond_sw_down", "L1_cond_g_norm", "L1_cond_Wq",
        "L1_cond_Wkv", "L1_cond_q_scale", "L1_cond_k_scale", "L1_cond_null_attn_bias", "L1_cond_w0", "L1_cond_b0",
        "L1_cond_g0", "L1_cond_w1", "L1_cond_b1", "L1_cond_g1", "L1_cond_w2", "L1_cond_b2", "L1_cond_Wout",
        "L1_cond_g_out"]


def shape_constants():
    eye = np.eye(128, dtype=np.float32)
    esel = np.zeros((3, E, EC, 128), np.float32)
    for e in range(E):
        esel[:, e, e // 2, (e % 2) * M:(e % 2 + 1) * M] = 1.0
    nsel = np.zeros((128, PAIRS, NH), np.float32)
    for c in range(PAIRS):
        for r in range(2):
            nsel[r * D:(r + 1) * D, c, 2 * c + r] = 1.0
    return {
        "c_ident": eye,
        "c_flip": np.ascontiguousarray(eye[::-1]),
        "c_esel": esel.reshape(3 * E, EC, 128),
        "c_nsel": nsel,
        "c_pos": np.arange(T, dtype=np.float32).reshape(T, 1),
        "c_rank": np.tile(np.arange(E, 0, -1, dtype=np.float32), (B, 1)),
    }


def kernel(**inputs):
    import concourse.bacc as _bacc
    from concourse import mybir as _mybir
    from concourse.bass_utils import run_bass_kernel_spmd as _run

    nc = _bacc.Bacc("TRN2", target_bir_lowering=False, num_devices=1)
    arrays, aps = {}, {}
    named = [(n, np.ascontiguousarray(inputs[n])) for n in _INS] + list(shape_constants().items())
    for name, v in named:
        if v.dtype == np.bool_:
            v = v.view(np.uint8)
        arrays[f"in_{name}"] = v
        aps[name] = nc.dram_tensor(f"in_{name}", v.shape, _mybir.dt.from_np(v.dtype), kind="ExternalInput").ap()
    aps["mask"] = aps["mask_BxS_bf1"]
    out = nc.dram_tensor("out_0", (B, T, H), F32, kind="ExternalOutput").ap()
    build(nc, aps, out)
    r = _run(nc, [arrays], core_ids=[0])
    return np.asarray(r.results[0]["out_0"])
```

```python
from contextlib import ExitStack

import numpy as np

import concourse.bass as bass
from concourse import mybir

F32 = mybir.dt.float32
BF16 = mybir.dt.bfloat16
F16 = mybir.dt.float16
U8 = mybir.dt.uint8
ALU = mybir.AluOpType
ACT = mybir.ActivationFunctionType
AX = mybir.AxisListType

B, T, H = 16, 128, 128
E, M = 8, 64
NH, D = 16, 64
EC = E * M // 128
MC = EC + 1
GB = 4
NG = B // GB
GT = GB * T
HG = 4
HGS = NH // HG
PAIRS = NH // 2
LN_EPS = 1e-5
NEG = -1e30
NORM_MIN = 1e-12
NORM_SCALE = 256.0
SLOPE = 0.01
REL = 2 * T - 1


def head_view(ap, g):
    v = ap.rearrange("p (G i r) -> p G r i", G=NH // 8, r=2)
    return v[:, g // 2, g % 2, :]


def build(nc, a, out):
    ctx = ExitStack()
    with ctx:
        def sb(name, shape, dt=F32):
            return ctx.enter_context(nc.sbuf_tensor(name, shape, dt))

        def psum(name, shape, dt=F32):
            return ctx.enter_context(nc.psum_tensor(name, shape, dt))

        def sem(name):
            return ctx.enter_context(nc.semaphore(name))

        ident = sb("ident", [128, 128])
        identb = sb("identb", [128, 128], BF16)
        flip = sb("flip", [128, 128])
        esel = sb("esel", [3 * E, EC, 128], BF16)
        eself = sb("eself", [3 * E, EC, 128])
        nsel = sb("nsel", [128, PAIRS, NH])
        pos = sb("pos", [128, 1])
        rank = sb("rank", [128, B, E])
        ones = sb("ones", [128, 128])
        wg = sb("wg", [128, MC, 128])
        wu = sb("wu", [128, MC, 128])
        wd = sb("wd", [128, MC, 128])
        wq = sb("wq", [128, NH * D])
        wkvn = sb("wkvn", [128, NH + 2 * D])
        wo = sb("wo", [128, PAIRS, 128])
        wt8 = sb("wt8", [E, H])
        wg8 = sb("wg8", [E, D])
        cond = sb("cond", [B, D])
        wtT = sb("wtT", [128, E])
        wgT = sb("wgT", [D, E])
        condT = sb("condT", [D, B])
        gl = sb("gl", [B, B, E])
        gnorm = sb("gnorm", [128, 1])
        gout = sb("gout", [128, H])
        qsc = sb("qsc", [128, 1])
        ksc = sb("ksc", [128, 1])
        ksc8 = sb("ksc8", [128, 1])
        nvcol = sb("nvcol", [128, 1])
        nvblk = sb("nvblk", [128, PAIRS, NH])
        nvw = sb("nvw", [NH, H])
        nkrow = sb("nkrow", [128, D])
        qrow = sb("qrow", [128, D])
        krow = sb("krow", [128, D])
        nullb = sb("nullb", [128, NH])
        nulls = sb("nulls", [128, 8])
        w0 = sb("w0", [128, H])
        b0 = sb("b0", [128, H])
        g0 = sb("g0", [128, H])
        b1 = sb("b1", [128, H])
        g1 = sb("g1", [128, H])
        w1 = sb("w1", [128, H])
        w2 = sb("w2", [128, NH])
        b2 = sb("b2", [128, NH])
        ph = sb("ph", [128, 4, H])
        phT = sb("phT", [128, H])
        pstat = sb("pstat", [128, 16])
        rel = sb("rel", [128, NH])
        relT = sb("relT", [NH, REL])
        bias = sb("bias", [128, NH, T])
        biasr = sb("biasr", [128, NH, T])
        masku = sb("masku", [128, B, T], U8)
        maskb = sb("maskb", [128, B, T])
        biasm = sb("biasm", [128, NH, T])
        xa = sb("xa", [128, B, H])
        xT = sb("xT", [128, B * T])
        xc = sb("xc", [128, B, H])
        sq = sb("sq", [128, GB, H])
        msum = sb("msum", [128, GB])
        nmean = sb("nmean", [128, GB])
        var = sb("var", [128, B])
        rstd = sb("rstd", [128, 4, B])
        lg = sb("lg", [128, B, E])
        rt = sb("rt", [128, 8, B, E])
        rs = sb("rs", [128, 8, B])
        cp = sb("cp", [128, B, 3, E], BF16)
        cT = sb("cT", [3 * E, B * T], BF16)
        gs = sb("gs", [128, MC, GT])
        hub = sb("hub", [128, 2, GT])
        hh = sb("hh", [128, MC, GT])
        xnb = sb("xnb", [128, T])
        q2 = sb("q2", [128, NH, D])
        kvs = sb("kvs", [128, NH + 2 * D])
        vaug = sb("vaug", [128, 2, D + 1], F16)
        fro = sb("fro", [128, 8])
        ss = sb("ss", [128, NH + 1])
        nw = sb("nw", [128, 4, NH + 1])
        lns = sb("lns", [128, NH + 1])
        qh = sb("qh", [128, NH, D])
        kk = sb("kk", [128, 2, D])
        nmr = sb("nmr", [128, 1])
        k2 = sb("k2", [128, D])
        qT = sb("qT", [128, PAIRS, T])
        kT = sb("kT", [128, T])
        nnl = sb("nnl", [128, 2, NH])
        ssb = sb("ssb", [128, 2, HG, T])
        mx = sb("mx", [128, NH])
        nm = sb("nm", [128, NH])
        pnd = sb("pnd", [128, NH])
        pn = sb("pn", [128, NH])
        pr = sb("pr", [128, 2, HG, T])
        pTh = sb("pTh", [128, 2, HG, T], F16)
        pTl = sb("pTl", [128, 2, HG, T], F16)
        den = sb("den", [128, 2, HG])
        on = sb("on", [128, NH, D])
        an = sb("an", [128, NH])
        oT = sb("oT", [128, PAIRS, T])
        anT = sb("anT", [NH, T])
        ost = sb("ost", [128, 6])
        omv = sb("omv", [128, 2])
        onw = sb("onw", [128, 6])
        olin = sb("olin", [128, H])
        osc = sb("osc", [128, H])
        ores = sb("ores", [128, H])

        bk = [psum(f"bk{i}", [128, 512]) for i in range(6)]
        bq = psum("bq", [128, 2, 512])

        scratch = nc.dram_tensor("relbias_scratch", (NH, REL), F32, kind="Internal").ap()

        l_pos, l_x, l_route, l_moe, l_att, l_mask = (sem(n) for n in (
            "l_pos", "l_x", "l_route", "l_moe", "l_att", "l_mask"))
        d_rel, d_bias, d_out = sem("d_rel"), sem("d_bias"), sem("d_out")
        one = {n: sem(n) for n in (
            "p_wt", "p_gl", "p_xT", "p_lg", "p_cT", "p_h1T", "p_h1", "p_h2T", "p_rel", "p_relT", "p_nvw", "p_bias", "p_xnT",
            "a_e1", "a_e2", "a_r1", "a_exp", "a_ln", "a_var", "a_nk", "a_bias",
            "v_wt", "v_gl", "v_gld", "v_xT", "v_d", "v_cp", "v_cT", "v_hs", "v_hg", "v_hT", "v_relT", "v_var", "v_xn",
            "v_xnT", "v_nk", "v_nv", "v_nvw", "v_wkvn", "v_lnp", "v_ones", "v_fro", "v_wo", "p_fro", "a_fro", "g_mask")}
        v_set, a_set = sem("v_set"), sem("a_set")
        m_gate, m_up, m_cb, m_y, m_gs, m_lk, m_hu, m_h, m_x1, m_st, m_sq = (sem(n) for n in (
            "m_gate", "m_up", "m_cb", "m_y", "m_gs", "m_lk", "m_hu", "m_h", "m_x1", "m_st", "m_sq"))
        t_s, t_pT, t_av, t_q, t_kv, t_qT, t_kT, t_oT, t_anT, t_out = (sem(n) for n in (
            "t_s", "t_pT", "t_av", "t_q", "t_kv", "t_qT", "t_kT", "t_oT", "t_anT", "t_out"))
        c_exp, c_pT, c_q2, c_kv, c_kk, c_kT, c_qT, c_oT, c_anT, c_lnq, c_lno, c_out = (sem(n) for n in (
            "c_exp", "c_pT", "c_q2", "c_kv", "c_kk", "c_kT", "c_qT", "c_oT", "c_anT", "c_lnq", "c_lno", "c_out"))
        e_s, e_mx, e_nm, e_pl, e_dn, e_on, e_sq, e_ss, e_nq, e_qh, e_nl, e_st, e_var, e_no, e_mr = (
            sem(n) for n in ("e_s", "e_mx", "e_nm", "e_pl", "e_dn", "e_on", "e_sq", "e_ss", "e_nq", "e_qh", "e_nl",
                             "e_st", "e_var", "e_no", "e_mr"))
        settled = sem("settled")
        g_xn, g_bias, g_v, g_o = (sem(n) for n in ("g_xn", "g_bias", "g_v", "g_o"))

        block = ctx.enter_context(nc.Block())

        def settle(engine):
            engine.sem_inc(settled, 1)

        def live(m):
            return not isinstance(m, int) or 0 <= m < B

        def later(m):
            return not isinstance(m, int) or m > 0

        @block.sync
        def _(sp):
            def load(dst, src, s):
                sp.dma_start(dst, src).then_inc(s, 16)

            def row(v):
                return v.rearrange("(o n) -> o n", o=1).partition_broadcast(128) if len(v.shape) == 1 else v

            for g in range(NG):
                load(xa[:, g * GB:(g + 1) * GB, :], a["x"][g * GB:(g + 1) * GB].rearrange("b t h -> t b h"), l_x)
                if g == 0:
                    load(ident[:], a["c_ident"], l_route)
                    load(wt8[:], a["L0_cond_wt"], l_route)
                    load(wg8[:], a["L0_cond_wg"], l_route)
                    load(cond[:], a["cond_64"], l_route)
                    load(rank[:], a["c_rank"].rearrange("(o b) e -> o b e", o=1).to_broadcast([128, B, E]), l_route)
                    load(eself[:], a["c_esel"], l_route)
            load(pos[:], a["c_pos"], l_pos)
            for dst, name in ((w0, "w0"), (b0, "b0"), (g0, "g0"), (b1, "b1"), (g1, "g1")):
                v = a["L1_cond_" + name]
                v = v if len(v.shape) == 2 else v.rearrange("(o n) -> o n", o=1)
                load(dst[:], v.to_broadcast([128, H]), l_pos)
            load(b2[:], a["L1_cond_b2"].rearrange("(o n) -> o n", o=1).to_broadcast([128, NH]), l_pos)
            load(w1[:], a["L1_cond_w1"], l_pos)
            load(w2[:], a["L1_cond_w2"], l_pos)
            load(flip[:], a["c_flip"], l_pos)
            for dst, ex, sh in ((wg, "L0_cond_w_gate", "L0_cond_sw_gate"), (wu, "L0_cond_w_up", "L0_cond_sw_up")):
                load(dst[:, 0:EC, :].rearrange("p c (e m) -> p (c e) m", m=M), a[ex].rearrange("e h m -> h e m"), l_moe)
                load(dst[:, EC, :], a[sh], l_moe)
            load(wd[:, 0:EC, :], a["L0_cond_w_down"].rearrange("(c e) m h -> (e m) c h", e=2), l_moe)
            load(wd[:, EC, :], a["L0_cond_sw_down"], l_moe)
            load(masku[:], a["mask"].rearrange("(o b) t -> o b t", o=1).to_broadcast([128, B, T]), l_mask)
            load(wq[:], a["L1_cond_Wq"], l_att)
            load(wkvn[:, NH:], a["L1_cond_Wkv"], l_att)
            load(wo[:], a["L1_cond_Wout"].rearrange("(c p) n -> p c n", p=128), l_att)
            load(nsel[:], a["c_nsel"], l_att)
            load(gnorm[:], a["L1_cond_g_norm"].rearrange("(n o) -> n o", o=1), l_att)
            load(gout[:], a["L1_cond_g_out"].rearrange("(o n) -> o n", o=1).to_broadcast([128, H]), l_att)
            load(nullb[:], a["L1_cond_null_attn_bias"].rearrange("(o n) -> o n", o=1).to_broadcast([128, NH]), l_att)
            for half in range(2):
                hs = slice(half * D, (half + 1) * D)
                load(qsc[hs], a["L1_cond_q_scale"].rearrange("(n o) -> n o", o=1), l_att)
                load(ksc[hs], a["L1_cond_k_scale"].rearrange("(n o) -> n o", o=1), l_att)
                load(nvcol[hs], a["cond_64"][1:2, :].rearrange("o n -> n o"), l_att)
            load(nkrow[:], a["cond_64"][0:1, :].to_broadcast([128, D]), l_att)
            load(qrow[:], a["L1_cond_q_scale"].rearrange("(o n) -> o n", o=1).to_broadcast([128, D]), l_att)
            load(krow[:], a["L1_cond_k_scale"].rearrange("(o n) -> o n", o=1).to_broadcast([128, D]), l_att)
            sp.wait_ge(one["v_relT"], 2)
            sp.dma_start(scratch, relT[:]).then_inc(d_rel, 16)
            sp.wait_ge(d_rel, 16)
            for g in range(HGS):
                first = (8 * (g // 2) + g % 2) * REL
                src = bass.AP(tensor=scratch.tensor, offset=first, ap=[[1, 128], [2 * REL, HG], [1, T]])
                sp.dma_start(biasr[:, g * HG:(g + 1) * HG, :], src).then_inc(d_bias, 16)

            def store(m):
                sp.wait_ge(g_o, 2 * m + 2)
                sp.dma_start(out[bass.ds(m, 1)].rearrange("o t h -> (o t) h"), ores[:]).then_inc(d_out, 16)

            with sp.Fori(0, B) as m:
                store(m)
            sp.wait_ge(d_out, 16 * B)
        L_ROUTE, L_POS, L_MOE, L_ATT = 16 * 6, 16 * 10, 16 * 6, 16 * 16

        @block.tensor
        def _(pe):
            mm, tr = nc.tensor.matmul, nc.tensor.transpose

            pe.wait_ge(l_route, L_ROUTE)
            tr(bk[0][:, 0:E], wt8[:], ident[0:E, 0:E])
            tr(bk[0][0:D, E:2 * E], wg8[:], ident[0:E, 0:E])
            tr(bk[0][0:D, 2 * E:2 * E + B], cond[:], ident[0:B, 0:B]).then_inc(one["p_wt"], 1)
            pe.wait_ge(l_x, 16 * NG)
            for g in range(NG):
                for i in range(GB):
                    last = tr(bk[1 + g][:, i * T:(i + 1) * T], xa[:, g * GB + i, :], ident[:])
                last.then_inc(one["p_xT"], 1)
            pe.wait_ge(one["v_wt"], 3)
            mm(bk[0][0:B, 64:64 + E], condT[:], wgT[:], start=True, stop=True).then_inc(one["p_gl"], 1)
            pe.wait_ge(one["v_gld"], 1)
            pe.wait_ge(one["v_ones"], 1)
            mm(bk[5][:, 0:B * E], ones[0:B, :], gl[:].rearrange("p b e -> p (b e)"), start=True, stop=False,
               skip_group_check=True)
            for b in range(B):
                pe.wait_ge(one["v_xT"], b // GB + 1)
                last = mm(bk[5][:, b * E:(b + 1) * E], xT[:, b * T:(b + 1) * T], wtT[:], start=False,
                          stop=(b == B - 1), skip_group_check=True)
            last.then_inc(one["p_lg"], 1)

            pe.wait_ge(l_pos, L_POS)
            pe.wait_ge(one["v_hs"], 1)
            tr(bk[0][:, 0:H], ph[:, 0, :], ident[:]).then_inc(one["p_h1T"], 1)
            pe.wait_ge(one["v_hT"], 1)
            mm(bk[0][:, 0:H], phT[:], w1[:], start=True, stop=True).then_inc(one["p_h1"], 1)
            pe.wait_ge(one["v_cp"], 1)
            for b in range(B):
                dst = bk[1 + b // 8][:].bitcast(BF16)
                last = tr(dst[0:3 * E, (b % 8) * T:(b % 8 + 1) * T], cp[:, b].rearrange("p s e -> p (s e)"), identb[:])
            last.then_inc(one["p_cT"], 1)
            pe.wait_ge(one["v_hs"], 2)
            tr(bk[0][:, 0:H], ph[:, 0, :], ident[:]).then_inc(one["p_h2T"], 1)
            pe.wait_ge(one["v_hT"], 2)
            mm(bk[0][:, 0:NH], phT[:], w2[:], start=True, stop=True).then_inc(one["p_rel"], 1)
            pe.wait_ge(one["v_relT"], 1)
            mm(bk[0][0:NH, 0:T], rel[:], flip[:], start=True, stop=True).then_inc(one["p_relT"], 1)

            pe.wait_ge(l_moe, L_MOE)
            pe.wait_ge(one["v_cT"], 2)
            GATE, UP, CB, Y = (bk[1], bk[2]), (bk[3], bk[4]), bk[5], bq[:, 0, :]

            def down(q):
                pe.wait_ge(m_hu, MC * (q + 1))
                pe.wait_ge(m_h, EC * (q + 1))
                if not isinstance(q, int) or q > 0:
                    pe.wait_ge(m_x1, q)
                for i in range(GB):
                    for c in range(MC):
                        last = mm(Y[:, i * H:(i + 1) * H], hh[:, c, i * T:(i + 1) * T], wd[:, c, :],
                                  start=(c == 0), stop=(c == MC - 1))
                last.then_inc(m_y, 1)

            def hidden(q, first):
                x_q = xT[:, bass.ds(q * GT, GT)]
                c_q = cT[:, bass.ds(q * GT, GT)]
                for c in range(MC):
                    if c >= 2 or not first:
                        pe.wait_ge(m_lk, MC * q + (c - 1 if c >= 2 else -c))
                        pe.wait_ge(m_hu, MC * q + (c - 1 if c >= 2 else -c))
                    mm(GATE[c % 2][:], wg[:, c, :], x_q, start=True, stop=True).then_inc(m_gate, 1)
                    mm(UP[c % 2][:], wu[:, c, :], x_q, start=True, stop=True).then_inc(m_up, 1)
                    if c == 1 and not first:
                        down(q - 1)
                    if c < EC:
                        if c > 0 or not first:
                            pe.wait_ge(m_h, EC * q + c)
                        settle(pe)
                        mm(CB[:], esel[:, c, :], c_q, start=True, stop=True).then_inc(m_cb, 1)

            hidden(0, True)
            pe.wait_ge(one["a_fro"], 1)
            mm(bk[0][:, 0:1], ones[:], fro[:, 1:2], start=True, stop=True).then_inc(one["p_fro"], 1)
            with pe.Fori(1, NG) as q:
                hidden(q, False)
            down(NG - 1)

            pe.wait_ge(one["v_wo"], 1)
            for c in range(PAIRS):
                last = mm(bk[0][0:NH, 0:H], nvblk[:, c, :], wo[:, c, :], start=(c == 0), stop=(c == PAIRS - 1))
            last.then_inc(one["p_nvw"], 1)
            pe.wait_ge(d_bias, 16 * HGS)
            pe.wait_ge(m_x1, NG)
            for g in range(HGS):
                if g >= 2:
                    pe.wait_ge(one["a_bias"], g - 1)
                mm(bq[:, g % 2, :], flip[:], biasr[:, g * HG:(g + 1) * HG, :].rearrange("p i t -> p (i t)"),
                   start=True, stop=True).then_inc(one["p_bias"], 1)
            for g in range(NG):
                pe.wait_ge(one["v_xn"], g + 1)
                for i in range(GB):
                    last = tr(bk[1 + g][:, i * T:(i + 1) * T], xc[:, g * GB + i, :], ident[:])
                last.then_inc(one["p_xnT"], 1)

            SB, PTB, OB, MB, XB = (bk[0], bk[1]), bk[2], bk[3], bk[4], bk[5]

            def scores(m, g):
                if not live(m):
                    return
                pe.wait_ge(c_qT, 2 * m + 1 + g // 2)
                pe.wait_ge(c_kT, m + 1)
                if later(m) or g >= 2:
                    pe.wait_ge(e_s, 4 * m + g - 1)
                half = slice(D * (g % 2), D * (g % 2) + D)
                for i in range(HG):
                    last = mm(SB[g % 2][:, i * T:(i + 1) * T], qT[half, HG * (g // 2) + i, :], kT[half, :],
                              start=True, stop=True)
                last.then_inc(t_s, 1)

            def probs_T(m, g):
                if not live(m):
                    return
                pe.wait_ge(c_exp, 4 * m + g + 1)
                if later(m) or g >= 1:
                    pe.wait_ge(e_pl, 4 * m + g)
                for i in range(HG):
                    last = tr(PTB[:, i * T:(i + 1) * T], pr[:, g % 2, i, :], ident[:])
                last.then_inc(t_pT, 1)

            def values(m, g):
                if not live(m):
                    return
                pe.wait_ge(e_pl, 4 * m + g + 1)
                pe.wait_ge(g_v, 2 * m + 2)
                if later(m) or g >= 1:
                    pe.wait_ge(e_on, 4 * m + g)
                for i in range(HG):
                    o = OB[:, i * (D + 1):(i + 1) * (D + 1)]
                    mm(o, pTh[:, g % 2, i, :], vaug[:, 0, :], start=True, stop=False)
                    mm(o, pTh[:, g % 2, i, :], vaug[:, 1, :], start=False, stop=False)
                    last = mm(o, pTl[:, g % 2, i, :], vaug[:, 0, :], start=False, stop=True)
                last.then_inc(t_av, 1)

            def queries(m, half):
                if not live(m):
                    return
                pe.wait_ge(g_xn, m + 1)
                if later(m):
                    pe.wait_ge(c_qT, 2 * m - 1 + half)
                mm(bq[:, half, :], xnb[:], wq[:, half * 512:(half + 1) * 512], start=True, stop=True).then_inc(t_q, 1)

            def keys_values(m):
                if not live(m):
                    return
                pe.wait_ge(g_xn, m + 1)
                if later(m):
                    pe.wait_ge(c_kT, m)
                mm(MB[:, 0:NH + 2 * D], xnb[:], wkvn[:], start=True, stop=True).then_inc(t_kv, 1)

            def queries_T(m, half):
                if not live(m):
                    return
                pe.wait_ge(e_qh, 2 * m + half + 1)
                for c in range(4):
                    cc = 4 * half + c
                    last = tr(bq[:, half, c * T:(c + 1) * T], qh[:, 2 * cc:2 * cc + 2, :].rearrange("p h d -> p (h d)"),
                              ident[:])
                last.then_inc(t_qT, 1)

            def keys_T(m):
                if not live(m):
                    return
                pe.wait_ge(c_kk, m + 1)
                if not isinstance(m, int) or m > 1:
                    pe.wait_ge(c_anT, m - 1)
                tr(MB[:, 0:T], kk[:].rearrange("p r d -> p (r d)"), ident[:]).then_inc(t_kT, 1)

            def outputs_T(m, half):
                if not live(m):
                    return
                pe.wait_ge(e_on, 4 * m + 2 * half + 2)
                if half == 1:
                    pe.wait_ge(c_oT, 2 * m + 1)
                elif later(m):
                    pe.wait_ge(c_out, m)
                for c in range(4 * half, 4 * half + 4):
                    last = tr(XB[:, (c % 4) * T:(c % 4 + 1) * T], on[:, 2 * c:2 * c + 2, :].rearrange("p h d -> p (h d)"),
                              ident[:])
                last.then_inc(t_oT, 1)

            def null_weights_T(m):
                if not live(m):
                    return
                pe.wait_ge(e_on, 4 * m + 4)
                if live(m + 2):
                    pe.wait_ge(c_kv, m + 3)
                else:
                    pe.wait_ge(c_kT, B)
                tr(MB[0:NH, 256:256 + T], an[:], ident[:]).then_inc(t_anT, 1)

            def project(m):
                if not live(m):
                    return
                pe.wait_ge(c_oT, 2 * m + 2)
                pe.wait_ge(c_anT, m + 1)
                for c in range(PAIRS):
                    mm(XB[:, 0:H], oT[:, c, :], wo[:, c, :], start=(c == 0), stop=False)
                mm(XB[:, 0:H], anT[:], nvw[:], start=False, stop=True).then_inc(t_out, 1)

            def step(n):
                p, x = n - 1, n + 1
                outputs_T(p, 0)
                queries(x, 0)
                probs_T(n, 0)
                values(p, 3)
                queries(x, 1)
                scores(n, 3)
                keys_values(x)
                outputs_T(p, 1)
                null_weights_T(p)
                probs_T(n, 1)
                values(n, 0)
                project(p)
                queries_T(x, 0)
                keys_T(x)
                probs_T(n, 2)
                values(n, 1)
                scores(x, 0)
                queries_T(x, 1)
                scores(x, 1)
                values(n, 2)
                probs_T(n, 3)
                scores(x, 2)

            pe.wait_ge(one["v_xnT"], NG)
            pe.wait_ge(one["a_bias"], HGS)
            pe.wait_ge(one["v_nvw"], 1)
            pe.wait_ge(one["v_wkvn"], 1)
            step(-1)
            step(0)
            step(1)
            with pe.Fori(2, B - 1) as n:
                step(n)
            step(B - 1)
            step(B)

        @block.scalar
        def _(act):
            fn = nc.scalar.activation
            nc.scalar.preload_act_table_set("natural_log_exp_and_others")

            def rsqrt_seed(dst, tmp, src, s, base):
                fn(tmp, src, ACT.Ln).then_inc(s, 1)
                act.wait_ge(s, base + 1)
                fn(dst, tmp, ACT.Exp, scale=-0.5).then_inc(s, 1)

            for k in range(2):
                act.wait_ge(one["v_lnp"], k + 1)
                rsqrt_seed(pstat[:, 11:12], pstat[:, 10:11], pstat[:, 8:9], one["a_r1"], 2 * k)
                act.wait_ge(one["v_hg"], k + 1)
                fn(ph[:, 2, :], ph[:, 1, :], ACT.Exp, scale=-1.0).then_inc(one["a_e1"], 1)
            act.wait_ge(one["v_d"], 1)
            fn(rt[:, 1], rt[:, 0], ACT.Exp).then_inc(one["a_exp"], 1)
            GATE = (bk[1], bk[2])

            def gates(q, first):
                for c in range(MC):
                    act.wait_ge(m_gate, MC * q + c + 1)
                    if not first:
                        act.wait_ge(m_hu, MC * (q - 1) + c + 1)
                    fn(gs[:, c, :], GATE[c % 2][:], ACT.Copy, scale=SLOPE).then_inc(m_gs, 1)

            gates(0, True)
            act.wait_ge(l_att, L_ATT)
            fn(k2[:], wkvn[:, NH + D:], ACT.Square, scale=gnorm[:, 0:1], accum_out=fro[:, 1:2]).then_inc(one["a_fro"], 1)
            act.wait_ge(one["v_fro"], 1)
            rsqrt_seed(fro[:, 4:5], fro[:, 3:4], fro[:, 2:3], one["a_fro"], 1)
            act.wait_ge(one["v_nk"], 1)
            rsqrt_seed(nulls[:, 2:3], nulls[:, 1:2], nulls[:, 0:1], one["a_nk"], 0)

            with act.Fori(1, NG) as q:
                gates(q, False)
            for g in range(HGS):
                act.wait_ge(one["p_bias"], g + 1)
                fn(bias[:, g * HG:(g + 1) * HG, :].rearrange("p i t -> p (i t)"), bq[:, g % 2, :],
                   ACT.Copy).then_inc(one["a_bias"], 1)
            act.wait_ge(one["v_var"], 1)
            rsqrt_seed(rstd[:, 2, :], rstd[:, 1, :], rstd[:, 0, :], one["a_var"], 0)

            PTB, OB, MB, XB = bk[2], bk[3], bk[4], bk[5]

            def exps(m, g):
                if not live(m):
                    return
                act.wait_ge(e_nm, 4 * m + g + 1)
                if later(m) or g >= 2:
                    act.wait_ge(t_pT, 4 * m + g - 1)
                if later(m):
                    act.wait_ge(e_on, 4 * m - 3 + g)
                hs = slice(HG * g, HG * g + HG)
                fn(pn[:, hs], pnd[:, hs], ACT.Exp)
                for i in range(HG):
                    last = fn(pr[:, g % 2, i, :], ssb[:, g % 2, i, :], ACT.Exp, bias=nm[:, HG * g + i:HG * g + i + 1])
                last.then_inc(c_exp, 1)

            def probs_T(m, g):
                if not live(m):
                    return
                act.wait_ge(t_pT, 4 * m + g + 1)
                if later(m) or g >= 2:
                    act.wait_ge(t_av, 4 * m + g - 1)
                fn(pTh[:, g % 2].rearrange("p i t -> p (i t)"), PTB[:], ACT.Copy).then_inc(c_pT, 1)

            def squared_queries(m, half):
                if not live(m):
                    return
                act.wait_ge(t_q, 2 * m + half + 1)
                if later(m):
                    act.wait_ge(e_sq, 3 * m - 2 + half)
                fn(q2[:, 8 * half:8 * half + 8].rearrange("p h d -> p (h d)"), bq[:, half, :],
                   ACT.Square).then_inc(c_q2, 1)

            def keys_values(m):
                if not live(m):
                    return
                act.wait_ge(t_kv, m + 1)
                if later(m):
                    act.wait_ge(g_v, 2 * m)
                    act.wait_ge(e_nl, 2 * m - 1)
                fn(kvs[:], MB[:, 0:NH + 2 * D], ACT.Copy).then_inc(c_kv, 1)

            def outputs_T(m, half):
                if not live(m):
                    return
                act.wait_ge(t_oT, 2 * m + half + 1)
                if later(m):
                    act.wait_ge(t_out, m)
                fn(oT[:, 4 * half:4 * half + 4, :].rearrange("p c t -> p (c t)"), XB[:], ACT.Copy).then_inc(c_oT, 1)

            def null_weights_T(m):
                if not live(m):
                    return
                act.wait_ge(t_anT, m + 1)
                if later(m):
                    act.wait_ge(t_out, m)
                fn(anT[:], MB[0:NH, 256:256 + T], ACT.Copy).then_inc(c_anT, 1)

            def norm_seeds(m):
                if not live(m):
                    return
                act.wait_ge(e_ss, m + 1)
                if later(m):
                    act.wait_ge(e_nq, 3 * m)
                rsqrt_seed(nw[:, 0, :], lns[:], ss[:], c_lnq, 2 * m)

            def unit_keys(m):
                if not live(m):
                    return
                act.wait_ge(e_nq, 3 * m + 3)
                if later(m):
                    act.wait_ge(t_kT, m)
                fn(kk[:], kvs[:, NH:NH + D].rearrange("p (o d) -> p o d", o=1).to_broadcast([128, 2, D]),
                   ACT.Copy, scale=nw[:, 2, NH:NH + 1]).then_inc(c_kk, 1)

            def keys_T(m):
                if not live(m):
                    return
                act.wait_ge(t_kT, m + 1)
                if later(m):
                    act.wait_ge(t_s, 4 * m)
                fn(kT[:], MB[:, 0:T], ACT.Copy, scale=ksc8[:, 0:1]).then_inc(c_kT, 1)

            def queries_T(m, half):
                if not live(m):
                    return
                act.wait_ge(t_qT, 2 * m + half + 1)
                if later(m):
                    act.wait_ge(t_s, 4 * m - 2 + 2 * half)
                fn(qT[:, 4 * half:4 * half + 4, :].rearrange("p c t -> p (c t)"), bq[:, half, :],
                   ACT.Copy).then_inc(c_qT, 1)

            def output_seed(m):
                if not live(m):
                    return
                act.wait_ge(e_var, m + 1)
                rsqrt_seed(onw[:, 2:3], onw[:, 1:2], onw[:, 0:1], c_lno, 2 * m)

            def output(m):
                if not live(m):
                    return
                act.wait_ge(e_mr, m + 1)
                if later(m):
                    act.wait_ge(g_o, 2 * m - 1)
                fn(olin[:], XB[:, 0:H], ACT.Identity, scale=onw[:, 4:5], bias=nmr[:, 0:1]).then_inc(c_out, 1)

            def step(n):
                p, x = n - 1, n + 1
                probs_T(p, 3)
                exps(n, 0)
                outputs_T(p, 0)
                squared_queries(x, 0)
                probs_T(n, 0)
                exps(n, 1)
                squared_queries(x, 1)
                keys_values(x)
                outputs_T(p, 1)
                null_weights_T(p)
                norm_seeds(x)
                probs_T(n, 1)
                exps(n, 2)
                unit_keys(x)
                queries_T(x, 0)
                keys_T(x)
                probs_T(n, 2)
                output_seed(p)
                exps(n, 3)
                output(p)
                queries_T(x, 1)

            step(-1)
            step(0)
            step(1)
            with act.Fori(2, B - 1) as n:
                step(n)
            step(B - 1)
            step(B)

        @block.vector
        def _(dve):
            v = nc.vector
            done = [0]

            def link(ins):
                done[0] += 1
                ins.then_inc(v_set, 1)
                dve.wait_ge(v_set, done[0])

            def newton(dst, y, x, t):
                link(v.tensor_tensor(t, y, y, ALU.mult))
                link(v.scalar_tensor_tensor(out=t, in0=t, scalar=-0.5, in1=x, op0=ALU.mult, op1=ALU.mult))
                link(v.scalar_tensor_tensor(out=dst, in0=t, scalar=1.5, in1=y, op0=ALU.add, op1=ALU.mult))

            v.memset(ones[:], 1.0).then_inc(one["v_ones"], 1)
            v.memset(vaug[:, 0, D:D + 1], 1.0)
            v.memset(vaug[:, 1, D:D + 1], 0.0)
            v.memset(relT[:, T:], NEG).then_inc(v_set, 1)
            done[0] += 1
            dve.wait_ge(one["p_wt"], 1)
            v.tensor_copy(wtT[:], bk[0][:, 0:E]).then_inc(one["v_wt"], 1)
            v.tensor_copy(wgT[:], bk[0][0:D, E:2 * E]).then_inc(one["v_wt"], 1)
            v.tensor_copy(condT[:], bk[0][0:D, 2 * E:2 * E + B]).then_inc(one["v_wt"], 1)
            for g in range(NG):
                dve.wait_ge(one["p_xT"], g + 1)
                v.tensor_copy(xT[:, g * GT:(g + 1) * GT], bk[1 + g][:]).then_inc(one["v_xT"], 1)
                if g == 0:
                    dve.wait_ge(one["p_gl"], 1)
                    link(v.tensor_copy(rs[0:B, 0, 0:E], bk[0][0:B, 64:64 + E]))
                    v.tensor_tensor(gl[:], rs[0:B, 0:1, 0:E].to_broadcast([B, B, E]),
                                    ident[0:B, 0:B].rearrange("p (b o) -> p b o", o=1).to_broadcast([B, B, E]),
                                    ALU.mult).then_inc(one["v_gld"], 1)

            def layer(k):
                link(v.bn_stats(pstat[:, 0:6], ph[:, 0, :]))
                link(v.bn_aggr(pstat[:, 6:8], pstat[:, 0:6]))
                v.tensor_scalar(pstat[:, 8:9], pstat[:, 7:8], LN_EPS, None, ALU.add).then_inc(one["v_lnp"], 1)
                dve.wait_ge(one["a_r1"], 2 * k)
                newton(pstat[:, 12:13], pstat[:, 11:12], pstat[:, 8:9], pstat[:, 13:14])
                link(v.tensor_scalar(ph[:, 3, :], ph[:, 0, :], pstat[:, 6:7], pstat[:, 12:13], ALU.subtract, ALU.mult))
                return v.tensor_tensor(ph[:, 1, :], ph[:, 3, :], (g0, g1)[k - 1][:], ALU.mult)

            def silu(k):
                dve.wait_ge(one["a_e1"], k)
                link(v.tensor_scalar(ph[:, 3, :], ph[:, 2, :], 1.0, None, ALU.add))
                link(v.reciprocal(ph[:, 2, :], ph[:, 3, :]))
                return v.tensor_tensor(ph[:, 0, :], ph[:, 1, :], ph[:, 2, :], ALU.mult)

            dve.wait_ge(l_pos, L_POS)
            link(v.scalar_tensor_tensor(out=ph[:, 0, :], in0=w0[:], scalar=pos[:, 0:1], in1=b0[:],
                                        op0=ALU.mult, op1=ALU.add))
            layer(1).then_inc(one["v_hg"], 1)
            silu(1).then_inc(one["v_hs"], 1)
            dve.wait_ge(one["p_h1T"], 1)
            v.tensor_copy(phT[:], bk[0][:, 0:H]).then_inc(one["v_hT"], 1)
            dve.wait_ge(one["p_h1"], 1)
            link(v.tensor_tensor(ph[:, 0, :], bk[0][:, 0:H], b1[:], ALU.add))
            layer(2).then_inc(one["v_hg"], 1)

            def by_batch(ap):
                return ap.rearrange("p (b o) -> p b o", o=1).to_broadcast([128, B, E])

            dve.wait_ge(one["p_lg"], 1)
            link(v.tensor_scalar(lg[:].rearrange("p b e -> p (b e)"), bk[5][:, 0:B * E], 0.5, None, ALU.mult))
            link(v.tensor_reduce(rs[:, 1, :], lg[:], AX.X, ALU.max))
            v.tensor_tensor(rt[:, 0], lg[:], by_batch(rs[:, 1, :]), ALU.subtract).then_inc(one["v_d"], 1)

            def first_of(dst, src, largest, r):
                link(v.tensor_tensor(dst, src, by_batch(largest), ALU.is_equal))
                link(v.tensor_tensor(dst, dst, rank[:], ALU.mult))
                link(v.tensor_reduce(rs[:, r, :], dst, AX.X, ALU.max))
                link(v.tensor_tensor(dst, dst, by_batch(rs[:, r, :]), ALU.is_equal))

            first_of(rt[:, 2], lg[:], rs[:, 1, :], 2)
            link(v.scalar_tensor_tensor(out=rt[:, 4], in0=rt[:, 2], scalar=NEG, in1=lg[:], op0=ALU.mult, op1=ALU.add))
            link(v.tensor_reduce(rs[:, 3, :], rt[:, 4], AX.X, ALU.max))
            first_of(rt[:, 5], rt[:, 4], rs[:, 3, :], 4)
            link(v.tensor_tensor(rt[:, 2], rt[:, 2], rt[:, 5], ALU.add))
            dve.wait_ge(one["a_exp"], 1)
            link(v.tensor_tensor(rt[:, 6], rt[:, 2], rt[:, 1], ALU.mult))
            link(v.tensor_reduce(rs[:, 5, :], rt[:, 6], AX.X, ALU.add))
            link(v.tensor_reduce(rs[:, 6, :], rt[:, 1], AX.X, ALU.add))
            link(v.scalar_tensor_tensor(out=rs[:, 7, :], in0=rs[:, 6, :], scalar=1e-20, in1=rs[:, 5, :],
                                        op0=ALU.mult, op1=ALU.add))
            link(v.reciprocal(rs[:, 0, :], rs[:, 7, :]))
            link(v.tensor_tensor(rt[:, 7], rt[:, 6], by_batch(rs[:, 0, :]), ALU.mult))
            link(v.tensor_copy(identb[:], ident[:]))
            link(v.tensor_copy(esel[:], eself[:]))
            link(v.tensor_copy(cp[:, :, 0, :], rt[:, 7]))
            link(v.tensor_tensor(rt[:, 0], rt[:, 7], cp[:, :, 0, :], ALU.subtract))
            link(v.tensor_copy(cp[:, :, 1, :], rt[:, 0]))
            link(v.tensor_tensor(rt[:, 3], rt[:, 0], cp[:, :, 1, :], ALU.subtract))
            v.tensor_copy(cp[:, :, 2, :], rt[:, 3]).then_inc(one["v_cp"], 1)

            silu(2).then_inc(one["v_hs"], 1)
            for half in range(2):
                dve.wait_ge(one["p_cT"], 1)
                v.tensor_copy(cT[:, half * 1024:(half + 1) * 1024],
                              bk[1 + half][:].bitcast(BF16)[0:3 * E, :]).then_inc(one["v_cT"], 1)
            dve.wait_ge(one["p_h2T"], 1)
            v.tensor_copy(phT[:], bk[0][:, 0:H]).then_inc(one["v_hT"], 1)
            dve.wait_ge(one["p_rel"], 1)
            v.tensor_tensor(rel[:], bk[0][:, 0:NH], b2[:], ALU.add).then_inc(one["v_relT"], 1)
            dve.wait_ge(one["p_relT"], 1)
            v.tensor_copy(relT[:, 0:T], bk[0][0:NH, 0:T]).then_inc(one["v_relT"], 1)

            GATE, UP, CB, Y = (bk[1], bk[2]), (bk[3], bk[4]), bk[5], bq[:, 0, :]

            def chunk(q, c, first):
                dve.wait_ge(m_gs, MC * q + c + 1)
                v.tensor_tensor(gs[:, c, :], gs[:, c, :], GATE[c % 2][:], ALU.max).then_inc(m_lk, 1)
                dve.wait_ge(m_up, MC * q + c + 1)
                dve.wait_ge(m_lk, MC * q + c + 1)
                if c < EC:
                    v.tensor_tensor(hub[:, c % 2, :], gs[:, c, :], UP[c % 2][:], ALU.mult).then_inc(m_hu, 1)
                    dve.wait_ge(m_hu, MC * q + c + 1)
                    dve.wait_ge(m_cb, EC * q + c + 1)
                if not first:
                    dve.wait_ge(m_y, q)
                if c < EC:
                    v.tensor_tensor(hh[:, c, :], hub[:, c % 2, :], CB[:], ALU.mult).then_inc(m_h, 1)
                else:
                    v.tensor_tensor(hh[:, c, :], gs[:, c, :], UP[c % 2][:], ALU.mult).then_inc(m_hu, 1)

            def residual(q):
                x_q, xc_q = xa[:, bass.ds(q * GB, GB), :], xc[:, bass.ds(q * GB, GB), :]
                dve.wait_ge(m_y, q + 1)
                v.tensor_tensor(x_q, x_q, Y.rearrange("p (b h) -> p b h", b=GB), ALU.add).then_inc(m_x1, 1)
                dve.wait_ge(m_x1, q + 1)
                settle(dve)
                v.tensor_reduce(msum[:], x_q, AX.X, ALU.add).then_inc(m_st, 1)
                dve.wait_ge(m_st, 4 * q + 1)
                v.tensor_scalar(nmean[:], msum[:], 1.0 / H, None, ALU.mult).then_inc(m_st, 1)
                dve.wait_ge(m_st, 4 * q + 2)
                v.tensor_tensor(xc_q, x_q, nmean[:].rearrange("p (b o) -> p b o", o=1).to_broadcast([128, GB, H]),
                                ALU.subtract).then_inc(m_st, 1)

            def variance(q):
                dve.wait_ge(m_sq, q + 1)
                settle(dve)
                v.tensor_reduce(var[:, bass.ds(q * GB, GB)], sq[:], AX.X, ALU.add).then_inc(m_st, 1)

            def group(q, first):
                for c in range(MC):
                    chunk(q, c, first)
                    if c == 1 and not first:
                        residual(q - 1)
                    if c == 3 and not first:
                        variance(q - 1)

            group(0, True)

            dve.wait_ge(l_att, L_ATT)
            dve.wait_ge(one["p_fro"], 1)
            v.tensor_scalar(fro[:, 2:3], bk[0][:, 0:1], 1e-30, H * 2.0 ** -28, ALU.max, ALU.mult).then_inc(one["v_fro"], 1)
            dve.wait_ge(one["a_fro"], 3)
            link(v.reciprocal(fro[:, 5:6], fro[:, 4:5]))
            link(v.tensor_scalar(wkvn[:, NH + D:], wkvn[:, NH + D:], fro[:, 4:5], None, ALU.mult))
            wo_all = wo[:].rearrange("p c n -> p (c n)")
            link(v.tensor_scalar(wo_all, wo_all, fro[:, 5:6], None, ALU.mult))
            v.tensor_scalar(nvblk[:].rearrange("p c h -> p (c h)"), nsel[:].rearrange("p c h -> p (c h)"),
                            nvcol[:, 0:1], fro[:, 4:5], ALU.mult, ALU.mult).then_inc(one["v_wo"], 1)
            SCALE = 8.0 * NORM_SCALE * NORM_SCALE
            link(v.tensor_scalar(ksc8[:], ksc[:], qsc[:, 0:1], SCALE, ALU.mult, ALU.mult))
            link(v.tensor_tensor_reduce(k2[:], nkrow[:], nkrow[:], 1.0, 0.0, ALU.mult, ALU.add, nulls[:, 3:4]))
            v.tensor_scalar(nulls[:, 0:1], nulls[:, 3:4], NORM_MIN ** 2, NORM_SCALE ** 2, ALU.max,
                            ALU.mult).then_inc(one["v_nk"], 1)
            link(v.tensor_tensor(qrow[:], qrow[:], krow[:], ALU.mult))
            dve.wait_ge(one["a_nk"], 2)
            newton(nulls[:, 4:5], nulls[:, 2:3], nulls[:, 0:1], nulls[:, 5:6])
            link(v.scalar_tensor_tensor(out=krow[:], in0=nkrow[:], scalar=nulls[:, 4:5], in1=qrow[:],
                                        op0=ALU.mult, op1=ALU.mult))
            link(v.tensor_scalar(nkrow[:], krow[:], SCALE, None, ALU.mult))
            link(v.tensor_tensor(q2[:], wq[:].rearrange("p (h d) -> p h d", d=D),
                                 nkrow[:].rearrange("p (o d) -> p o d", o=1).to_broadcast([128, NH, D]), ALU.mult))
            v.tensor_reduce(wkvn[:, 0:NH], q2[:], AX.X, ALU.add).then_inc(one["v_wkvn"], 1)

            with dve.Fori(1, NG) as q:
                group(q, False)
            residual(NG - 1)
            variance(NG - 1)
            dve.wait_ge(m_st, 4 * NG)
            v.tensor_scalar(rstd[:, 0, :], var[:], 1.0 / H, LN_EPS, ALU.mult, ALU.add).then_inc(one["v_var"], 1)
            dve.wait_ge(one["a_var"], 2)
            newton(rstd[:, 3, :], rstd[:, 2, :], rstd[:, 0, :], rstd[:, 1, :])
            for g in range(NG):
                gg = slice(g * GB, (g + 1) * GB)
                v.tensor_tensor(xc[:, gg, :], xc[:, gg, :],
                                rstd[:, 3, gg].rearrange("p (b o) -> p b o", o=1).to_broadcast([128, GB, H]),
                                ALU.mult).then_inc(one["v_xn"], 1)
            dve.wait_ge(one["p_nvw"], 1)
            v.tensor_copy(nvw[:], bk[0][0:NH, 0:H]).then_inc(one["v_nvw"], 1)
            for g in range(NG):
                dve.wait_ge(one["p_xnT"], g + 1)
                v.tensor_scalar(xT[:, g * GT:(g + 1) * GT], bk[1 + g][:], gnorm[:, 0:1], None,
                                ALU.mult).then_inc(one["v_xnT"], 1)

            SB, PTB, OB, XB = (bk[0], bk[1]), bk[2], bk[3], bk[5]

            def biased_scores(m, g):
                if not live(m):
                    return
                dve.wait_ge(t_s, 4 * m + g + 1)
                dve.wait_ge(g_bias, 4 * m + g + 1)
                if later(m) or g >= 2:
                    dve.wait_ge(c_exp, 4 * m + g - 1)
                settle(dve)
                for i in range(HG):
                    h = HG * g + i
                    last = v.tensor_tensor_reduce(ssb[:, g % 2, i, :], SB[g % 2][:, i * T:(i + 1) * T],
                                                  biasm[:, h, :], 1.0, -3e38, ALU.add, ALU.max, mx[:, h:h + 1])
                last.then_inc(e_s, 1)

            def maxima(m, g):
                if not live(m):
                    return
                hs = slice(HG * g, HG * g + HG)
                dve.wait_ge(e_s, 4 * m + g + 1)
                dve.wait_ge(e_nl, 2 * m + 2)
                v.scalar_tensor_tensor(out=nm[:, hs], in0=mx[:, hs], scalar=-1.0, in1=nnl[:, 0, hs],
                                       op0=ALU.mult, op1=ALU.min).then_inc(e_mx, 1)

            def null_shifts(m, g):
                if not live(m):
                    return
                hs = slice(HG * g, HG * g + HG)
                dve.wait_ge(e_mx, 4 * m + g + 1)
                v.tensor_tensor(pnd[:, hs], nm[:, hs], nnl[:, 0, hs], ALU.subtract).then_inc(e_nm, 1)

            def low_part(m, g):
                if not live(m):
                    return
                dve.wait_ge(c_pT, 4 * m + g + 1)
                if later(m) or g >= 2:
                    dve.wait_ge(t_av, 4 * m + g - 1)
                v.tensor_tensor(pTl[:, g % 2].rearrange("p i t -> p (i t)"), PTB[:],
                                pTh[:, g % 2].rearrange("p i t -> p (i t)"), ALU.subtract).then_inc(e_pl, 1)

            o_g = OB[:, 0:HG * (D + 1)].rearrange("p (i d) -> p i d", d=D + 1)

            def sums(m, g):
                if not live(m):
                    return
                dve.wait_ge(t_av, 4 * m + g + 1)
                v.tensor_tensor(den[:, 0, :], o_g[:, :, D], pn[:, HG * g:HG * g + HG], ALU.add).then_inc(e_dn, 1)

            def inverse_sums(m, g):
                if not live(m):
                    return
                dve.wait_ge(e_dn, 8 * m + 2 * g + 1)
                v.reciprocal(den[:, 1, :], den[:, 0, :]).then_inc(e_dn, 1)

            def attention(m, g):
                if not live(m):
                    return
                dve.wait_ge(e_dn, 8 * m + 2 * g + 2)
                if later(m):
                    dve.wait_ge(t_oT, 2 * m - 1 + g // 2)
                    dve.wait_ge(t_anT, m)
                v.tensor_tensor(head_view(an[:], g), pn[:, HG * g:HG * g + HG], den[:, 1, :], ALU.mult)
                on_g = on[:].rearrange("p (G i r) d -> p G r i d", G=2, r=2)[:, g // 2, g % 2]
                v.tensor_tensor(on_g, o_g[:, :, 0:D],
                                den[:, 1, :].rearrange("p (i o) -> p i o", o=1).to_broadcast([128, HG, D]),
                                ALU.mult).then_inc(e_on, 1)

            def query_norms(m, half):
                if not live(m):
                    return
                dve.wait_ge(c_q2, 2 * m + half + 1)
                if later(m):
                    dve.wait_ge(c_lnq, 2 * m - 1)
                v.tensor_reduce(ss[:, 8 * half:8 * half + 8], q2[:, 8 * half:8 * half + 8], AX.X,
                                ALU.add).then_inc(e_sq, 1)

            def key_norm(m):
                if not live(m):
                    return
                dve.wait_ge(c_kv, m + 1)
                v.tensor_tensor_reduce(k2[:], kvs[:, NH:NH + D], kvs[:, NH:NH + D], 1.0, 0.0, ALU.mult, ALU.add,
                                       ss[:, NH:NH + 1]).then_inc(e_sq, 1)

            def scaled_norms(m):
                if not live(m):
                    return
                dve.wait_ge(e_sq, 3 * m + 3)
                v.tensor_scalar(ss[:], ss[:], NORM_MIN ** 2, NORM_SCALE ** 2, ALU.max, ALU.mult).then_inc(e_ss, 1)

            def inverse_norms(m, part):
                if not live(m):
                    return
                if part == 0:
                    dve.wait_ge(c_lnq, 2 * m + 2)
                    v.tensor_tensor(nw[:, 1, :], nw[:, 0, :], nw[:, 0, :], ALU.mult).then_inc(e_nq, 1)
                if part == 1:
                    dve.wait_ge(e_nq, 3 * m + 1)
                    v.scalar_tensor_tensor(out=nw[:, 1, :], in0=nw[:, 1, :], scalar=-0.5, in1=ss[:],
                                           op0=ALU.mult, op1=ALU.mult).then_inc(e_nq, 1)
                if part == 2:
                    dve.wait_ge(e_nq, 3 * m + 2)
                    if later(m):
                        dve.wait_ge(c_kk, m)
                    v.scalar_tensor_tensor(out=nw[:, 2, :], in0=nw[:, 1, :], scalar=1.5, in1=nw[:, 0, :],
                                           op0=ALU.add, op1=ALU.mult).then_inc(e_nq, 1)

            def unit_queries(m, half):
                if not live(m):
                    return
                dve.wait_ge(e_nq, 3 * m + 3)
                if later(m):
                    dve.wait_ge(t_qT, 2 * m - 1 + half)
                hs = slice(8 * half, 8 * half + 8)
                v.tensor_tensor(qh[:, hs], bq[:, half, :].rearrange("p (h d) -> p h d", d=D),
                                nw[:, 2, hs].rearrange("p (h o) -> p h o", o=1).to_broadcast([128, 8, D]),
                                ALU.mult).then_inc(e_qh, 1)

            def null_logits(m):
                if not live(m):
                    return
                dve.wait_ge(e_nq, 3 * m + 3)
                dve.wait_ge(c_kv, m + 1)
                v.scalar_tensor_tensor(out=nnl[:, 1, :], in0=kvs[:, 0:NH], scalar=-1.0, in1=nw[:, 2, 0:NH],
                                       op0=ALU.mult, op1=ALU.mult).then_inc(e_nl, 1)

            def biased_null_logits(m):
                if not live(m):
                    return
                dve.wait_ge(e_nl, 2 * m + 1)
                order = "p (G i r) -> p G r i"
                for G in range(2):
                    last = v.tensor_tensor(nnl[:, 0, :].rearrange("p (G r i) -> p G r i", G=2, r=2)[:, G],
                                           nnl[:, 1, :].rearrange(order, G=2, r=2)[:, G],
                                           nullb[:].rearrange(order, G=2, r=2)[:, G], ALU.subtract)
                last.then_inc(e_nl, 1)

            def output_sums(m):
                if not live(m):
                    return
                dve.wait_ge(t_out, m + 1)
                v.bn_stats(ost[:], XB[:, 0:H]).then_inc(e_st, 1)

            def output_variance(m):
                if not live(m):
                    return
                dve.wait_ge(e_st, 2 * m + 1)
                if later(m):
                    dve.wait_ge(e_mr, m)
                settle(dve)
                v.bn_aggr(omv[:], ost[:]).then_inc(e_st, 1)

            def step(n):
                p, x = n - 1, n + 1
                sums(p, 3)
                query_norms(x, 0)
                inverse_sums(p, 3)
                maxima(n, 2)
                attention(p, 3)
                low_part(n, 0)
                query_norms(x, 1)
                key_norm(x)
                null_shifts(n, 2)
                scaled_norms(x)
                biased_scores(n, 3)
                inverse_norms(x, 0)
                sums(n, 0)
                inverse_norms(x, 1)
                inverse_sums(n, 0)
                inverse_norms(x, 2)
                maxima(n, 3)
                unit_queries(x, 0)
                low_part(n, 1)
                attention(n, 0)
                output_sums(p)
                null_logits(x)
                null_shifts(n, 3)
                output_variance(p)
                unit_queries(x, 1)
                sums(n, 1)
                low_part(n, 2)
                inverse_sums(n, 1)
                biased_null_logits(x)
                attention(n, 1)
                biased_scores(x, 0)
                sums(n, 2)
                maxima(x, 0)
                inverse_sums(n, 2)
                null_shifts(x, 0)
                biased_scores(x, 1)
                low_part(n, 3)
                maxima(x, 1)
                attention(n, 2)
                null_shifts(x, 1)
                biased_scores(x, 2)

            step(-1)
            step(0)
            step(1)
            with dve.Fori(2, B - 1) as n:
                step(n)
            step(B - 1)
            step(B)

        @block.gpsimd
        def _(pool):
            g_ = nc.gpsimd

            pool.wait_ge(l_mask, 16)
            g_.tensor_scalar(maskb[:], masku[:], -1.0, -NEG, ALU.add, ALU.mult).then_inc(one["g_mask"], 1)

            def squares(q):
                pool.wait_ge(m_st, 4 * q + 3)
                xc_q = xc[:, bass.ds(q * GB, GB), :]
                settle(pool)
                g_.tensor_tensor(sq[:], xc_q, xc_q, ALU.mult).then_inc(m_sq, 1)

            with pool.Fori(0, NG) as q:
                squares(q)

            def tokens(m):
                if not live(m):
                    return
                if later(m):
                    pool.wait_ge(t_kv, m)
                settle(pool)
                g_.tensor_copy(xnb[:], xT[:, bass.ds(m * T, T)]).then_inc(g_xn, 1)

            def masked_bias(m, g):
                if not live(m):
                    return
                if later(m):
                    pool.wait_ge(e_s, 4 * m - 3 + g)
                hs = slice(HG * g, HG * g + HG)
                settle(pool)
                g_.tensor_tensor(biasm[:, hs, :], bias[:, hs, :], maskb[:, bass.ds(m, 1), :].to_broadcast([128, HG, T]),
                                 ALU.add).then_inc(g_bias, 1)

            def batch_values(m):
                if not live(m):
                    return
                pool.wait_ge(c_kv, m + 1)
                if later(m):
                    pool.wait_ge(t_av, 4 * m)
                settle(pool)
                g_.tensor_copy(vaug[:, 0, 0:D], kvs[:, NH + D:NH + 2 * D]).then_inc(g_v, 1)
                pool.wait_ge(g_v, 2 * m + 1)
                g_.tensor_tensor(vaug[:, 1, 0:D], kvs[:, NH + D:NH + 2 * D], vaug[:, 0, 0:D],
                                 ALU.subtract).then_inc(g_v, 1)

            def output(m):
                if not live(m):
                    return
                pool.wait_ge(e_st, 2 * m + 2)
                settle(pool)
                g_.tensor_scalar(onw[:, 0:1], omv[:, 1:2], LN_EPS, None, ALU.add).then_inc(e_var, 1)
                pool.wait_ge(c_lno, 2 * m + 2)
                g_.tensor_tensor(onw[:, 3:4], onw[:, 2:3], onw[:, 2:3], ALU.mult).then_inc(e_no, 1)
                pool.wait_ge(e_no, 4 * m + 1)
                g_.tensor_tensor(onw[:, 5:6], onw[:, 3:4], onw[:, 0:1], ALU.mult).then_inc(e_no, 1)
                pool.wait_ge(e_no, 4 * m + 2)
                settle(pool)
                g_.tensor_scalar(onw[:, 3:4], onw[:, 5:6], -0.5, 1.5, ALU.mult, ALU.add).then_inc(e_no, 1)
                pool.wait_ge(e_no, 4 * m + 3)
                if later(m):
                    pool.wait_ge(c_out, m)
                g_.tensor_tensor(onw[:, 4:5], onw[:, 3:4], onw[:, 2:3], ALU.mult).then_inc(e_no, 1)
                pool.wait_ge(e_no, 4 * m + 4)
                settle(pool)
                g_.tensor_scalar(nmr[:], omv[:, 0:1], onw[:, 4:5], -1.0, ALU.mult, ALU.mult).then_inc(e_mr, 1)
                pool.wait_ge(c_out, m + 1)
                g_.tensor_tensor(osc[:], olin[:], gout[:], ALU.mult).then_inc(g_o, 1)
                pool.wait_ge(g_o, 2 * m + 1)
                if later(m):
                    pool.wait_ge(d_out, 16 * m)
                settle(pool)
                g_.tensor_tensor(ores[:], osc[:], xa[:, bass.ds(m, 1), :].rearrange("p o h -> p (o h)"),
                                 ALU.add).then_inc(g_o, 1)

            def step(n):
                p, x = n - 1, n + 1
                tokens(x)
                masked_bias(n, 3)
                batch_values(n)
                masked_bias(x, 0)
                masked_bias(x, 1)
                masked_bias(x, 2)
                output(p)

            pool.wait_ge(one["v_xnT"], NG)
            tokens(0)
            pool.wait_ge(one["a_bias"], HGS)
            pool.wait_ge(one["g_mask"], 1)
            for g in range(3):
                masked_bias(0, g)
            step(0)
            step(1)
            with pool.Fori(2, B - 1) as n:
                step(n)
            step(B - 1)
            step(B)


_INS = ["x", "cond_64", "mask_BxS_bf1", "L0_cond_wt", "L0_cond_wg", "L0_cond_w_gate", "L0_cond_w_up",
        "L0_cond_w_down", "L0_cond_sw_gate", "L0_cond_sw_up", "L0_cond_sw_down", "L1_cond_g_norm", "L1_cond_Wq",
        "L1_cond_Wkv", "L1_cond_q_scale", "L1_cond_k_scale", "L1_cond_null_attn_bias", "L1_cond_w0", "L1_cond_b0",
        "L1_cond_g0", "L1_cond_w1", "L1_cond_b1", "L1_cond_g1", "L1_cond_w2", "L1_cond_b2", "L1_cond_Wout",
        "L1_cond_g_out"]


def shape_constants():
    eye = np.eye(128, dtype=np.float32)
    esel = np.zeros((3, E, EC, 128), np.float32)
    for e in range(E):
        esel[:, e, e // 2, (e % 2) * M:(e % 2 + 1) * M] = 1.0
    nsel = np.zeros((128, PAIRS, NH), np.float32)
    for c in range(PAIRS):
        for r in range(2):
            nsel[r * D:(r + 1) * D, c, 2 * c + r] = 1.0
    return {
        "c_ident": eye,
        "c_flip": np.ascontiguousarray(eye[::-1]),
        "c_esel": esel.reshape(3 * E, EC, 128),
        "c_nsel": nsel,
        "c_pos": np.arange(T, dtype=np.float32).reshape(T, 1),
        "c_rank": np.tile(np.arange(E, 0, -1, dtype=np.float32), (B, 1)),
    }


def kernel(**inputs):
    import concourse.bacc as _bacc
    from concourse import mybir as _mybir
    from concourse.bass_utils import run_bass_kernel_spmd as _run

    nc = _bacc.Bacc("TRN2", target_bir_lowering=False, num_devices=1)
    arrays, aps = {}, {}
    named = [(n, np.ascontiguousarray(inputs[n])) for n in _INS] + list(shape_constants().items())
    for name, v in named:
        if v.dtype == np.bool_:
            v = v.view(np.uint8)
        arrays[f"in_{name}"] = v
        aps[name] = nc.dram_tensor(f"in_{name}", v.shape, _mybir.dt.from_np(v.dtype), kind="ExternalInput").ap()
    aps["mask"] = aps["mask_BxS_bf1"]
    out = nc.dram_tensor("out_0", (B, T, H), F32, kind="ExternalOutput").ap()
    build(nc, aps, out)
    r = _run(nc, [arrays], core_ids=[0])
    return np.asarray(r.results[0]["out_0"])
```

```python
from contextlib import ExitStack

import numpy as np

import concourse.bass as bass
from concourse import mybir

F32 = mybir.dt.float32
BF16 = mybir.dt.bfloat16
F16 = mybir.dt.float16
U8 = mybir.dt.uint8
ALU = mybir.AluOpType
ACT = mybir.ActivationFunctionType
AX = mybir.AxisListType

B, T, H = 16, 128, 128
E, M = 8, 64
NH, D = 16, 64
EC = E * M // 128
MC = EC + 1
GB = 4
NG = B // GB
GT = GB * T
HG = 4
HGS = NH // HG
PAIRS = NH // 2
LN_EPS = 1e-5
NEG = -1e30
NORM_MIN = 1e-12
NORM_SCALE = 256.0
SLOPE = 0.01
REL = 2 * T - 1
C_IDENT, C_RANK, C_POS = 0, 128, 128 + B * E
C_FLIP, C_NSEL = C_POS + 1, C_POS + 129
CONST = C_NSEL + PAIRS * NH
C_FIRST, C_LAST = slice(0, C_FLIP), slice(C_FLIP, CONST)
ROWS = 6 * H + 2 * NH + 3 * D


def head_view(ap, g):
    v = ap.rearrange("p (G i r) -> p G r i", G=NH // 8, r=2)
    return v[:, g // 2, g % 2, :]


def build(nc, a, out):
    ctx = ExitStack()
    with ctx:
        def sb(name, shape, dt=F32):
            return ctx.enter_context(nc.sbuf_tensor(name, shape, dt))

        def psum(name, shape, dt=F32):
            return ctx.enter_context(nc.psum_tensor(name, shape, dt))

        def sem(name):
            return ctx.enter_context(nc.semaphore(name))

        const = sb("const", [128, CONST])
        ident, flip = const[:, C_IDENT:C_IDENT + 128], const[:, C_FLIP:C_FLIP + 128]
        nsel = const[:, C_NSEL:C_NSEL + PAIRS * NH]
        rank = const[:, C_RANK:C_RANK + B * E].rearrange("p (b e) -> p b e", e=E)
        pos = const[:, C_POS:C_POS + 1]
        identb = sb("identb", [128, 128], BF16)
        esel = sb("esel", [3 * E, EC, 128], BF16)
        eself = sb("eself", [3 * E, EC, 128])
        ones = sb("ones", [128, 128])
        zrow = sb("zrow", [1, GT], BF16)
        wg = sb("wg", [128, MC, 128])
        wu = sb("wu", [128, MC, 128])
        wd = sb("wd", [128, MC, 128])
        wq = sb("wq", [128, NH * D])
        wkvn = sb("wkvn", [128, NH + 2 * D])
        wo = sb("wo", [128, PAIRS, 128])
        router = sb("router", [E, H + D])
        rows = sb("rows", [128, ROWS])
        w0, b0, g0, b1, g1, gout = (rows[:, k * H:(k + 1) * H] for k in range(6))
        b2, nullb = (rows[:, 6 * H + k * NH:6 * H + (k + 1) * NH] for k in range(2))
        nkrow, qrow, krow = (rows[:, 6 * H + 2 * NH + k * D:6 * H + 2 * NH + (k + 1) * D] for k in range(3))
        cond = sb("cond", [B, D])
        wtT = sb("wtT", [128, E])
        wgT = sb("wgT", [D, E])
        condT = sb("condT", [D, B])
        gl = sb("gl", [B, B, E])
        gnorm = sb("gnorm", [128, 1])
        qsc = sb("qsc", [128, 1])
        ksc = sb("ksc", [128, 1])
        ksc8 = sb("ksc8", [128, 1])
        nvcol = sb("nvcol", [128, 1])
        nvblk = sb("nvblk", [128, PAIRS, NH])
        nvw = sb("nvw", [NH, H])
        frs = sb("frs", [128, D])
        nulls = sb("nulls", [128, 8])
        w1 = sb("w1", [128, H])
        w2 = sb("w2", [128, NH])
        ph = sb("ph", [128, 4, H])
        phT = sb("phT", [128, H])
        pstat = sb("pstat", [128, 16])
        rel = sb("rel", [128, NH])
        relT = sb("relT", [NH, REL])
        bias = sb("bias", [128, NH, T])
        biasr = sb("biasr", [128, NH, T])
        masku = sb("masku", [128, B, T], U8)
        maskb = sb("maskb", [128, B, T])
        biasm = sb("biasm", [128, NH, T])
        xa = sb("xa", [128, B, H])
        xT = sb("xT", [128, B * T])
        xc = sb("xc", [128, B, H])
        sq = sb("sq", [128, GB, H])
        msum = sb("msum", [128, GB])
        nmean = sb("nmean", [128, GB])
        var = sb("var", [128, GB])
        rstd = sb("rstd", [128, 4, GB])
        rt = sb("rt", [128, 8, B, E])
        rs = sb("rs", [128, 8, B])
        cp = sb("cp", [128, B, 3, E], BF16)
        cT = sb("cT", [3 * E, B * T], BF16)
        gs = sb("gs", [128, MC, GT])
        hub = sb("hub", [128, 2, GT])
        hh = sb("hh", [128, MC, GT])
        xnb = sb("xnb", [128, T])
        q2 = sb("q2", [128, NH, D])
        kvs = sb("kvs", [128, NH + 2 * D])
        vaug = sb("vaug", [128, 2, D + 1], F16)
        fro = sb("fro", [128, 8])
        ss = sb("ss", [128, NH + 1])
        nw = sb("nw", [128, 4, NH + 1])
        lns = sb("lns", [128, NH + 1])
        qh = sb("qh", [128, NH, D])
        kk = sb("kk", [128, 2, D])
        nmr = sb("nmr", [128, 1])
        k2 = sb("k2", [128, D])
        qT = sb("qT", [128, PAIRS, T])
        kT = sb("kT", [128, T])
        nnl = sb("nnl", [128, 2, NH])
        ssb = sb("ssb", [128, 2, HG, T])
        mx = sb("mx", [128, NH])
        nm = sb("nm", [128, NH])
        pnd = sb("pnd", [128, NH])
        pn = sb("pn", [128, NH])
        pr = sb("pr", [128, 2, HG, T])
        pTh = sb("pTh", [128, 2, HG, T], F16)
        pTl = sb("pTl", [128, 2, HG, T], F16)
        den = sb("den", [128, 2, HG])
        on = sb("on", [128, NH, D])
        an = sb("an", [128, NH])
        oT = sb("oT", [128, PAIRS, T])
        anT = sb("anT", [NH, T])
        ost = sb("ost", [128, 6])
        omv = sb("omv", [128, 2])
        onw = sb("onw", [128, 6])
        olin = sb("olin", [128, H])
        osc = sb("osc", [128, H])
        ores = sb("ores", [128, H])

        bk = [psum(f"bk{i}", [128, 512]) for i in range(6)]
        bq = psum("bq", [128, 2, 512])

        scratch = nc.dram_tensor("relbias_scratch", (NH, REL), F32, kind="Internal").ap()

        l_pos, l_route, l_moe, l_att, l_mask = (sem(n) for n in (
            "l_pos", "l_route", "l_moe", "l_att", "l_mask"))
        l_rows, l_late = sem("l_rows"), sem("l_late")
        l_x = [sem(f"l_x{g}") for g in range(NG)]
        d_rel, d_bias, d_out = sem("d_rel"), sem("d_bias"), sem("d_out")
        one = {n: sem(n) for n in (
            "p_wt", "p_gl", "p_xT", "p_lg", "p_cT", "p_h1T", "p_h1", "p_h2T", "p_rel", "p_relT", "p_nvw",
            "p_bias", "p_xnT", "a_e1", "a_r1", "a_exp", "a_nk", "a_bias", "a_xT", "a_cT", "a_xnT", "a_hT",
            "a_relT", "a_wo", "g_nvblk", "g_nk", "v_fror", "v_nkrow", "v_wt", "v_gld", "v_d", "v_cp", "v_hs",
            "v_hg", "v_hT", "v_relT", "v_nk", "v_nvw", "v_wkvn", "v_lnp", "v_ones", "v_fro", "p_fro",
            "a_fro", "g_mask")}
        v_set = sem("v_set")
        m_gate, m_up, m_cb, m_d, m_lk, m_hu, m_h, m_x1, m_st, m_sq, m_vr, m_sd, m_nt, m_xn = (sem(n) for n in (
            "m_gate", "m_up", "m_cb", "m_d", "m_lk", "m_hu", "m_h", "m_x1", "m_st", "m_sq", "m_vr", "m_sd", "m_nt",
            "m_xn"))
        m_gs = sem("m_gs")
        t_s, t_pT, t_av, t_q, t_kv, t_qT, t_kT, t_oT, t_anT, t_out = (sem(n) for n in (
            "t_s", "t_pT", "t_av", "t_q", "t_kv", "t_qT", "t_kT", "t_oT", "t_anT", "t_out"))
        c_exp, c_pT, c_q2, c_kv, c_kk, c_kT, c_qT, c_oT, c_anT, c_lnq, c_lno, c_out = (sem(n) for n in (
            "c_exp", "c_pT", "c_q2", "c_kv", "c_kk", "c_kT", "c_qT", "c_oT", "c_anT", "c_lnq", "c_lno", "c_out"))
        e_s, e_mx, e_nm, e_pl, e_dn, e_on, e_sq, e_ss, e_nq, e_qh, e_nl, e_st, e_var, e_no, e_mr = (
            sem(n) for n in ("e_s", "e_mx", "e_nm", "e_pl", "e_dn", "e_on", "e_sq", "e_ss", "e_nq", "e_qh", "e_nl",
                             "e_st", "e_var", "e_no", "e_mr"))
        settled = sem("settled")
        g_xn, g_bias, g_v, g_o = (sem(n) for n in ("g_xn", "g_bias", "g_v", "g_o"))

        block = ctx.enter_context(nc.Block())

        def settle(engine):
            engine.sem_inc(settled, 1)

        def live(m):
            return not isinstance(m, int) or 0 <= m < B

        def later(m):
            return not isinstance(m, int) or m > 0

        def projected(m):
            return bk[0] if isinstance(m, int) and m == B - 1 else bk[5]

        @block.sync
        def _(sp):
            def load(dst, src, s):
                sp.dma_start(dst, src).then_inc(s, 16)

            load(const[:, C_FIRST], a["c_const"][:, C_FIRST], l_route)
            load(router[:], a["p_router"], l_route)
            load(cond[:], a["cond_64"], l_route)
            for g in range(NG):
                load(xa[:, g * GB:(g + 1) * GB, :], a["x"][g * GB:(g + 1) * GB].rearrange("b t h -> t b h"), l_x[g])
                if g == 1:
                    early = slice(0, 3 * H)
                    load(rows[:, early], a["p_rows"][:, early].to_broadcast([128, 3 * H]), l_rows)
            load(w1[:], a["L1_cond_w1"], l_pos)
            late = slice(3 * H, ROWS)
            load(rows[:, late], a["p_rows"][:, late].to_broadcast([128, ROWS - 3 * H]), l_pos)
            for dst, ex, sh in ((wg, "L0_cond_w_gate", "L0_cond_sw_gate"), (wu, "L0_cond_w_up", "L0_cond_sw_up")):
                load(dst[:, 0:EC, :].rearrange("p c (e m) -> p (c e) m", m=M), a[ex].rearrange("e h m -> h e m"), l_moe)
                load(dst[:, EC, :], a[sh], l_moe)
            load(eself[:], a["c_esel"], l_moe)
            load(w2[:], a["L1_cond_w2"], l_late)
            load(const[:, C_LAST], a["c_const"][:, C_LAST], l_late)
            load(wd[:, 0:EC, :], a["L0_cond_w_down"].rearrange("(c e) m h -> (e m) c h", e=2), l_moe)
            load(wd[:, EC, :], a["L0_cond_sw_down"], l_moe)
            load(wq[:], a["L1_cond_Wq"], l_att)
            load(wkvn[:, NH:], a["L1_cond_Wkv"], l_att)
            load(wo[:], a["L1_cond_Wout"].rearrange("(c p) n -> p c n", p=128), l_att)
            load(gnorm[:], a["L1_cond_g_norm"].rearrange("(n o) -> n o", o=1), l_att)
            for half in range(2):
                hs = slice(half * D, (half + 1) * D)
                load(qsc[hs], a["L1_cond_q_scale"].rearrange("(n o) -> n o", o=1), l_att)
                load(ksc[hs], a["L1_cond_k_scale"].rearrange("(n o) -> n o", o=1), l_att)
                load(nvcol[hs], a["cond_64"][1:2, :].rearrange("o n -> n o"), l_att)
            load(masku[:], a["mask"].rearrange("(o b) t -> o b t", o=1).to_broadcast([128, B, T]), l_mask)
            sp.wait_ge(one["a_relT"], 1)
            sp.dma_start(scratch, relT[:]).then_inc(d_rel, 16)
            sp.wait_ge(d_rel, 16)
            for g in range(HGS):
                first = (8 * (g // 2) + g % 2) * REL
                src = bass.AP(tensor=scratch.tensor, offset=first, ap=[[1, 128], [2 * REL, HG], [1, T]])
                sp.dma_start(biasr[:, g * HG:(g + 1) * HG, :], src).then_inc(d_bias, 16)

            def store(m):
                sp.wait_ge(g_o, 2 * m + 2)
                sp.dma_start(out[bass.ds(m, 1)].rearrange("o t h -> (o t) h"), ores[:]).then_inc(d_out, 16)

            with sp.Fori(0, B) as m:
                store(m)
            sp.wait_ge(d_out, 16 * B)
        L_ROUTE, L_POS, L_LATE, L_MOE, L_ATT = 16 * 3, 16 * 2, 16 * 2, 16 * 7, 16 * 10
        GATE, UP = (bk[1], bk[2], bk[1], bk[2], bk[0]), (bk[3], bk[4], bk[3], bk[4], bq[:, 1, :])
        CB, Y = bk[5], bq[:, 0, :]

        def filled(q, c):
            return c + 2 if isinstance(q, int) and q == 0 and c in (2, 3) else MC * q + c + 1


        @block.tensor
        def _(pe):
            mm, tr = nc.tensor.matmul, nc.tensor.transpose

            pe.wait_ge(l_route, L_ROUTE)
            tr(bk[0][:, 0:E], router[:, 0:H], ident[0:E, 0:E])
            tr(bk[0][0:D, E:2 * E], router[:, H:], ident[0:E, 0:E])
            tr(bk[0][0:D, 2 * E:2 * E + B], cond[:], ident[0:B, 0:B]).then_inc(one["p_wt"], 1)
            def logits(g):
                pe.wait_ge(one["a_xT"], g + 1)
                for b in range(g * GB, (g + 1) * GB):
                    last = mm(bk[5][:, b * E:(b + 1) * E], xT[:, b * T:(b + 1) * T], wtT[:], start=False,
                              stop=(b == B - 1), skip_group_check=True)
                if g == NG - 1:
                    last.then_inc(one["p_lg"], 1)

            pe.wait_ge(one["v_wt"], 3)
            mm(bk[0][0:B, 64:64 + E], condT[:], wgT[:], start=True, stop=True).then_inc(one["p_gl"], 1)
            for g in range(NG):
                pe.wait_ge(l_x[g], 16)
                for i in range(GB):
                    last = tr(bk[1 + g][:, i * T:(i + 1) * T], xa[:, g * GB + i, :], ident)
                last.then_inc(one["p_xT"], 1)
                if g == 0:
                    pe.wait_ge(one["v_gld"], 1)
                    pe.wait_ge(one["v_ones"], 1)
                    mm(bk[5][:, 0:B * E], ones[0:B, :], gl[:].rearrange("p b e -> p (b e)"), start=True, stop=False,
                       skip_group_check=True)
                else:
                    if g == 3:
                        pe.wait_ge(one["v_hT"], 1)
                        pe.wait_ge(l_pos, L_POS)
                        mm(bk[0][:, 0:H], phT[:], w1[:], start=True, stop=True).then_inc(one["p_h1"], 1)
                    logits(g - 1)
                if g == 2:
                    pe.wait_ge(one["v_hs"], 1)
                    tr(bk[0][:, 0:H], ph[:, 0, :], ident).then_inc(one["p_h1T"], 1)
            logits(NG - 1)

            def gate_up(q, c):
                x_q = xT[:, bass.ds(q * GT, GT)]
                first = isinstance(q, int) and q == 0
                if c in (2, 3):
                    read = MC * q + c - 1
                elif not first:
                    read = MC * q if c == EC else MC * q - 2 + c
                if c in (2, 3) or not first:
                    pe.wait_ge(m_lk, read)
                mm(GATE[c][:], wg[:, c, :], x_q, start=True, stop=True).then_inc(m_gate, 1)
                if c in (2, 3) or not first:
                    pe.wait_ge(m_hu, read)
                mm(UP[c][:], wu[:, c, :], x_q, start=True, stop=True).then_inc(m_up, 1)

            def coefficients(q, c):
                if c > 0 or not isinstance(q, int) or q > 0:
                    pe.wait_ge(m_h, EC * q + c)
                settle(pe)
                mm(CB[:], esel[:, c, :], cT[:, bass.ds(q * GT, GT)], start=True, stop=True).then_inc(m_cb, 1)

            def down(q, c):
                if c < EC:
                    pe.wait_ge(m_h, EC * q + c + 1)
                else:
                    pe.wait_ge(m_hu, MC * q + MC)
                if c == 0:
                    if not isinstance(q, int) or q > 0:
                        pe.wait_ge(m_x1, q)
                    mm(Y, zrow[:, 0:128], zrow[:], start=True, stop=False, skip_group_check=True)
                for i in range(GB):
                    last = mm(Y[:, i * H:(i + 1) * H], hh[:, c, i * T:(i + 1) * T], wd[:, c, :],
                              start=False, stop=(c == MC - 1), skip_group_check=True)
                last.then_inc(m_d, 1)

            pe.wait_ge(l_moe, L_MOE)
            gate_up(0, 0)
            pe.wait_ge(l_late, L_LATE)
            pe.wait_ge(one["v_hs"], 2)
            tr(Y[:, 0:H], ph[:, 0, :], ident).then_inc(one["p_h2T"], 1)
            gate_up(0, 1)
            pe.wait_ge(one["a_hT"], 1)
            mm(Y[:, 0:NH], phT[:], w2[:], start=True, stop=True).then_inc(one["p_rel"], 1)
            x_0 = xT[:, 0:GT]
            mm(GATE[EC][:], wg[:, EC, :], x_0, start=True, stop=True).then_inc(m_gate, 1)
            pe.wait_ge(one["v_relT"], 1)
            mm(Y[0:NH, 0:T], rel[:], flip, start=True, stop=True).then_inc(one["p_relT"], 1)
            mm(UP[EC][:], wu[:, EC, :], x_0, start=True, stop=True).then_inc(m_up, 1)
            pe.wait_ge(one["v_cp"], 1)
            pe.wait_ge(one["a_relT"], 1)
            for b in range(B):
                dst = (CB[:], Y)[b // 8].bitcast(BF16)
                last = tr(dst[0:3 * E, (b % 8) * T:(b % 8 + 1) * T], cp[:, b].rearrange("p s e -> p (s e)"), identb[:])
                if b % 8 == 7:
                    last.then_inc(one["p_cT"], 1)
            pe.wait_ge(one["a_cT"], 2)
            coefficients(0, 0)
            gate_up(0, 2)
            pe.wait_ge(one["a_cT"], 3)
            pe.wait_ge(one["a_fro"], 1)
            mm(Y[:, 0:1], ones[:], fro[:, 1:2], start=True, stop=True).then_inc(one["p_fro"], 1)
            coefficients(0, 1)
            coefficients(0, 2)
            pe.wait_ge(one["v_fro"], 1)
            down(0, 0)
            gate_up(0, 3)
            coefficients(0, 3)
            down(0, 1)
            down(0, 2)
            with pe.Fori(1, NG) as q:
                for c in range(MC):
                    gate_up(q, c)
                    if c < EC:
                        coefficients(q, c)
                    if c >= 2:
                        down(q, c - 2)
                    else:
                        down(q - 1, c + 3)
            down(NG - 1, 3)
            down(NG - 1, 4)

            SB, PTB, OB, MB, XB = (bk[0], bk[1]), bk[2], bk[3], bk[4], bk[5]

            def scores(m, g):
                if not live(m):
                    return
                if g < 2:
                    pe.wait_ge(c_kT, m + 1)
                else:
                    pe.wait_ge(c_qT, 2 * m + 2)
                if later(m) or g >= 2:
                    pe.wait_ge(e_s, 4 * m + g - 1)
                half = slice(D * (g % 2), D * (g % 2) + D)
                for i in range(HG):
                    last = mm(SB[g % 2][:, i * T:(i + 1) * T], qT[half, HG * (g // 2) + i, :], kT[half, :],
                              start=True, stop=True)
                last.then_inc(t_s, 1)

            def probs_T(m, g):
                if not live(m):
                    return
                pe.wait_ge(c_exp, 4 * m + g + 1)
                if later(m) or g >= 1:
                    pe.wait_ge(e_pl, 4 * m + g)
                for i in range(HG):
                    last = tr(PTB[:, i * T:(i + 1) * T], pr[:, g % 2, i, :], ident)
                last.then_inc(t_pT, 1)

            def values(m, g):
                if not live(m):
                    return
                pe.wait_ge(e_pl, 4 * m + g + 1)
                if g == 0:
                    pe.wait_ge(g_v, 2 * m + 2)
                if later(m) or g >= 1:
                    pe.wait_ge(e_on, 4 * m + g)
                for i in range(HG):
                    o = OB[:, i * (D + 1):(i + 1) * (D + 1)]
                    mm(o, pTh[:, g % 2, i, :], vaug[:, 0, :], start=True, stop=False)
                    mm(o, pTh[:, g % 2, i, :], vaug[:, 1, :], start=False, stop=False)
                    last = mm(o, pTl[:, g % 2, i, :], vaug[:, 0, :], start=False, stop=True)
                last.then_inc(t_av, 1)

            def queries(m, half):
                if not live(m):
                    return
                if half == 0:
                    pe.wait_ge(g_xn, m + 1)
                mm(bq[:, half, :], xnb[:], wq[:, half * 512:(half + 1) * 512], start=True, stop=True).then_inc(t_q, 1)

            def keys_values(m):
                if not live(m):
                    return
                mm(MB[:, 0:NH + 2 * D], xnb[:], wkvn[:], start=True, stop=True).then_inc(t_kv, 1)

            def queries_T(m, half):
                if not live(m):
                    return
                pe.wait_ge(e_qh, 2 * m + half + 1)
                for c in range(4):
                    cc = 4 * half + c
                    last = tr(bq[:, half, c * T:(c + 1) * T], qh[:, 2 * cc:2 * cc + 2, :].rearrange("p h d -> p (h d)"),
                              ident)
                last.then_inc(t_qT, 1)

            def keys_T(m):
                if not live(m):
                    return
                pe.wait_ge(c_kk, m + 1)
                tr(MB[:, 0:T], kk[:].rearrange("p r d -> p (r d)"), ident).then_inc(t_kT, 1)

            def outputs_T(m, half):
                if not live(m):
                    return
                pe.wait_ge(e_on, 4 * m + 2 * half + 2)
                if half == 1:
                    pe.wait_ge(c_oT, 2 * m + 1)
                elif later(m):
                    pe.wait_ge(c_out, m)
                for c in range(4 * half, 4 * half + 4):
                    last = tr(XB[:, (c % 4) * T:(c % 4 + 1) * T], on[:, 2 * c:2 * c + 2, :].rearrange("p h d -> p (h d)"),
                              ident)
                last.then_inc(t_oT, 1)

            def null_weights_T(m):
                if not live(m):
                    return
                if live(m + 2):
                    pe.wait_ge(c_kv, m + 3)
                else:
                    pe.wait_ge(c_kT, B)
                tr(MB[0:NH, 256:256 + T], an[:], ident).then_inc(t_anT, 1)

            def project(m):
                if not live(m):
                    return
                pe.wait_ge(c_oT, 2 * m + 2)
                pe.wait_ge(c_anT, m + 1)
                for c in range(PAIRS):
                    mm(XB[:, 0:H], oT[:, c, :], wo[:, c, :], start=(c == 0), stop=False)
                mm(XB[:, 0:H], anT[:], nvw[:], start=False, stop=True).then_inc(t_out, 1)

            def null_value():
                pe.wait_ge(one["a_xnT"], NG)
                pe.wait_ge(one["g_nvblk"], 1)
                pe.wait_ge(one["a_wo"], 2)
                for c in range(PAIRS):
                    last = mm(XB[0:NH, 0:H], nvblk[:, c, :], wo[:, c, :], start=(c == 0), stop=(c == PAIRS - 1))
                last.then_inc(one["p_nvw"], 1)

            def step(n):
                p, x = n - 1, n + 1
                outputs_T(p, 0)
                queries(x, 0)
                probs_T(n, 0)
                values(p, 3)
                queries(x, 1)
                scores(n, 3)
                keys_values(x)
                outputs_T(p, 1)
                null_weights_T(p)
                probs_T(n, 1)
                values(n, 0)
                if live(p):
                    project(p)
                else:
                    null_value()
                queries_T(x, 0)
                keys_T(x)
                probs_T(n, 2)
                values(n, 1)
                scores(x, 0)
                queries_T(x, 1)
                scores(x, 1)
                values(n, 2)
                probs_T(n, 3)
                scores(x, 2)

            def normalised_T(g, bank):
                pe.wait_ge(m_xn, g + 2)
                for i in range(GB):
                    last = tr(bank[:, i * T:(i + 1) * T], xc[:, g * GB + i, :], ident)
                last.then_inc(one["p_xnT"], 1)

            def biases(g):
                if g >= 2:
                    pe.wait_ge(one["a_bias"], g - 1)
                mm((bk[0], bk[5])[g % 2][:], flip, biasr[:, g * HG:(g + 1) * HG, :].rearrange("p i t -> p (i t)"),
                   start=True, stop=True).then_inc(one["p_bias"], 1)

            pe.wait_ge(m_lk, MC * NG)
            pe.wait_ge(m_hu, MC * NG)
            for g in range(NG - 1):
                normalised_T(g, bk[1 + g])
            pe.wait_ge(d_bias, 16 * HGS)
            biases(0)
            pe.wait_ge(m_h, EC * NG)
            biases(1)
            pe.wait_ge(m_x1, NG)
            pe.wait_ge(one["v_wkvn"], 1)
            queries(0, 0)
            queries(0, 1)
            keys_values(0)
            biases(2)
            biases(3)
            queries_T(0, 0)
            keys_T(0)
            queries_T(0, 1)
            pe.wait_ge(one["a_bias"], HGS)
            scores(0, 0)
            pe.wait_ge(one["a_xnT"], NG - 1)
            normalised_T(NG - 1, XB)
            scores(0, 1)
            scores(0, 2)
            step(0)
            pe.wait_ge(one["v_nvw"], 1)
            step(1)
            with pe.Fori(2, B - 1) as n:
                step(n)
            step(B - 1)
            last_half = PAIRS // 2
            outputs_T(B - 1, 0)
            values(B - 1, 3)
            pe.wait_ge(c_oT, 2 * B - 1)
            for c in range(last_half):
                mm(projected(B - 1)[:, 0:H], oT[:, c, :], wo[:, c, :], start=(c == 0), stop=False)
            outputs_T(B - 1, 1)
            null_weights_T(B - 1)
            pe.wait_ge(c_oT, 2 * B)
            pe.wait_ge(c_anT, B)
            for c in range(last_half, PAIRS):
                mm(projected(B - 1)[:, 0:H], oT[:, c, :], wo[:, c, :], start=False, stop=False)
            mm(projected(B - 1)[:, 0:H], anT[:], nvw[:], start=False, stop=True).then_inc(t_out, 1)

        @block.scalar
        def _(act):
            fn = nc.scalar.activation
            nc.scalar.preload_act_table_set("natural_log_exp_and_others")

            def rsqrt_seed(dst, tmp, src, s, base):
                fn(tmp, src, ACT.Ln).then_inc(s, 1)
                act.wait_ge(s, base + 1)
                fn(dst, tmp, ACT.Exp, scale=-0.5).then_inc(s, 1)

            def x_T(g):
                act.wait_ge(one["p_xT"], g + 1)
                fn(xT[:, g * GT:(g + 1) * GT], bk[1 + g][:], ACT.Copy).then_inc(one["a_xT"], 1)

            def deviation(k):
                act.wait_ge(one["v_lnp"], k)
                rsqrt_seed(pstat[:, 11:12], pstat[:, 10:11], pstat[:, 8:9], one["a_r1"], 2 * k - 2)

            def silu(k):
                act.wait_ge(one["v_hg"], k)
                fn(ph[:, 2, :], ph[:, 1, :], ACT.Exp, scale=-1.0).then_inc(one["a_e1"], 1)

            x_T(0)
            deviation(1)
            x_T(1)
            silu(1)
            x_T(2)
            x_T(3)
            deviation(2)
            silu(2)
            act.wait_ge(one["v_nk"], 1)
            rsqrt_seed(nulls[:, 2:3], nulls[:, 1:2], nulls[:, 0:1], one["a_nk"], 0)
            act.wait_ge(one["v_d"], 1)
            fn(rt[:, 1], rt[:, 0], ACT.Exp, scale=0.5).then_inc(one["a_exp"], 1)
            act.wait_ge(one["p_h2T"], 1)
            fn(phT[:], bq[:, 0, 0:H], ACT.Copy).then_inc(one["a_hT"], 1)
            act.wait_ge(l_moe, L_MOE)
            fn(esel[:], eself[:], ACT.Copy).then_inc(one["a_cT"], 1)

            def gate(q, c):
                act.wait_ge(m_gate, filled(q, c))
                if not isinstance(q, int):
                    act.wait_ge(m_hu, MC * q - MC + c + 1)
                fn(gs[:, c, :], GATE[c][:], ACT.Copy, scale=SLOPE).then_inc(m_gs, 1)

            gate(0, 0)
            gate(0, 1)
            act.wait_ge(one["p_relT"], 1)
            fn(relT[:, 0:T], bq[0:NH, 0, 0:T], ACT.Copy).then_inc(one["a_relT"], 1)
            act.wait_ge(l_att, L_ATT)
            fn(frs[:], wkvn[:, NH + D:], ACT.Square, scale=gnorm[:, 0:1], accum_out=fro[:, 1:2]).then_inc(one["a_fro"], 1)
            for half in range(2):
                act.wait_ge(one["p_cT"], half + 1)
                fn(cT[:, half * 1024:(half + 1) * 1024], (bk[5][:], bq[:, 0, :])[half].bitcast(BF16)[0:3 * E, :],
                   ACT.Copy).then_inc(one["a_cT"], 1)
            gate(0, 2)
            gate(0, 3)
            act.wait_ge(one["v_fro"], 1)
            rsqrt_seed(fro[:, 4:5], fro[:, 3:4], fro[:, 2:3], one["a_fro"], 1)
            gate(0, 4)
            act.wait_ge(one["a_fro"], 3)
            fn(wkvn[:, NH + D:], wkvn[:, NH + D:], ACT.Copy, scale=fro[:, 4:5]).then_inc(one["a_wo"], 1)
            act.wait_ge(one["v_fror"], 1)
            wo_all = wo[:].rearrange("p c n -> p (c n)")
            fn(wo_all, wo_all, ACT.Copy, scale=fro[:, 5:6]).then_inc(one["a_wo"], 1)

            def token_deviation(r):
                act.wait_ge(m_vr, 2 * r + 2)
                rsqrt_seed(rstd[:, 2, :], rstd[:, 1, :], rstd[:, 0, :], m_sd, 2 * r)

            with act.Fori(1, NG) as q:
                for c in range(MC):
                    gate(q, c)
                token_deviation(q - 1)

            PTB, OB, MB, XB = bk[2], bk[3], bk[4], bk[5]

            def exps(m, g):
                if not live(m):
                    return
                act.wait_ge(e_nm, 4 * m + g + 1)
                if later(m) or g >= 2:
                    act.wait_ge(t_pT, 4 * m + g - 1)
                hs = slice(HG * g, HG * g + HG)
                fn(pn[:, hs], pnd[:, hs], ACT.Exp)
                for i in range(HG):
                    last = fn(pr[:, g % 2, i, :], ssb[:, g % 2, i, :], ACT.Exp, bias=nm[:, HG * g + i:HG * g + i + 1])
                last.then_inc(c_exp, 1)

            def probs_T(m, g):
                if not live(m):
                    return
                act.wait_ge(t_pT, 4 * m + g + 1)
                fn(pTh[:, g % 2].rearrange("p i t -> p (i t)"), PTB[:], ACT.Copy).then_inc(c_pT, 1)

            def squared_queries(m, half):
                if not live(m):
                    return
                act.wait_ge(t_q, 2 * m + half + 1)
                fn(q2[:, 8 * half:8 * half + 8].rearrange("p h d -> p (h d)"), bq[:, half, :],
                   ACT.Square).then_inc(c_q2, 1)

            def keys_values(m):
                if not live(m):
                    return
                act.wait_ge(t_kv, m + 1)
                if later(m):
                    act.wait_ge(g_v, 2 * m)
                fn(kvs[:], MB[:, 0:NH + 2 * D], ACT.Copy).then_inc(c_kv, 1)

            def outputs_T(m, half):
                if not live(m):
                    return
                act.wait_ge(t_oT, 2 * m + half + 1)
                fn(oT[:, 4 * half:4 * half + 4, :].rearrange("p c t -> p (c t)"), XB[:], ACT.Copy).then_inc(c_oT, 1)

            def null_weights_T(m):
                if not live(m):
                    return
                act.wait_ge(t_anT, m + 1)
                fn(anT[:], MB[0:NH, 256:256 + T], ACT.Copy).then_inc(c_anT, 1)

            def norm_seeds(m):
                if not live(m):
                    return
                act.wait_ge(e_ss, m + 1)
                rsqrt_seed(nw[:, 0, :], lns[:], ss[:], c_lnq, 2 * m)

            def unit_keys(m):
                if not live(m):
                    return
                act.wait_ge(e_nq, 3 * m + 3)
                fn(kk[:], kvs[:, NH:NH + D].rearrange("p (o d) -> p o d", o=1).to_broadcast([128, 2, D]),
                   ACT.Copy, scale=nw[:, 2, NH:NH + 1]).then_inc(c_kk, 1)

            def keys_T(m):
                if not live(m):
                    return
                act.wait_ge(t_kT, m + 1)
                fn(kT[:], MB[:, 0:T], ACT.Copy, scale=ksc8[:, 0:1]).then_inc(c_kT, 1)

            def queries_T(m, half):
                if not live(m):
                    return
                act.wait_ge(t_qT, 2 * m + half + 1)
                fn(qT[:, 4 * half:4 * half + 4, :].rearrange("p c t -> p (c t)"), bq[:, half, :],
                   ACT.Copy).then_inc(c_qT, 1)

            def output_seed(m):
                if not live(m):
                    return
                act.wait_ge(e_var, m + 1)
                rsqrt_seed(onw[:, 2:3], onw[:, 1:2], onw[:, 0:1], c_lno, 2 * m)

            def output(m):
                if not live(m):
                    return
                act.wait_ge(e_mr, m + 1)
                fn(olin[:], projected(m)[:, 0:H], ACT.Identity, scale=onw[:, 4:5], bias=nmr[:, 0:1]).then_inc(c_out, 1)

            def step(n):
                p, x = n - 1, n + 1
                probs_T(p, 3)
                exps(n, 0)
                outputs_T(p, 0)
                squared_queries(x, 0)
                probs_T(n, 0)
                exps(n, 1)
                squared_queries(x, 1)
                keys_values(x)
                outputs_T(p, 1)
                null_weights_T(p)
                norm_seeds(x)
                probs_T(n, 1)
                exps(n, 2)
                unit_keys(x)
                queries_T(x, 0)
                keys_T(x)
                probs_T(n, 2)
                output_seed(p)
                exps(n, 3)
                output(p)
                queries_T(x, 1)

            def normalised_T(g, bank):
                act.wait_ge(one["p_xnT"], g + 1)
                fn(xT[:, g * GT:(g + 1) * GT], bank[:], ACT.Copy, scale=gnorm[:, 0:1]).then_inc(one["a_xnT"], 1)

            def biases(g):
                act.wait_ge(one["p_bias"], g + 1)
                fn(bias[:, g * HG:(g + 1) * HG, :].rearrange("p i t -> p (i t)"), (bk[0], bk[5])[g % 2][:],
                   ACT.Copy).then_inc(one["a_bias"], 1)

            for g in range(NG - 1):
                normalised_T(g, bk[1 + g])
            biases(0)
            biases(1)
            squared_queries(0, 0)
            squared_queries(0, 1)
            keys_values(0)
            token_deviation(NG - 1)
            biases(2)
            norm_seeds(0)
            biases(3)
            unit_keys(0)
            queries_T(0, 0)
            keys_T(0)
            queries_T(0, 1)
            normalised_T(NG - 1, XB)
            step(0)
            step(1)
            with act.Fori(2, B - 1) as n:
                step(n)
            step(B - 1)
            step(B)

        @block.vector
        def _(dve):
            v = nc.vector
            done = [0]

            def link(*instrs):
                for ins in instrs:
                    ins.then_inc(v_set, 1)
                done[0] += len(instrs)
                dve.wait_ge(v_set, done[0])

            def newton(dst, y, x, t):
                link(v.tensor_tensor(t, y, y, ALU.mult))
                link(v.scalar_tensor_tensor(out=t, in0=t, scalar=-0.5, in1=x, op0=ALU.mult, op1=ALU.mult))
                link(v.scalar_tensor_tensor(out=dst, in0=t, scalar=1.5, in1=y, op0=ALU.add, op1=ALU.mult))

            v.memset(ones[:], 1.0).then_inc(one["v_ones"], 1)
            v.memset(zrow[:], 0.0)
            v.memset(vaug[:, 0, D:D + 1], 1.0)
            v.memset(vaug[:, 1, D:D + 1], 0.0)
            v.memset(relT[:, T:], NEG).then_inc(v_set, 1)
            done[0] += 1
            dve.wait_ge(one["p_wt"], 1)
            v.tensor_copy(wtT[:], bk[0][:, 0:E]).then_inc(one["v_wt"], 1)
            v.tensor_copy(wgT[:], bk[0][0:D, E:2 * E]).then_inc(one["v_wt"], 1)
            v.tensor_copy(condT[:], bk[0][0:D, 2 * E:2 * E + B]).then_inc(one["v_wt"], 1)
            link(v.tensor_copy(identb[:], ident))

            dve.wait_ge(one["p_gl"], 1)
            link(v.tensor_copy(rs[0:B, 0, 0:E], bk[0][0:B, 64:64 + E]))
            v.tensor_tensor(gl[:], rs[0:B, 0:1, 0:E].to_broadcast([B, B, E]),
                            ident[0:B, 0:B].rearrange("p (b o) -> p b o", o=1).to_broadcast([B, B, E]),
                            ALU.mult).then_inc(one["v_gld"], 1)
            h, hn, he = ph[:, 0, :], ph[:, 1, :], ph[:, 2, :]
            mean, dev = pstat[:, 6:7], pstat[:, 12:13]
            y0, y2, xv = pstat[:, 11:12], pstat[:, 13:14], pstat[:, 8:9]
            dve.wait_ge(l_rows, 16)
            link(v.scalar_tensor_tensor(out=h, in0=w0, scalar=pos, in1=b0, op0=ALU.mult, op1=ALU.add))

            def layer(k, g):
                link(v.bn_stats(pstat[:, 0:6], h))
                link(v.bn_aggr(pstat[:, 6:8], pstat[:, 0:6]))
                v.tensor_scalar(xv, pstat[:, 7:8], LN_EPS, None, ALU.add).then_inc(one["v_lnp"], 1)
                dve.wait_ge(one["a_r1"], 2 * k)
                newton(dev, y0, xv, y2)
                link(v.tensor_scalar(ph[:, 3, :], h, mean, dev, ALU.subtract, ALU.mult))
                v.tensor_tensor(hn, ph[:, 3, :], g, ALU.mult).then_inc(one["v_hg"], 1)
                dve.wait_ge(one["a_e1"], k)
                link(v.tensor_scalar(ph[:, 3, :], he, 1.0, None, ALU.add))
                link(v.reciprocal(he, ph[:, 3, :]))
                v.tensor_tensor(h, hn, he, ALU.mult).then_inc(one["v_hs"], 1)

            layer(1, g0)
            dve.wait_ge(one["p_h1T"], 1)
            v.tensor_copy(phT[:], bk[0][:, 0:H]).then_inc(one["v_hT"], 1)
            dve.wait_ge(l_pos, L_POS)
            link(v.tensor_tensor_reduce(k2[:], nkrow, nkrow, 1.0, 0.0, ALU.mult, ALU.add, nulls[:, 3:4]),
                 v.tensor_tensor(qrow, qrow, krow, ALU.mult))
            v.tensor_scalar(nulls[:, 0:1], nulls[:, 3:4], NORM_MIN ** 2, NORM_SCALE ** 2, ALU.max,
                            ALU.mult).then_inc(one["v_nk"], 1)
            dve.wait_ge(one["p_h1"], 1)
            link(v.tensor_tensor(h, bk[0][:, 0:H], b1, ALU.add))
            layer(2, g1)

            def by_batch(ap):
                return ap.rearrange("p (b o) -> p b o", o=1).to_broadcast([128, B, E])

            top1, top2, both, d2, ex = rt[:, 2], rt[:, 5], rt[:, 3], rt[:, 4], rt[:, 1]
            lg = bk[5][:, 0:B * E].rearrange("p (b e) -> p b e", e=E)
            dve.wait_ge(one["p_lg"], 1)
            link(v.tensor_reduce(rs[:, 1, :], lg, AX.X, ALU.max))
            link(v.tensor_tensor(top1, lg, by_batch(rs[:, 1, :]), ALU.is_equal))
            v.tensor_tensor(rt[:, 0], lg, by_batch(rs[:, 1, :]), ALU.subtract).then_inc(one["v_d"], 1)
            link(v.tensor_tensor(top1, top1, rank, ALU.mult))
            link(v.tensor_reduce(rs[:, 2, :], top1, AX.X, ALU.max))
            link(v.tensor_tensor(top1, top1, by_batch(rs[:, 2, :]), ALU.is_equal))
            link(v.scalar_tensor_tensor(out=d2, in0=top1, scalar=NEG, in1=lg, op0=ALU.mult, op1=ALU.add))
            link(v.tensor_reduce(rs[:, 3, :], d2, AX.X, ALU.max))
            link(v.tensor_tensor(top2, d2, by_batch(rs[:, 3, :]), ALU.is_equal))
            link(v.tensor_tensor(top2, top2, rank, ALU.mult))
            link(v.tensor_reduce(rs[:, 4, :], top2, AX.X, ALU.max))
            link(v.tensor_tensor(top2, top2, by_batch(rs[:, 4, :]), ALU.is_equal))
            link(v.tensor_tensor(both, top1, top2, ALU.add))
            dve.wait_ge(one["a_exp"], 1)
            link(v.tensor_tensor(rt[:, 6], both, ex, ALU.mult),
                 v.tensor_reduce(rs[:, 6, :], ex, AX.X, ALU.add))
            link(v.tensor_reduce(rs[:, 5, :], rt[:, 6], AX.X, ALU.add))
            dve.wait_ge(one["p_rel"], 1)
            v.tensor_tensor(rel[:], bq[:, 0, 0:NH], b2, ALU.add).then_inc(one["v_relT"], 1)
            link(v.scalar_tensor_tensor(out=rs[:, 7, :], in0=rs[:, 6, :], scalar=1e-20, in1=rs[:, 5, :],
                                        op0=ALU.mult, op1=ALU.add))
            link(v.reciprocal(rs[:, 0, :], rs[:, 7, :]))
            link(v.tensor_tensor(rt[:, 7], rt[:, 6], by_batch(rs[:, 0, :]), ALU.mult))
            link(v.tensor_copy(cp[:, :, 0, :], rt[:, 7]))
            link(v.tensor_tensor(rt[:, 0], rt[:, 7], cp[:, :, 0, :], ALU.subtract))
            link(v.tensor_copy(cp[:, :, 1, :], rt[:, 0]))
            v.tensor_tensor(cp[:, :, 2, :], rt[:, 0], cp[:, :, 1, :], ALU.subtract).then_inc(one["v_cp"], 1)

            def later_group(q):
                return not isinstance(q, int) or q > 0

            def leaky(q, c):
                dve.wait_ge(m_gs, MC * q + c + 1)
                v.tensor_tensor(gs[:, c, :], gs[:, c, :], GATE[c][:], ALU.max).then_inc(m_lk, 1)

            def weighted(q, c):
                dve.wait_ge(m_hu, MC * q + c + 1)
                dve.wait_ge(m_cb, EC * q + c + 1)
                if later_group(q):
                    dve.wait_ge(m_d, MC * q - MC + c + 1)
                v.tensor_tensor(hh[:, c, :], hub[:, c % 2, :], CB[:], ALU.mult).then_inc(m_h, 1)

            def gated(q, c):
                dve.wait_ge(m_up, filled(q, c))
                dve.wait_ge(m_lk, MC * q + c + 1)
                if c == EC and later_group(q):
                    dve.wait_ge(m_d, MC * q)
                dst = hub[:, c % 2, :] if c < EC else hh[:, c, :]
                v.tensor_tensor(dst, gs[:, c, :], UP[c][:], ALU.mult).then_inc(m_hu, 1)

            def groups_tokens(r):
                return xa[:, bass.ds(r * GB, GB), :], xc[:, bass.ds(r * GB, GB), :]

            def residual(r):
                x_r, _ = groups_tokens(r)
                dve.wait_ge(m_d, MC * r + MC)
                v.tensor_tensor(x_r, x_r, Y.rearrange("p (b h) -> p b h", b=GB), ALU.add).then_inc(m_x1, 1)
                dve.wait_ge(m_x1, r + 1)
                settle(dve)
                v.tensor_reduce(msum[:], x_r, AX.X, ALU.add).then_inc(m_st, 1)

            def centre(r):
                x_r, xc_r = groups_tokens(r)
                dve.wait_ge(m_st, 3 * r + 1)
                v.tensor_scalar(nmean[:], msum[:], 1.0 / H, None, ALU.mult).then_inc(m_st, 1)
                dve.wait_ge(m_st, 3 * r + 2)
                v.tensor_tensor(xc_r, x_r, nmean[:].rearrange("p (b o) -> p b o", o=1).to_broadcast([128, GB, H]),
                                ALU.subtract).then_inc(m_st, 1)

            def variance(r):
                dve.wait_ge(m_sq, r + 1)
                settle(dve)
                v.tensor_reduce(var[:], sq[:], AX.X, ALU.add).then_inc(m_vr, 1)
                dve.wait_ge(m_vr, 2 * r + 1)
                v.tensor_scalar(rstd[:, 0, :], var[:], 1.0 / H, LN_EPS, ALU.mult, ALU.add).then_inc(m_vr, 1)

            def deviation(r):
                dve.wait_ge(m_sd, 2 * r + 2)
                v.tensor_tensor(rstd[:, 1, :], rstd[:, 2, :], rstd[:, 2, :], ALU.mult).then_inc(m_nt, 1)
                dve.wait_ge(m_nt, 3 * r + 1)
                v.scalar_tensor_tensor(out=rstd[:, 1, :], in0=rstd[:, 1, :], scalar=-0.5, in1=rstd[:, 0, :],
                                       op0=ALU.mult, op1=ALU.mult).then_inc(m_nt, 1)
                dve.wait_ge(m_nt, 3 * r + 2)
                dve.wait_ge(m_xn, r + 1)
                v.scalar_tensor_tensor(out=rstd[:, 3, :], in0=rstd[:, 1, :], scalar=1.5, in1=rstd[:, 2, :],
                                       op0=ALU.add, op1=ALU.mult).then_inc(m_nt, 1)

            leaky(0, 0)
            gated(0, 0)
            leaky(0, 1)
            SCALE = 8.0 * NORM_SCALE * NORM_SCALE
            dve.wait_ge(one["a_nk"], 2)
            newton(nulls[:, 4:5], nulls[:, 2:3], nulls[:, 0:1], nulls[:, 5:6])
            link(v.scalar_tensor_tensor(out=krow, in0=nkrow, scalar=nulls[:, 4:5], in1=qrow,
                                        op0=ALU.mult, op1=ALU.mult))
            v.tensor_scalar(nkrow, krow, SCALE, None, ALU.mult).then_inc(one["v_nkrow"], 1)
            weighted(0, 0)
            gated(0, 1)
            dve.wait_ge(one["p_fro"], 1)
            v.tensor_scalar(fro[:, 2:3], bq[:, 0, 0:1], 1e-30, H * 2.0 ** -28, ALU.max, ALU.mult).then_inc(one["v_fro"], 1)
            weighted(0, 1)
            leaky(0, 2)
            gated(0, 2)
            weighted(0, 2)
            leaky(0, 3)
            gated(0, 3)
            weighted(0, 3)
            link(v.tensor_scalar(ksc8[:], ksc[:], qsc[:, 0:1], SCALE, ALU.mult, ALU.mult))
            leaky(0, 4)
            gated(0, 4)
            dve.wait_ge(one["a_fro"], 3)
            v.reciprocal(fro[:, 5:6], fro[:, 4:5]).then_inc(one["v_fror"], 1)

            with dve.Fori(1, NG) as q:
                for c in range(MC):
                    leaky(q, c)
                    gated(q, c)
                    if c < EC:
                        weighted(q, c)
                    if c == 1:
                        residual(q - 1)
                    if c == 2:
                        centre(q - 1)
                    if c == 3:
                        variance(q - 1)
                    if c == 4:
                        deviation(q - 1)
            SB, PTB, OB, XB = (bk[0], bk[1]), bk[2], bk[3], bk[5]

            def biased_scores(m, g):
                if not live(m):
                    return
                dve.wait_ge(t_s, 4 * m + g + 1)
                dve.wait_ge(g_bias, 4 * m + g + 1)
                if later(m) or g >= 2:
                    dve.wait_ge(c_exp, 4 * m + g - 1)
                settle(dve)
                for i in range(HG):
                    h = HG * g + i
                    last = v.tensor_tensor_reduce(ssb[:, g % 2, i, :], SB[g % 2][:, i * T:(i + 1) * T],
                                                  biasm[:, h, :], 1.0, -3e38, ALU.add, ALU.max, mx[:, h:h + 1])
                last.then_inc(e_s, 1)

            def maxima(m, g):
                if not live(m):
                    return
                hs = slice(HG * g, HG * g + HG)
                dve.wait_ge(e_s, 4 * m + g + 1)
                if g == 0:
                    dve.wait_ge(e_nl, 2 * m + 2)
                v.scalar_tensor_tensor(out=nm[:, hs], in0=mx[:, hs], scalar=-1.0, in1=nnl[:, 0, hs],
                                       op0=ALU.mult, op1=ALU.min).then_inc(e_mx, 1)

            def null_shifts(m, g):
                if not live(m):
                    return
                hs = slice(HG * g, HG * g + HG)
                dve.wait_ge(e_mx, 4 * m + g + 1)
                v.tensor_tensor(pnd[:, hs], nm[:, hs], nnl[:, 0, hs], ALU.subtract).then_inc(e_nm, 1)

            def low_part(m, g):
                if not live(m):
                    return
                dve.wait_ge(c_pT, 4 * m + g + 1)
                v.tensor_tensor(pTl[:, g % 2].rearrange("p i t -> p (i t)"), PTB[:],
                                pTh[:, g % 2].rearrange("p i t -> p (i t)"), ALU.subtract).then_inc(e_pl, 1)

            o_g = OB[:, 0:HG * (D + 1)].rearrange("p (i d) -> p i d", d=D + 1)

            def sums(m, g):
                if not live(m):
                    return
                dve.wait_ge(t_av, 4 * m + g + 1)
                v.tensor_tensor(den[:, 0, :], o_g[:, :, D], pn[:, HG * g:HG * g + HG], ALU.add).then_inc(e_dn, 1)

            def inverse_sums(m, g):
                if not live(m):
                    return
                dve.wait_ge(e_dn, 8 * m + 2 * g + 1)
                v.reciprocal(den[:, 1, :], den[:, 0, :]).then_inc(e_dn, 1)

            def attention(m, g):
                if not live(m):
                    return
                dve.wait_ge(e_dn, 8 * m + 2 * g + 2)
                v.tensor_tensor(head_view(an[:], g), pn[:, HG * g:HG * g + HG], den[:, 1, :], ALU.mult)
                on_g = on[:].rearrange("p (G i r) d -> p G r i d", G=2, r=2)[:, g // 2, g % 2]
                v.tensor_tensor(on_g, o_g[:, :, 0:D],
                                den[:, 1, :].rearrange("p (i o) -> p i o", o=1).to_broadcast([128, HG, D]),
                                ALU.mult).then_inc(e_on, 1)

            def query_norms(m, half):
                if not live(m):
                    return
                dve.wait_ge(c_q2, 2 * m + half + 1)
                v.tensor_reduce(ss[:, 8 * half:8 * half + 8], q2[:, 8 * half:8 * half + 8], AX.X,
                                ALU.add).then_inc(e_sq, 1)

            def key_norm(m):
                if not live(m):
                    return
                dve.wait_ge(c_kv, m + 1)
                v.tensor_tensor_reduce(k2[:], kvs[:, NH:NH + D], kvs[:, NH:NH + D], 1.0, 0.0, ALU.mult, ALU.add,
                                       ss[:, NH:NH + 1]).then_inc(e_sq, 1)

            def scaled_norms(m):
                if not live(m):
                    return
                dve.wait_ge(e_sq, 3 * m + 3)
                v.tensor_scalar(ss[:], ss[:], NORM_MIN ** 2, NORM_SCALE ** 2, ALU.max, ALU.mult).then_inc(e_ss, 1)

            def inverse_norms(m, part):
                if not live(m):
                    return
                if part == 0:
                    dve.wait_ge(c_lnq, 2 * m + 2)
                    v.tensor_tensor(nw[:, 1, :], nw[:, 0, :], nw[:, 0, :], ALU.mult).then_inc(e_nq, 1)
                if part == 1:
                    dve.wait_ge(e_nq, 3 * m + 1)
                    v.scalar_tensor_tensor(out=nw[:, 1, :], in0=nw[:, 1, :], scalar=-0.5, in1=ss[:],
                                           op0=ALU.mult, op1=ALU.mult).then_inc(e_nq, 1)
                if part == 2:
                    dve.wait_ge(e_nq, 3 * m + 2)
                    v.scalar_tensor_tensor(out=nw[:, 2, :], in0=nw[:, 1, :], scalar=1.5, in1=nw[:, 0, :],
                                           op0=ALU.add, op1=ALU.mult).then_inc(e_nq, 1)

            def unit_queries(m, half):
                if not live(m):
                    return
                if half == 0:
                    dve.wait_ge(e_nq, 3 * m + 3)
                hs = slice(8 * half, 8 * half + 8)
                v.tensor_tensor(qh[:, hs], bq[:, half, :].rearrange("p (h d) -> p h d", d=D),
                                nw[:, 2, hs].rearrange("p (h o) -> p h o", o=1).to_broadcast([128, 8, D]),
                                ALU.mult).then_inc(e_qh, 1)

            def null_logits(m):
                if not live(m):
                    return
                v.scalar_tensor_tensor(out=nnl[:, 1, :], in0=kvs[:, 0:NH], scalar=-1.0, in1=nw[:, 2, 0:NH],
                                       op0=ALU.mult, op1=ALU.mult).then_inc(e_nl, 1)

            def biased_null_logits(m):
                if not live(m):
                    return
                dve.wait_ge(e_nl, 2 * m + 1)
                order = "p (G i r) -> p G r i"
                for G in range(2):
                    last = v.tensor_tensor(nnl[:, 0, :].rearrange("p (G r i) -> p G r i", G=2, r=2)[:, G],
                                           nnl[:, 1, :].rearrange(order, G=2, r=2)[:, G],
                                           nullb.rearrange(order, G=2, r=2)[:, G], ALU.subtract)
                last.then_inc(e_nl, 1)

            def output_sums(m):
                if not live(m):
                    return
                dve.wait_ge(t_out, m + 1)
                v.bn_stats(ost[:], projected(m)[:, 0:H]).then_inc(e_st, 1)

            def output_variance(m):
                if not live(m):
                    return
                dve.wait_ge(e_st, 2 * m + 1)
                settle(dve)
                v.bn_aggr(omv[:], ost[:]).then_inc(e_st, 1)

            def step(n):
                p, x = n - 1, n + 1
                sums(p, 3)
                query_norms(x, 0)
                inverse_sums(p, 3)
                maxima(n, 2)
                attention(p, 3)
                low_part(n, 0)
                query_norms(x, 1)
                key_norm(x)
                null_shifts(n, 2)
                scaled_norms(x)
                biased_scores(n, 3)
                inverse_norms(x, 0)
                sums(n, 0)
                inverse_norms(x, 1)
                inverse_sums(n, 0)
                inverse_norms(x, 2)
                maxima(n, 3)
                unit_queries(x, 0)
                low_part(n, 1)
                attention(n, 0)
                output_sums(p)
                if not live(p):
                    dve.wait_ge(one["p_nvw"], 1)
                    v.tensor_copy(nvw[:], XB[0:NH, 0:H]).then_inc(one["v_nvw"], 1)
                null_logits(x)
                null_shifts(n, 3)
                output_variance(p)
                unit_queries(x, 1)
                sums(n, 1)
                low_part(n, 2)
                inverse_sums(n, 1)
                biased_null_logits(x)
                attention(n, 1)
                biased_scores(x, 0)
                sums(n, 2)
                maxima(x, 0)
                inverse_sums(n, 2)
                null_shifts(x, 0)
                biased_scores(x, 1)
                low_part(n, 3)
                maxima(x, 1)
                attention(n, 2)
                null_shifts(x, 1)
                biased_scores(x, 2)

            dve.wait_ge(one["g_nk"], 1)
            v.tensor_reduce(wkvn[:, 0:NH], q2[:], AX.X, ALU.add).then_inc(one["v_wkvn"], 1)
            residual(NG - 1)
            centre(NG - 1)
            variance(NG - 1)
            query_norms(0, 0)
            query_norms(0, 1)
            key_norm(0)
            scaled_norms(0)
            deviation(NG - 1)
            for part in range(3):
                inverse_norms(0, part)
            unit_queries(0, 0)
            unit_queries(0, 1)
            null_logits(0)
            biased_null_logits(0)
            dve.wait_ge(m_nt, 3 * NG)
            gg = slice((NG - 1) * GB, NG * GB)
            v.tensor_tensor(xc[:, gg, :], xc[:, gg, :],
                            rstd[:, 3, :].rearrange("p (b o) -> p b o", o=1).to_broadcast([128, GB, H]),
                            ALU.mult).then_inc(m_xn, 1)
            biased_scores(0, 0)
            maxima(0, 0)
            null_shifts(0, 0)
            biased_scores(0, 1)
            maxima(0, 1)
            null_shifts(0, 1)
            biased_scores(0, 2)
            step(0)
            step(1)
            with dve.Fori(2, B - 1) as n:
                step(n)
            step(B - 1)
            step(B)

        @block.gpsimd
        def _(pool):
            g_ = nc.gpsimd

            pool.sem_inc(m_xn, 1)
            pool.wait_ge(l_mask, 16)
            g_.tensor_scalar(maskb[:], masku[:], -1.0, -NEG, ALU.add, ALU.mult).then_inc(one["g_mask"], 1)
            pool.wait_ge(l_att, L_ATT)
            pool.wait_ge(l_late, L_LATE)
            pool.wait_ge(one["a_fro"], 3)
            g_.tensor_scalar(nvblk[:].rearrange("p c h -> p (c h)"), nsel, nvcol[:, 0:1], fro[:, 4:5], ALU.mult,
                             ALU.mult).then_inc(one["g_nvblk"], 1)
            pool.wait_ge(one["v_nkrow"], 1)
            g_.tensor_tensor(q2[:], wq[:].rearrange("p (h d) -> p h d", d=D),
                             nkrow.rearrange("p (o d) -> p o d", o=1).to_broadcast([128, NH, D]),
                             ALU.mult).then_inc(one["g_nk"], 1)

            def squares(r):
                pool.wait_ge(m_st, 3 * r + 3)
                xc_r = xc[:, bass.ds(r * GB, GB), :]
                settle(pool)
                g_.tensor_tensor(sq[:], xc_r, xc_r, ALU.mult).then_inc(m_sq, 1)

            with pool.Fori(0, NG - 1) as r:
                squares(r)
                pool.wait_ge(m_nt, 3 * r + 3)
                xc_r = xc[:, bass.ds(r * GB, GB), :]
                settle(pool)
                g_.tensor_tensor(xc_r, xc_r, rstd[:, 3, :].rearrange("p (b o) -> p b o", o=1).to_broadcast([128, GB, H]),
                                 ALU.mult).then_inc(m_xn, 1)
            def tokens(m):
                if not live(m):
                    return
                if later(m):
                    pool.wait_ge(t_kv, m)
                settle(pool)
                g_.tensor_copy(xnb[:], xT[:, bass.ds(m * T, T)]).then_inc(g_xn, 1)

            def masked_bias(m, g):
                if not live(m):
                    return
                if later(m):
                    pool.wait_ge(e_s, 4 * m - 3 + g)
                hs = slice(HG * g, HG * g + HG)
                settle(pool)
                g_.tensor_tensor(biasm[:, hs, :], bias[:, hs, :], maskb[:, bass.ds(m, 1), :].to_broadcast([128, HG, T]),
                                 ALU.add).then_inc(g_bias, 1)

            def batch_values(m):
                if not live(m):
                    return
                pool.wait_ge(c_kv, m + 1)
                if later(m):
                    pool.wait_ge(t_av, 4 * m)
                settle(pool)
                g_.tensor_copy(vaug[:, 0, 0:D], kvs[:, NH + D:NH + 2 * D]).then_inc(g_v, 1)
                pool.wait_ge(g_v, 2 * m + 1)
                g_.tensor_tensor(vaug[:, 1, 0:D], kvs[:, NH + D:NH + 2 * D], vaug[:, 0, 0:D],
                                 ALU.subtract).then_inc(g_v, 1)

            def output(m):
                if not live(m):
                    return
                pool.wait_ge(e_st, 2 * m + 2)
                settle(pool)
                g_.tensor_scalar(onw[:, 0:1], omv[:, 1:2], LN_EPS, None, ALU.add).then_inc(e_var, 1)
                pool.wait_ge(c_lno, 2 * m + 2)
                g_.tensor_tensor(onw[:, 3:4], onw[:, 2:3], onw[:, 2:3], ALU.mult).then_inc(e_no, 1)
                pool.wait_ge(e_no, 4 * m + 1)
                g_.tensor_tensor(onw[:, 5:6], onw[:, 3:4], onw[:, 0:1], ALU.mult).then_inc(e_no, 1)
                pool.wait_ge(e_no, 4 * m + 2)
                settle(pool)
                g_.tensor_scalar(onw[:, 3:4], onw[:, 5:6], -0.5, 1.5, ALU.mult, ALU.add).then_inc(e_no, 1)
                pool.wait_ge(e_no, 4 * m + 3)
                if later(m):
                    pool.wait_ge(c_out, m)
                g_.tensor_tensor(onw[:, 4:5], onw[:, 3:4], onw[:, 2:3], ALU.mult).then_inc(e_no, 1)
                pool.wait_ge(e_no, 4 * m + 4)
                settle(pool)
                g_.tensor_scalar(nmr[:], omv[:, 0:1], onw[:, 4:5], -1.0, ALU.mult, ALU.mult).then_inc(e_mr, 1)
                pool.wait_ge(c_out, m + 1)
                g_.tensor_tensor(osc[:], olin[:], gout, ALU.mult).then_inc(g_o, 1)
                pool.wait_ge(g_o, 2 * m + 1)
                if later(m):
                    pool.wait_ge(d_out, 16 * m)
                settle(pool)
                g_.tensor_tensor(ores[:], osc[:], xa[:, bass.ds(m, 1), :].rearrange("p o h -> p (o h)"),
                                 ALU.add).then_inc(g_o, 1)

            def step(n):
                p, x = n - 1, n + 1
                tokens(x)
                masked_bias(n, 3)
                batch_values(n)
                masked_bias(x, 0)
                masked_bias(x, 1)
                masked_bias(x, 2)
                output(p)

            pool.wait_ge(one["a_xnT"], 1)
            tokens(0)
            squares(NG - 1)
            pool.wait_ge(one["g_mask"], 1)
            for g in range(3):
                pool.wait_ge(one["a_bias"], g + 1)
                masked_bias(0, g)
            pool.wait_ge(one["a_bias"], HGS)
            step(0)
            pool.wait_ge(one["a_xnT"], NG)
            step(1)
            with pool.Fori(2, B - 1) as n:
                step(n)
            step(B - 1)
            step(B)


_INS = ["x", "cond_64", "mask_BxS_bf1", "L0_cond_w_gate", "L0_cond_w_up", "L0_cond_w_down", "L0_cond_sw_gate",
        "L0_cond_sw_up", "L0_cond_sw_down", "L1_cond_g_norm", "L1_cond_Wq", "L1_cond_Wkv", "L1_cond_q_scale",
        "L1_cond_k_scale", "L1_cond_w1", "L1_cond_w2", "L1_cond_Wout"]


def shape_constants():
    eye = np.eye(128, dtype=np.float32)
    esel = np.zeros((3, E, EC, 128), np.float32)
    for e in range(E):
        esel[:, e, e // 2, (e % 2) * M:(e % 2 + 1) * M] = 1.0
    nsel = np.zeros((128, PAIRS, NH), np.float32)
    for c in range(PAIRS):
        for r in range(2):
            nsel[r * D:(r + 1) * D, c, 2 * c + r] = 1.0
    rank = np.tile(np.arange(E, 0, -1, dtype=np.float32), (128, B))
    pos = np.arange(T, dtype=np.float32).reshape(T, 1)
    return {
        "c_const": np.concatenate([eye, rank, pos, eye[::-1], nsel.reshape(128, PAIRS * NH)], axis=1),
        "c_esel": esel.reshape(3 * E, EC, 128),
    }


def packed(inputs):
    names = ("L1_cond_w0", "L1_cond_b0", "L1_cond_g0", "L1_cond_b1", "L1_cond_g1", "L1_cond_g_out", "L1_cond_b2",
             "L1_cond_null_attn_bias")
    vectors = [inputs[n].reshape(-1) for n in names]
    vectors += [inputs["cond_64"][0], inputs["L1_cond_q_scale"], inputs["L1_cond_k_scale"]]
    return {
        "p_rows": np.concatenate(vectors).reshape(1, ROWS),
        "p_router": np.concatenate([inputs["L0_cond_wt"], inputs["L0_cond_wg"]], axis=1),
    }


def kernel(**inputs):
    import concourse.bacc as _bacc
    from concourse import mybir as _mybir
    from concourse.bass_utils import run_bass_kernel_spmd as _run

    nc = _bacc.Bacc("TRN2", target_bir_lowering=False, num_devices=1)
    arrays, aps = {}, {}
    named = [(n, np.ascontiguousarray(inputs[n])) for n in _INS] + list(packed(inputs).items())
    named += list(shape_constants().items())
    for name, v in named:
        if v.dtype == np.bool_:
            v = v.view(np.uint8)
        arrays[f"in_{name}"] = v
        aps[name] = nc.dram_tensor(f"in_{name}", v.shape, _mybir.dt.from_np(v.dtype), kind="ExternalInput").ap()
    aps["mask"] = aps["mask_BxS_bf1"]
    out = nc.dram_tensor("out_0", (B, T, H), F32, kind="ExternalOutput").ap()
    build(nc, aps, out)
    r = _run(nc, [arrays], core_ids=[0])
    return np.asarray(r.results[0]["out_0"])
```
